# Optimizing a Trainium2 kernel written in Bass

```python
import numpy as np
import jax
import jax.numpy as jnp

def _softmax(x, axis=-1):
    return jax.nn.softmax(x, axis=axis)

def _gelu(x):
    return jax.nn.gelu(x, approximate=True)

def _silu(x):
    return jax.nn.silu(x)

def _sigmoid(x):
    return jax.nn.sigmoid(x)

def _layernorm(x, axis=-1, eps=1e-05):
    m = jnp.mean(x, axis=axis, keepdims=True)
    v = jnp.var(x, axis=axis, keepdims=True)
    return (x - m) / jnp.sqrt(v + eps)

def _scatter_add(tgt, idx, src, axis=0):
    return tgt.at[idx].add(src)

def _segment_sum(src, seg, n):
    return jax.ops.segment_sum(src, seg, n)
kernel_name = 'mk_adaln_d1_jaxref_r8_d2fa8e'

def setup_inputs(seed: int=0):
    np.random.seed(seed)
    _w = jnp.asarray

    def _L0_attn_setup():
        import jax, jax.numpy as jnp
        import numpy as np
        B, T, D, N = (2, 128, 256, 16)
        G, C, K = (1, 4, 128)
        DHD = 2
        HD = D // N

        def _rmsnorm_noscale(x, eps=1e-06):
            var = jnp.mean(x * x, axis=-1, keepdims=True)
            return x * jax.lax.rsqrt(var + eps)

        def _cross_head_proj(inputs, qw1, qw2, kw1, kw2, qdd, kdd):
            h_q = jnp.einsum('bnts,btin->btsi', inputs, qw1)
            out = inputs + jnp.einsum('btsi,btin->bnts', h_q, qw2)
            h_k = jnp.einsum('bnts,bsin->btsi', inputs, kw1)
            out = out + jnp.einsum('btsi,bsin->bnts', h_k, kw2)
            out = out + inputs * jnp.transpose(qdd, (0, 2, 1))[:, :, :, None]
            out = out + inputs * jnp.transpose(kdd, (0, 2, 1))[:, :, None, :]
            return out
        key = jax.random.key(seed)
        ks = jax.random.split(key, 6)
        x = jax.random.normal(ks[0], (B, T, D), dtype=jnp.float32)
        w_qkv = jax.random.normal(ks[1], (D, 3 * D), dtype=jnp.float32) * 0.02
        w_o = jax.random.normal(ks[2], (D, D), dtype=jnp.float32) * 0.02
        dw1 = jax.random.normal(ks[3], (D, G, C, K), dtype=jnp.float32) * 0.02
        qkw = jax.random.normal(ks[4], (G, C, K, 2 * DHD, N), dtype=jnp.float32) * 0.02
        dd_w = jax.random.normal(ks[5], (D, G, 4 * N), dtype=jnp.float32) * 0.02
        return {'x': x, 'w_qkv': w_qkv, 'w_o': w_o, 'dw1': dw1, 'qkw': qkw, 'dd_w': dd_w}
    _L0_attn_in = _L0_attn_setup()

    def _L0_ffn_setup():
        import jax, jax.numpy as jnp
        import numpy as np
        SEQ, BS, D, F, E = (128, 2, 256, 256, 8)
        key = jax.random.key(seed)
        ks = jax.random.split(key, 8)
        s = 0.02
        return {'hidden_states': jax.random.normal(ks[0], (SEQ, BS, D), jnp.float32), 'router_w': jax.random.normal(ks[1], (D, E), jnp.float32) * s, 'gate_w': jax.random.normal(ks[2], (E, D, F), jnp.float32) * s, 'up_w': jax.random.normal(ks[3], (E, D, F), jnp.float32) * s, 'down_w': jax.random.normal(ks[4], (E, F, D), jnp.float32) * s, 'shared_gate_w': jax.random.normal(ks[5], (D, F), jnp.float32) * s, 'shared_up_w': jax.random.normal(ks[6], (D, F), jnp.float32) * s, 'shared_down_w': jax.random.normal(ks[7], (F, D), jnp.float32) * s}
    _L0_ffn_in = _L0_ffn_setup()
    _L0_c = _w((lambda *s: np.random.randn(*s).astype(np.float32) * 0.05)(2, 256))
    _L0_wmod = _w((lambda *s: np.random.randn(*s).astype(np.float32) * 0.05)(256, 6 * 256) * 256 ** (-0.5))
    _d = {'L0_attn_x': _L0_attn_in['x'], 'L0_attn_w_qkv': _L0_attn_in['w_qkv'], 'L0_attn_w_o': _L0_attn_in['w_o'], 'L0_attn_dw1': _L0_attn_in['dw1'], 'L0_attn_qkw': _L0_attn_in['qkw'], 'L0_attn_dd_w': _L0_attn_in['dd_w'], 'L0_ffn_router_w': _L0_ffn_in['router_w'], 'L0_ffn_gate_w': _L0_ffn_in['gate_w'], 'L0_ffn_up_w': _L0_ffn_in['up_w'], 'L0_ffn_down_w': _L0_ffn_in['down_w'], 'L0_ffn_shared_gate_w': _L0_ffn_in['shared_gate_w'], 'L0_ffn_shared_up_w': _L0_ffn_in['shared_up_w'], 'L0_ffn_shared_down_w': _L0_ffn_in['shared_down_w'], 'L0_c': _L0_c, 'L0_wmod': _L0_wmod}
    _x0 = _d['L0_attn_x']
    _d['L0_attn_x'] = jax.random.normal(jax.random.fold_in(jax.random.key(seed), 1), (2, 512, 256), dtype=_x0.dtype)
    del _x0
    return _d

def reference(L0_attn_x, L0_attn_w_qkv, L0_attn_w_o, L0_attn_dw1, L0_attn_qkw, L0_attn_dd_w, L0_ffn_router_w, L0_ffn_gate_w, L0_ffn_up_w, L0_ffn_down_w, L0_ffn_shared_gate_w, L0_ffn_shared_up_w, L0_ffn_shared_down_w, L0_c, L0_wmod):

    def _L0_attn_ref(x, w_qkv, w_o, dw1, qkw, dd_w):
        import jax, jax.numpy as jnp
        import numpy as np
        B, T, D, N = (2, 128, 256, 16)
        G, C, K = (1, 4, 128)
        DHD = 2
        HD = D // N

        def _rmsnorm_noscale(x, eps=1e-06):
            var = jnp.mean(x * x, axis=-1, keepdims=True)
            return x * jax.lax.rsqrt(var + eps)

        def _cross_head_proj(inputs, qw1, qw2, kw1, kw2, qdd, kdd):
            h_q = jnp.einsum('bnts,btin->btsi', inputs, qw1)
            out = inputs + jnp.einsum('btsi,btin->bnts', h_q, qw2)
            h_k = jnp.einsum('bnts,bsin->btsi', inputs, kw1)
            out = out + jnp.einsum('btsi,bsin->bnts', h_k, kw2)
            out = out + inputs * jnp.transpose(qdd, (0, 2, 1))[:, :, :, None]
            out = out + inputs * jnp.transpose(kdd, (0, 2, 1))[:, :, None, :]
            return out
        b, t, d = x.shape
        qkv = x @ w_qkv
        q, k, v = jnp.split(qkv, 3, axis=-1)
        q = q.reshape(b, t, N, HD).transpose(0, 2, 1, 3) * HD ** (-0.5)
        k = k.reshape(b, t, N, HD).transpose(0, 2, 1, 3)
        v = v.reshape(b, t, N, HD).transpose(0, 2, 1, 3)
        dw_hidden = jax.nn.gelu(jnp.einsum('btd,dgck->btgck', x, dw1))
        w = jnp.einsum('btgck,gckim->btgcim', dw_hidden, qkw)
        w1, w2 = jnp.split(w, 2, axis=-2)
        w1 = _rmsnorm_noscale(w1)
        pre_qw1, pre_kw1, post_qw1, post_kw1 = (w1[:, :, 0, c] for c in range(4))
        pre_qw2, pre_kw2, post_qw2, post_kw2 = (w2[:, :, 0, c] for c in range(4))
        dd = jnp.tanh(jnp.einsum('btd,dgm->btgm', x, dd_w))[:, :, 0]
        pre_qdd, pre_kdd, post_qdd, post_kdd = jnp.split(dd, 4, axis=-1)
        logits = jnp.einsum('bnth,bnsh->bnts', q, k)
        logits = _cross_head_proj(logits, pre_qw1, pre_qw2, pre_kw1, pre_kw2, pre_qdd, pre_kdd)
        mask = jnp.tril(jnp.ones((t, t), dtype=bool))
        logits = jnp.where(mask, logits, jnp.finfo(jnp.float32).min)
        probs = jax.nn.softmax(logits, axis=-1)
        probs = _cross_head_proj(probs, post_qw1, post_qw2, post_kw1, post_kw2, post_qdd, post_kdd)
        o = jnp.einsum('bnts,bnsh->bnth', probs, v)
        o = o.transpose(0, 2, 1, 3).reshape(b, t, d)
        return o @ w_o.T

    def _L0_ffn_ref(hidden_states, router_w, gate_w, up_w, down_w, shared_gate_w, shared_up_w, shared_down_w):
        import jax, jax.numpy as jnp
        import numpy as np
        SEQ, BS, D, F, E = (128, 2, 256, 256, 8)
        S, B, Dm = hidden_states.shape
        x = hidden_states.reshape(-1, Dm)
        logits = x @ router_w
        expert_idx = jnp.argmax(logits, axis=-1)
        score = jax.nn.sigmoid(jnp.max(logits, axis=-1))
        xs = x * score[:, None]
        n_experts = router_w.shape[1]
        out = jnp.zeros_like(x)
        for e in range(n_experts):
            m = (expert_idx == e)[:, None]
            xe = jnp.where(m, xs, 0.0)
            h = jax.nn.silu(xe @ gate_w[e]) * (xe @ up_w[e])
            out = out + jnp.where(m, h @ down_w[e], 0.0)
        shared = jax.nn.silu(x @ shared_gate_w) * (x @ shared_up_w) @ shared_down_w
        return (out + shared).reshape(S, B, Dm)
    x = L0_attn_x
    mod = (_silu(L0_c) @ L0_wmod).reshape(L0_c.shape[0], 6, 1, -1)
    sa, ca, ga, sb, cb, gb = (mod[:, 0], mod[:, 1], mod[:, 2], mod[:, 3], mod[:, 4], mod[:, 5])
    ga = (2 * (ga >= 0) - 1) * jnp.maximum(jnp.abs(ga), 0.25)
    gb = (2 * (gb >= 0) - 1) * jnp.maximum(jnp.abs(gb), 0.25)
    h = _layernorm(x, axis=-1) * (1 + ca) + sa
    x = x + ga * _L0_attn_ref(h, L0_attn_w_qkv, L0_attn_w_o, L0_attn_dw1, L0_attn_qkw, L0_attn_dd_w)
    h = _layernorm(x, axis=-1) * (1 + cb) + sb
    x = x + gb * _L0_ffn_ref(h, L0_ffn_router_w, L0_ffn_gate_w, L0_ffn_up_w, L0_ffn_down_w, L0_ffn_shared_gate_w, L0_ffn_shared_up_w, L0_ffn_shared_down_w)
    return x

_drawn_inputs = setup_inputs


def setup_inputs(seed=0):
    import zlib

    import numpy as np

    out = dict(_drawn_inputs(seed))
    spreads = {}
    factors = {'L0_attn_w_qkv': 8.0,
     'L0_attn_w_o': 8.0,
     'L0_attn_dw1': 8.0,
     'L0_attn_qkw': 8.0,
     'L0_attn_dd_w': 8.0,
     'L0_ffn_router_w': 8.0,
     'L0_ffn_gate_w': 8.0,
     'L0_ffn_up_w': 8.0,
     'L0_ffn_down_w': 8.0,
     'L0_ffn_shared_gate_w': 8.0,
     'L0_ffn_shared_up_w': 8.0,
     'L0_ffn_shared_down_w': 8.0,
     'L0_c': 8.0,
     'L0_wmod': 8.0}
    for name, (base, spread) in spreads.items():
        noise = np.random.default_rng([zlib.crc32(name.encode()), seed]).standard_normal(out[name].shape)
        drawn = base * np.exp(spread * noise) if base else spread * noise
        out[name] = jnp.asarray(drawn.astype(out[name].dtype))
    for name, factor in factors.items():
        out[name] = (out[name] * factor).astype(out[name].dtype)
    return out
```

```python
import concourse.bass as bass
from concourse import mybir
from contextlib import ExitStack

P = 128
F32 = mybir.dt.float32
BF16 = mybir.dt.bfloat16
ALU = mybir.AluOpType
ACT = mybir.ActivationFunctionType
AX = mybir.AxisListType
MASKED = 1e30


class Done:

    def __init__(self, sem):
        self.sem, self.base, self.n = sem, 0, 0

    def mark(self, ins, by=1):
        ins.then_inc(self.sem, by)
        self.n += by
        return self.base + self.n

    def now(self):
        return self.base + self.n

    def enter(self, var, per):
        saved = (self.base, self.n)
        self.base, self.n = self.base + self.n + var * per, 0
        return saved

    def leave(self, saved, times, per):
        assert self.n == per, (self.n, per)
        self.base, self.n = saved[0], saved[1] + times * per


def adaln_layer(nc, x, w_qkv, w_oT, dw1, qkw, dd_w, router_w, gate_w, up_w, down_w,
                shared_gate, shared_up, shared_down, cT, wmod, out):
    BT, D = x.shape
    B = cT.shape[1]
    T = BT // B
    NT = BT // P
    TI = T // P
    KT = D // P
    C, _, M4 = qkw.shape
    N = M4 // 4
    HD = D // N
    R = 2
    G = N // 4
    E = router_w.shape[1]
    F = gate_w.shape[2]
    QSCALE = -float(HD) ** -0.5
    LN_EPS, RMS_EPS = 1e-5, 1e-6
    TRI = [P * (t * (t + 1) // 2) for t in range(TI + 1)]
    TRK = [P * (TI * s - s * (s - 1) // 2) for s in range(TI + 1)]
    assert D == 256 and N == 16 and C == 4 and TI == 4 and F == D and E == 8

    with ExitStack() as ctx:
        def sb(name, shape, dt=F32):
            return ctx.enter_context(nc.sbuf_tensor(name, shape, dt))

        def sem(name):
            return ctx.enter_context(nc.semaphore(name))

        bank = [ctx.enter_context(nc.psum_tensor(f"bank{i}", [P, 512], F32)) for i in range(8)]

        xs = sb("xs", [P, NT, D])
        mod = sb("mod", [P, B, 6 * D])
        ident = sb("ident", [P, P])
        ident_b = sb("ident_b", [P, P], BF16)
        mask_b = sb("mask_b", [P, P], BF16)
        ones = sb("ones", [P, P])
        stats = sb("stats", [P, NT, 6])
        mean_var = sb("mean_var", [P, NT, 2])
        nw = sb("nw", [P, 3, 64])
        rstd = sb("rstd", [P, NT])
        rrms = sb("rrms", [P, 64])
        early = sb("early", [P, KT * 3 * D + KT * C * P])
        wqkv_s = early[:, 0:KT * 3 * D].rearrange("p (k n) -> p k n", k=KT)
        dw1_s = early[:, KT * 3 * D:].rearrange("p (k n) -> p k n", k=KT)
        qkw_s = sb("qkw_s", [P, C, M4])
        ddw_s = sb("ddw_s", [P, KT, 64])
        woT_s = sb("woT_s", [P, KT, D])
        c_s = sb("c_s", [P, KT * B])
        c_e = sb("c_e", [P, 3, KT * B])
        W = sb("W", [P, NT, C * M4])
        DD = sb("DD", [P, NT, 64])
        QK = sb("QK", [P, NT, 2 * D])
        V = sb("V", [P, NT, D])
        QC = sb("QC", [P, G, T])
        KC = sb("KC", [P, G, T])
        QT = sb("QT", [P, KT, T])
        KTr = sb("KTr", [P, KT, T])
        QW = sb("QW", [P, R * KT, T])
        KW = sb("KW", [P, R * KT, T])
        HQ = sb("HQ", [P, R, TRI[TI]])
        HK = sb("HK", [P, R, TRK[TI]])
        Hp = early[:, :].rearrange("p (r n) -> p r n", r=R)
        O = sb("O", [P, TI, D])
        Bp = sb("Bp", [P, TI, N, N])
        Vb = sb("Vb", [P, TI, D])
        QCg = sb("QCg", [P, T])
        KCg = sb("KCg", [P, T])
        Wq2 = sb("Wq2", [P, TI, R, 4])
        Wp1 = sb("Wp1", [P, TI, R, 4])
        Wk2 = sb("Wk2", [P, TI, R, 4])
        DG = sb("DG", [P, 2, TI, R, 2, P])
        VP = sb("VP", [P, 2, TI, 2, D])
        X = sb("X", [P, 4, T])
        Y = sb("Y", [P, 2, T])
        PT = sb("PT", [P, 2, T])
        rowmin = sb("rowmin", [P, 4])
        rowsum = sb("rowsum", [P, 4])
        rsum = sb("rsum", [P, 4])
        ou = sb("ou", [P, 2, D])
        c_rows = [Y[:, i // 2, D + P * (i % 2):D + P * (i % 2) + P] for i in range(KT * B)]
        hT = sb("hT", [P, 2, KT, P])
        h = Y[:, :, 0:D]
        late = DG[:, 1, :, :, :, :].rearrange("p a b c d -> p (a b c d)")
        gl = late[:, 0:1024].rearrange("p (a n) -> p a n", a=2)
        gh = late[:, 1024:2048].rearrange("p (a c t) -> p a c t", a=2, c=C)

        wmod_s = [QC[:, :, :].rearrange("p a b -> p (a b)")[:, 0:6 * D],
                  KC[:, :, :].rearrange("p a b -> p (a b)")[:, 0:6 * D]]
        stackv = VP[:, :, :, :, :].rearrange("p a b c d -> p (a b c d)")
        stack = [stackv[:, 512 * i:512 * i + 512] for i in range(5)]
        sq = DG[:, 0, :, :, :, :].rearrange("p a b c d -> p (a b c d)")[:, 0:1024]
        bt = DG[:, 1, :, :, :, :].rearrange("p a b c d -> p (a b c d)")[:, 0:512]
        gu_s = QK[:, :, :].rearrange("p a b -> p (a b)")
        x2T = QW[:, 0:KT * 2, :].rearrange("p (k a) t -> p k (a t)", k=KT)
        rl = sb("rl", [P, NT, E])
        rbest = sb("rbest", [P, NT])
        rone = sb("rone", [P, NT, E])
        eio = sb("eio", [P, E])
        half = sb("half", [P, NT, E + 1])
        pick = sb("pick", [P, NT, E + 1])
        rw_s = sb("rw_s", [P, KT, E])

        d_x, d_c, d_wm, d_w, d_out = (sem(n) for n in ("d_x", "d_c", "d_wm", "d_w", "d_out"))
        d_gu = [sem("d_gu0"), sem("d_gu1")]
        dve_done, pool_done = sem("dve_done"), sem("pool_done")
        dve_step, pe_step = sem("dve_step"), sem("pe_step")
        pool_ready, ones_ready = sem("pool_ready"), sem("ones_ready")
        c_exp, c_ready, mod_mm, mod_copied = (sem(n) for n in ("c_exp", "c_ready", "mod_mm", "mod_copied"))
        var_ready, root_ready = sem("var_ready"), sem("root_ready")
        h_ready, hT_mm, hT_ready = sem("h_ready"), sem("hT_mm"), sem("hT_ready")
        dwh_mm, g_sq, g_arg, g_tanh, g_ready = (sem(n) for n in ("dwh_mm", "g_sq", "g_arg", "g_tanh", "g_ready"))
        proj_mm, proj_copied = sem("proj_mm"), sem("proj_copied")
        stack_ready, stack_mm, stack_act, stack_dve = (sem(n) for n in ("stack_ready", "stack_mm", "stack_act", "stack_dve"))
        hh_mm, hq_copied, hk_copied = sem("hh_mm"), sem("hq_copied"), sem("hk_copied")
        wk2_ready, group_ready, pair_ready = sem("wk2_ready"), sem("group_ready"), sem("pair_ready")
        logit_mm, logit_read, prod_ready = sem("logit_mm"), sem("logit_read"), sem("prod_ready")
        exp_done, prob_ready, hp_added = sem("exp_done"), sem("prob_ready"), sem("hp_added")
        pt_mm, pt_ready, pv_mm, o_read = sem("pt_mm"), sem("pt_ready"), sem("pv_mm"), sem("o_read")
        hp_mm, hp_ready, hv_mm = sem("hp_mm"), sem("hp_ready"), sem("hv_mm")
        o_ready, oT_mm, oT_ready, ao_mm, x1_ready = (sem(n) for n in ("o_ready", "oT_mm", "oT_ready", "ao_mm", "x1_ready"))
        h2_ready, h2_mm, h2_T, r_mm, r_max = (sem(n) for n in ("h2_ready", "h2_mm", "h2_T", "r_mm", "r_max"))
        half_ready, pick_ready = sem("half_ready"), sem("pick_ready")
        gu_mm, th_ready, hm_ready, hmT_mm, hmT_ready, dn_mm, out_ready = (
            sem(n) for n in ("gu_mm", "th_ready", "hm_ready", "hmT_mm", "hmT_ready", "dn_mm", "out_ready"))
        C_LOGIT, C_PT, C_PV, C_O, C_ONE, C_E = 4, 4, 16, 2, 1, 2

        HEADS = 16

        def at(k):
            return (k % 8) // 2, k // 8, k % 2

        def bc(ap, axis, n):
            a = ap.unsqueeze(axis)
            shape = list(a.shape)
            shape[axis] = n
            return a.broadcast_to(shape)

        def weights_of(tile):
            return W[:, bass.ds(tile, 1), :].rearrange("p a (c i n) -> p (a c) i n", c=C, i=4)

        def expert_slot(slot):
            base = slot * 6 * D
            return (gu_s[:, base:base + 4 * D].rearrange("p (k n) -> p k n", k=KT),
                    gu_s[:, base + 4 * D:base + 6 * D].rearrange("p (k n) -> p k n", k=KT))

        block = ctx.enter_context(nc.Block())

        @block.sync
        def _(sp):
            sp.dma_start(c_s[:, :].rearrange("p (k b) -> p k b", k=KT),
                         cT.rearrange("(k p) b -> p k b", p=P)).then_inc(d_c, 16)
            for k in range(KT):
                sp.dma_start(wmod_s[k], wmod[P * k:P * (k + 1), :]).then_inc(d_wm, 16)
            sp.dma_start(xs[:, :, :], x.rearrange("(a p) d -> p a d", p=P)).then_inc(d_x, 16)
            sp.dma_start(wqkv_s[:, :, :], w_qkv.rearrange("(k p) n -> p k n", p=P)).then_inc(d_w, 16)
            sp.dma_start(dw1_s[:, :, :], dw1.rearrange("(k p) n -> p k n", p=P)).then_inc(d_w, 16)
            sp.dma_start(qkw_s[:, :, :], qkw.rearrange("c k m -> k c m")).then_inc(d_w, 16)
            sp.dma_start(ddw_s[:, :, :], dd_w.rearrange("(k p) n -> p k n", p=P)).then_inc(d_w, 16)
            sp.dma_start(woT_s[:, :, :], w_oT.rearrange("(k p) n -> p k n", p=P)).then_inc(d_w, 16)
            sp.dma_start(rw_s[:, :, :], router_w.rearrange("(k p) n -> p k n", p=P)).then_inc(d_w, 16)

            def load_expert(slot, gate, up, down):
                g, d = expert_slot(slot)
                sp.dma_start(g[:, :, 0:D], gate.rearrange("(k p) n -> p k n", p=P)).then_inc(d_gu[slot], 16)
                sp.dma_start(g[:, :, D:2 * D], up.rearrange("(k p) n -> p k n", p=P)).then_inc(d_gu[slot], 16)
                sp.dma_start(d, down.rearrange("(k p) n -> p k n", p=P)).then_inc(d_gu[slot], 16)

            sp.wait_ge(stack_mm, 5 * NT)
            load_expert(0, shared_gate, shared_up, shared_down)
            load_expert(1, gate_w[0], up_w[0], down_w[0])
            for e in range(1, E):
                sp.wait_ge(dn_mm, C_E + NT * e)
                load_expert((e + 1) % 2, gate_w[e], up_w[e], down_w[e])
            for t in range(NT):
                sp.wait_ge(out_ready, t + 1)
                sp.dma_start(out[P * t:P * (t + 1), :], xs[:, t, :]).then_inc(d_out, 16)
            sp.wait_ge(d_out, 16 * NT)

        @block.gpsimd
        def _(pool):
            pool.memset(ident[:, :], 0.0)
            pool.memset(mask_b[:, :], 0.0)
            pool.memset(ident_b[:, :], 0.0).then_inc(pool_done, 1)
            pool.wait_ge(pool_done, 1)
            for m in (ident, ident_b):
                pool.affine_select(out=m[:, :], in_=m[:, :], compare_op=ALU.not_equal, fill=1.0,
                                   base=0, pattern=[[-1, P]], channel_multiplier=1)
            pool.affine_select(out=mask_b[:, :], in_=mask_b[:, :], compare_op=ALU.is_ge, fill=MASKED,
                               base=0, pattern=[[-1, P]], channel_multiplier=1)
            pool.iota(eio[:, :], pattern=[[1, E]], base=0, channel_multiplier=0,
                      allow_small_or_imprecise_dtypes=True).then_inc(pool_ready, 1)
            pool.wait_ge(pool_ready, 1)
            pool.sem_inc(pair_ready, C_ONE)

            with pool.Fori(0, B) as b:
                with pool.Fori(0, G) as g:
                    bg = b * G + g

                    def copy_rows(dst, c, i):
                        src = W[:, bass.ds(b * TI, TI), bass.ds(g * 4 + (c * M4 + i * N), N + 4)]
                        for r in range(R):
                            last = pool.tensor_copy(dst[:, :, r, :], src[:, :, r * N:r * N + 4])
                        return last

                    def make_pair(p):
                        for s in range(TI):
                            for r in range(R):
                                pool.tensor_tensor(DG[:, p, s, r, :, :], bc(ident[:, :], 1, 2),
                                                   bc(Wk2[:, s, r, 2 * p:2 * p + 2], 2, P), ALU.mult)
                            for j in range(2):
                                m = g * 4 + (2 * p + j)
                                last = pool.tensor_tensor(
                                    VP[:, p, s, j, :].rearrange("p (n h) -> p n h", n=N),
                                    Vb[:, s, :].rearrange("p (n h) -> p n h", n=N),
                                    bc(Bp[:, s, bass.ds(m, 1), :].rearrange("p a n -> p (a n)"), 2, HD), ALU.mult)
                        last.then_inc(pair_ready, 1)

                    pool.wait_ge(stack_act, (b + 1) * 3 * TI)
                    pool.wait_ge(stack_dve, (b + 1) * 2 * TI)
                    pool.wait_ge(pair_ready, bg * 2 + C_ONE)
                    copy_rows(Wk2, 1, 2).then_inc(wk2_ready, 1)
                    pool.wait_ge(wk2_ready, bg + 1)
                    pool.wait_ge(pv_mm, bg * HEADS + (C_PV - 8))
                    make_pair(0)
                    pool.wait_ge(exp_done, bg * HEADS + C_ONE)
                    pool.wait_ge(hp_added, bg * HEADS + C_ONE)
                    pool.wait_ge(pv_mm, bg * HEADS + C_PV)
                    pool.tensor_copy(QCg[:, :], QC[:, g, :])
                    pool.tensor_copy(KCg[:, :], KC[:, g, :])
                    copy_rows(Wq2, 0, 2)
                    copy_rows(Wp1, 2, 0).then_inc(group_ready, 1)
                    make_pair(1)

        @block.scalar
        def _(act):
            act.sem_inc(exp_done, C_ONE)
            act.sem_inc(pt_ready, C_E)
            act.sem_inc(hmT_ready, C_E)
            act.sem_inc(proj_copied, C_E)
            act.wait_ge(d_c, 16)
            act.activation(c_e[:, 0, :], c_s[:, :], ACT.Exp, scale=-1.0).then_inc(c_exp, 1)
            for i in range(3 * B):
                act.wait_ge(mod_mm, i + 1)
                act.activation(mod[:, i // 3, 512 * (i % 3):512 * (i % 3) + 512], bank[i][:, :], ACT.Copy).then_inc(mod_copied, 1)

            def root(i, n):
                act.wait_ge(var_ready, i + 1)
                act.activation(nw[:, 1, 0:n], nw[:, 0, 0:n], ACT.Sqrt).then_inc(root_ready, 1)

            root(0, NT)

            with act.Fori(0, B) as b:
                for t in range(TI):
                    tile, p = b * TI + t, t % 2
                    bk = bank[4 * p:4 * p + 4]
                    act.wait_ge(hT_mm, tile + 1)
                    act.activation(hT[:, p, :, :], bk[0][:, 0:D].rearrange("p (k t) -> p k t", k=KT), ACT.Copy).then_inc(hT_ready, 1)
                    act.wait_ge(dwh_mm, tile + 1)
                    act.activation(gl[:, p, :], bk[2][:, :], ACT.Square).then_inc(g_sq, 1)
                    act.wait_ge(g_arg, tile + 1)
                    act.activation(gl[:, p, :], gl[:, p, :], ACT.Tanh, scale=0.7978845608028654).then_inc(g_tanh, 1)
                    act.wait_ge(proj_mm, tile + 1)
                    act.activation(QK[:, tile, 0:D], bk[1][:, 0:D], ACT.Copy, scale=QSCALE)
                    act.activation(QK[:, tile, D:2 * D], bk[1][:, D:2 * D], ACT.Copy)
                    act.activation(V[:, tile, :], bk[0][:, D:2 * D], ACT.Copy)
                    act.activation(DD[:, tile, :], bk[3][:, D:D + 64], ACT.Tanh)
                    act.activation(W[:, tile, :], bk[3][:, 0:D], ACT.Copy, scale=0.5).then_inc(proj_copied, 1)

            root(1, 64)

            with act.Fori(0, B) as b:
                for t in range(TI):
                    tile = b * TI + t
                    act.wait_ge(stack_mm, tile * 5 + 1)
                    act.activation(QC[:, :, P * t:P * (t + 1)], bank[0][:, :].rearrange("p (a t) -> p a t", t=P), ACT.Copy).then_inc(stack_act, 1)
                    act.wait_ge(stack_mm, tile * 5 + 3)
                    act.activation(KC[:, :, P * t:P * (t + 1)], bank[2][:, :].rearrange("p (a t) -> p a t", t=P), ACT.Copy).then_inc(stack_act, 1)
                    act.wait_ge(stack_mm, tile * 5 + 5)
                    act.activation(QT[:, :, P * t:P * (t + 1)], bank[4][:, 0:2 * P].rearrange("p (a t) -> p a t", t=P), ACT.Copy)
                    act.activation(KTr[:, :, P * t:P * (t + 1)], bank[4][:, 2 * P:4 * P].rearrange("p (a t) -> p a t", t=P), ACT.Copy).then_inc(stack_act, 1)
                for t in range(TI):
                    for r in range(R):
                        n = 4 * t + 2 * r
                        act.wait_ge(hh_mm, b * 16 + (n + 1))
                        act.activation(HQ[:, r, TRI[t]:TRI[t + 1]], bank[n % 8][:, 0:P * (t + 1)], ACT.Copy).then_inc(hq_copied, 1)
                act.wait_ge(hq_copied, (b + 1) * 8)

                with act.Fori(0, G) as g:
                    base = (b * G + g) * HEADS
                    act.wait_ge(group_ready, b * G + g + 1)

                    def product(k):
                        t, p, j = at(k)
                        act.wait_ge(logit_read, base + (k - 1 + C_LOGIT))
                        act.activation(Y[:, k % 2, 0:P * (t + 1)], HQ[:, 0, TRI[t]:TRI[t + 1]], ACT.Copy,
                                       scale=Wq2[:, t, 0, 2 * p + j:2 * p + j + 1]).then_inc(prod_ready, 1)

                    def exponential(k):
                        t, p, j = at(k)
                        xk = X[:, k % 4, 0:P * (t + 1)]
                        act.wait_ge(logit_read, base + (k + 1 + C_LOGIT))
                        act.activation(xk, xk, ACT.Exp, bias=rowmin[:, k % 4:k % 4 + 1], scale=-1.0,
                                       accum_out=rowsum[:, k % 4:k % 4 + 1]).then_inc(exp_done, 1)

                    def transposed(k):
                        t, p, j = at(k)
                        act.wait_ge(pt_mm, base + (k + 1 + C_PT))
                        act.wait_ge(pv_mm, base + (k - 1 + C_PV))
                        act.activation(PT[:, k % 2, 0:P * (t + 1)], bank[4 + k % 2][:, 0:P * (t + 1)], ACT.Copy).then_inc(pt_ready, 1)

                    product(0)
                    for k in range(HEADS + 2):
                        if k + 1 < HEADS:
                            product(k + 1)
                        if k < HEADS:
                            exponential(k)
                        if k >= 2:
                            transposed(k - 2)

                for t in range(TI):
                    for r in range(R):
                        act.wait_ge(hp_mm, b * 8 + (2 * t + r + 1))
                        act.activation(X[:, r, 0:P * (t + 1)], bank[r][:, 0:P * (t + 1)], ACT.Copy).then_inc(hp_ready, 1)
                    act.wait_ge(oT_mm, b * TI + t + 1)
                    act.activation(hT[:, 0, :, :], bank[3][:, 0:D].rearrange("p (k t) -> p k t", k=KT), ACT.Copy).then_inc(oT_ready, 1)

            root(2, NT)
            for t in range(NT):
                act.wait_ge(h2_mm, t + 1)
                act.activation(x2T[:, :, P * t:P * (t + 1)], bank[t % 2][:, 0:D].rearrange("p (k t) -> p k t", k=KT), ACT.Copy).then_inc(h2_T, 1)
            act.wait_ge(r_max, 1)
            act.activation(rbest[:, :], rbest[:, :], ACT.Tanh, scale=0.5).then_inc(half_ready, 1)
            act.wait_ge(pick_ready, 1)

            def experts(first, count):
                def tanh(k):
                    e, t = first + k // NT, k % NT
                    act.wait_ge(gu_mm, first * NT + (k + 1))
                    act.wait_ge(hm_ready, first * NT + (k - 1 + C_E))
                    act.activation(Y[:, t % 2, 0:F], bank[t % 2][:, 0:F], ACT.Tanh, scale=half[:, t, bass.ds(e, 1)]).then_inc(th_ready, 1)

                def transposed(k):
                    t = k % NT
                    act.wait_ge(hmT_mm, first * NT + (k + 1 + C_E))
                    act.wait_ge(dn_mm, first * NT + (k - 1 + C_E))
                    act.activation(hT[:, t % 2, :, :], bank[2 + t % 2][:, 0:F].rearrange("p (k t) -> p k t", k=KT), ACT.Copy).then_inc(hmT_ready, 1)

                for k in range(NT * count + 1):
                    if k < NT * count:
                        tanh(k)
                    if k >= 1:
                        transposed(k - 1)

            experts(0, 1)
            with act.Fori(0, E // 2) as i:
                experts(i * 2 + 1, 2)

        @block.vector
        def _(dve):
            done = Done(dve_done)

            def wait(v):
                dve.wait_ge(dve_done, v)

            dve.sem_inc(logit_read, C_LOGIT)
            dve.sem_inc(o_read, C_O)
            dve.sem_inc(hp_added, C_ONE)
            dve.sem_inc(hm_ready, C_E)
            dve.memset(ones[:, :], 1.0).then_inc(ones_ready, 1)
            dve.wait_ge(ones_ready, 1)
            dve.wait_ge(c_exp, 1)
            wait(done.mark(dve.tensor_scalar(c_e[:, 1, :], c_e[:, 0, :], 1.0, None, ALU.add)))
            wait(done.mark(dve.reciprocal(c_e[:, 2, :], c_e[:, 1, :])))
            wait(done.mark(dve.tensor_tensor(c_e[:, 0, :], c_e[:, 2, :], c_s[:, :], ALU.mult)))
            for i in range(KT * B):
                ins = dve.tensor_scalar(c_rows[i], ones[:, :], c_e[:, 0, i:i + 1], None, ALU.mult)
            ins.then_inc(c_ready, 1)

            def layernorm_stats():
                for t in range(NT):
                    v = done.mark(dve.bn_stats(stats[:, t, :], xs[:, t, :]))
                wait(v)
                for t in range(NT):
                    v = done.mark(dve.bn_aggr(mean_var[:, t, :], stats[:, t, :]))
                wait(v)
                dve.tensor_scalar(nw[:, 0, 0:NT], mean_var[:, :, 1], LN_EPS, None, ALU.add).then_inc(var_ready, 1)

            def rsqrt(i, n, r):
                dve.wait_ge(root_ready, i + 1)
                wait(done.mark(dve.reciprocal(r, nw[:, 1, 0:n])))
                wait(done.mark(dve.tensor_tensor(nw[:, 2, 0:n], r, r, ALU.mult)))
                wait(done.mark(dve.tensor_tensor(nw[:, 2, 0:n], nw[:, 2, 0:n], nw[:, 0, 0:n], ALU.mult)))
                wait(done.mark(dve.tensor_scalar(nw[:, 2, 0:n], nw[:, 2, 0:n], -0.5, 1.5, ALU.mult, ALU.add)))
                wait(done.mark(dve.tensor_tensor(r, r, nw[:, 2, 0:n], ALU.mult)))

            dve.wait_ge(d_x, 16)
            layernorm_stats()
            rsqrt(0, NT, rstd[:, :])

            dve.wait_ge(mod_copied, 3 * B)
            for o in (1, 4):
                v = done.mark(dve.tensor_scalar(mod[:, :, o * D:(o + 1) * D], mod[:, :, o * D:(o + 1) * D], 1.0, None, ALU.add))
            for o in (2, 5):
                gate = mod[:, :, o * D:(o + 1) * D]
                up, low = (sq[:, i * B * D:(i + 1) * B * D].rearrange("p (b d) -> p b d", b=B) for i in range(2))
                done.mark(dve.tensor_scalar(up, gate, 0.0, None, ALU.is_ge))
                wait(done.mark(dve.tensor_scalar(low, gate, 0.0, None, ALU.is_lt)))
                done.mark(dve.scalar_tensor_tensor(up, gate, 0.25, up, ALU.max, ALU.mult))
                wait(done.mark(dve.scalar_tensor_tensor(low, gate, -0.25, low, ALU.min, ALU.mult)))
                wait(done.mark(dve.tensor_tensor(gate, up, low, ALU.add)))

            def modulated(dst, tile, b, scale, shift):
                wait(done.mark(dve.tensor_scalar(dst, xs[:, tile, :], mean_var[:, tile, 0:1], rstd[:, bass.ds(tile, 1)], ALU.subtract, ALU.mult)))
                wait(done.mark(dve.tensor_tensor(dst, dst, mod[:, b, scale * D:(scale + 1) * D], ALU.mult)))
                return dve.tensor_tensor(dst, dst, mod[:, b, shift * D:(shift + 1) * D], ALU.add)

            PER = 3 * TI
            with dve.Fori(0, B) as b:
                saved = done.enter(b, PER)
                modulated(h[:, 0, :], b * TI, b, 1, 0).then_inc(h_ready, 1)
                for t in range(TI):
                    tile, p = b * TI + t, t % 2
                    pre = bank[4 * p + 2]
                    if t + 1 < TI:
                        modulated(h[:, 1 - p, :], tile + 1, b, 1, 0).then_inc(h_ready, 1)
                    dve.wait_ge(g_sq, tile + 1)
                    wait(done.mark(dve.tensor_scalar(gl[:, p, :], gl[:, p, :], 0.044715, 1.0, ALU.mult, ALU.add)))
                    dve.tensor_tensor(gl[:, p, :], pre[:, :], gl[:, p, :], ALU.mult).then_inc(g_arg, 1)
                    dve.wait_ge(g_tanh, tile + 1)
                    dve.scalar_tensor_tensor(gh[:, p, :, :].rearrange("p c t -> p (c t)"), gl[:, p, :], 1.0, pre[:, :], ALU.add, ALU.mult).then_inc(g_ready, 1)
                done.leave(saved, B, PER)

            dve.wait_ge(proj_copied, NT + C_E)
            w1 = W[:, :, :].rearrange("p t (c i n) -> p (t c) (i n)", c=C, i=4)[:, :, 0:2 * N]
            wait(done.mark(dve.tensor_tensor(sq.rearrange("p (a b) -> p a b", b=2 * N), w1, w1, ALU.mult)))
            wait(done.mark(dve.tensor_reduce(nw[:, 0, :], sq.rearrange("p (a b) -> p a b", b=N), AX.X, ALU.add)))
            dve.tensor_scalar(nw[:, 0, :], nw[:, 0, :], 1.0 / N, RMS_EPS, ALU.mult, ALU.add).then_inc(var_ready, 1)
            rsqrt(1, 64, rrms[:, :])
            w1 = W[:, :, :].rearrange("p t (c i n) -> p (t c) i n", c=C, i=4)[:, :, 0:2, :]
            done.mark(dve.tensor_tensor(w1, w1, bc(rrms[:, :].rearrange("p (a i) -> p a i", i=2), 3, N), ALU.mult))
            for o in (0, 2 * N):
                v = done.mark(dve.tensor_scalar(DD[:, :, o:o + N], DD[:, :, o:o + N], 1.0, None, ALU.add))
            wait(v)
            dve.wait_ge(pool_ready, 1)

            PER_G = HEADS * 2 + HEADS // 2 * 2
            PER_TAIL = TI * 3
            PER_B = TI * 3 + 1 + G * PER_G + PER_TAIL
            with dve.Fori(0, B) as b:
                saved_b = done.enter(b, PER_B)
                for t in range(TI):
                    tile = b * TI + t
                    w = weights_of(tile)
                    q3 = QK[:, tile, 0:D].rearrange("p (n h) -> p n h", n=N)
                    k3 = QK[:, tile, D:2 * D].rearrange("p (n h) -> p n h", n=N)
                    qc = stack[0].rearrange("p (n u h) -> p n u h", n=N, u=2)
                    kc = stack[2].rearrange("p (n u h) -> p n u h", n=N, u=2)
                    if t > 0:
                        dve.wait_ge(stack_mm, tile * 5)
                    dve.tensor_copy(stack[4], QK[:, tile, :])
                    dve.tensor_tensor(qc[:, :, 0, :], q3, bc(DD[:, tile, 0:N], 2, HD), ALU.mult)
                    dve.tensor_copy(qc[:, :, 1, :], q3).then_inc(stack_ready, 1)
                    for r in range(R):
                        ins = dve.tensor_tensor(stack[1][:, r * D:(r + 1) * D].rearrange("p (n h) -> p n h", n=N), q3, bc(w[:, 0, r, :], 2, HD), ALU.mult)
                    ins.then_inc(stack_ready, 1)
                    dve.tensor_copy(kc[:, :, 0, :], k3)
                    dve.tensor_tensor(kc[:, :, 1, :], k3, bc(DD[:, tile, N:2 * N], 2, HD), ALU.mult).then_inc(stack_ready, 1)
                    for r in range(R):
                        ins = dve.tensor_tensor(stack[3][:, r * D:(r + 1) * D].rearrange("p (n h) -> p n h", n=N), k3, bc(w[:, 1, r, :], 2, HD), ALU.mult)
                    ins.then_inc(stack_ready, 1)
                    for r in range(R):
                        ins = dve.tensor_tensor(bt[:, r * D:(r + 1) * D].rearrange("p (m n) -> p m n", m=N),
                                                bc(w[:, 3, r, :], 2, N), bc(w[:, 3, 2 + r, :], 1, N), ALU.mult)
                    wait(done.mark(ins))
                    flat = Bp[:, t, :, :].rearrange("p m n -> p (m n)")
                    wait(done.mark(dve.tensor_tensor(flat, bt[:, 0:D], bt[:, D:2 * D], ALU.add)))
                    dve.tensor_copy(Vb[:, t, :], V[:, tile, :])
                    wait(done.mark(dve.tensor_tensor(flat[:, 0:N * N:N + 1], flat[:, 0:N * N:N + 1], DD[:, tile, 3 * N:4 * N], ALU.add)))
                    for i, dst in ((1, QW), (3, KW)):
                        dve.wait_ge(stack_mm, tile * 5 + i + 1)
                        dve.tensor_copy(dst[:, :, P * t:P * (t + 1)], bank[i][:, :].rearrange("p (a t) -> p a t", t=P)).then_inc(stack_dve, 1)
                for s in range(TI):
                    for r in range(R):
                        n = 4 * s + 2 * r + 1
                        dve.wait_ge(hh_mm, b * 16 + (n + 1))
                        dve.tensor_copy(HK[:, r, TRK[s]:TRK[s + 1]], bank[n % 8][:, 0:P * (TI - s)]).then_inc(hk_copied, 1)
                for r in range(R):
                    dve.memset(Hp[:, r, :], 0.0)
                wait(done.mark(dve.memset(O[:, :, :], 0.0)))
                dve.wait_ge(hq_copied, (b + 1) * 8)
                dve.sem_inc(dve_step, 1)

                with dve.Fori(0, G) as g:
                    saved_g = done.enter(g, PER_G)
                    base = (b * G + g) * HEADS
                    dve.wait_ge(group_ready, b * G + g + 1)

                    def query_term(k):
                        t, p, j = at(k)
                        yk = Y[:, k % 2, 0:P * (t + 1)]
                        dve.wait_ge(prod_ready, base + (k + 1))
                        return done.mark(dve.scalar_tensor_tensor(yk, HQ[:, 1, TRI[t]:TRI[t + 1]], Wq2[:, t, 1, 2 * p + j:2 * p + j + 1], yk, ALU.mult, ALU.add))

                    def logits(k, term):
                        t, p, j = at(k)
                        dve.wait_ge(logit_mm, base + (k + 1))
                        dve.wait_ge(pt_mm, base + (k - 3 + C_PT))
                        wait(term)
                        dve.sem_inc(dve_step, 1)
                        dve.tensor_tensor_reduce(out=X[:, k % 4, 0:P * (t + 1)], in0=bank[k % 4][:, 0:P * (t + 1)], in1=Y[:, k % 2, 0:P * (t + 1)],
                                                 scale=1.0, scalar=3e38, op0=ALU.add, op1=ALU.min,
                                                 accum_out=rowmin[:, k % 4:k % 4 + 1]).then_inc(logit_read, 1)

                    def probabilities(k):
                        t, p, j = at(k)
                        xk = X[:, k % 4, 0:P * (t + 1)]
                        dve.wait_ge(exp_done, base + (k + 1 + C_ONE))
                        wait(done.mark(dve.reciprocal(rsum[:, k % 4:k % 4 + 1], rowsum[:, k % 4:k % 4 + 1])))
                        dve.tensor_scalar(xk, xk, rsum[:, k % 4:k % 4 + 1], None, ALU.mult).then_inc(prob_ready, 1)
                        dve.wait_ge(prob_ready, base + (k + 1))
                        dve.wait_ge(hp_added, base + (k + C_ONE))
                        for r in range(R):
                            hp = Hp[:, r, TRI[t]:TRI[t + 1]]
                            ins = dve.scalar_tensor_tensor(hp, xk, Wp1[:, t, r, 2 * p + j:2 * p + j + 1], hp, ALU.mult, ALU.add)
                        ins.then_inc(hp_added, 1)

                    def outputs(u):
                        t, p = u % TI, u // TI
                        tile, n0 = b * TI + t, g * 4 + 2 * p
                        bk = bank[6 + u % 2]
                        dve.wait_ge(pv_mm, base + (2 * u + 2 + C_PV))
                        v = done.mark(dve.tensor_tensor(O[:, t, :], bk[:, 0:D], O[:, t, :], ALU.add))
                        dve.tensor_tensor(ou[:, u % 2, 0:2 * HD].rearrange("p (n h) -> p n h", n=2),
                                          bk[:, D:D + 2 * HD].rearrange("p (n h) -> p n h", n=2),
                                          bc(DD[:, tile, bass.ds(n0 + 2 * N, 2)], 2, HD), ALU.mult).then_inc(o_read, 1)
                        wait(v)
                        dve.wait_ge(o_read, (b * G + g) * 8 + (u + 1 + C_O))
                        on = O[:, t, bass.ds(n0 * HD, 2 * HD)]
                        done.mark(dve.tensor_tensor(on, on, ou[:, u % 2, 0:2 * HD], ALU.add))

                    for k in range(HEADS + 1):
                        if k < HEADS:
                            term = query_term(k)
                        if k >= 1:
                            probabilities(k - 1)
                        if k < HEADS:
                            logits(k, term)
                        if k >= 6 and k % 2 == 0:
                            outputs(k // 2 - 3)
                    for u in (6, 7):
                        outputs(u)
                    done.leave(saved_g, G, PER_G)

                wait(done.now())
                for t in range(TI):
                    tile = b * TI + t
                    w = weights_of(tile)
                    dve.wait_ge(hv_mm, tile + 1)
                    for r in range(R):
                        ins = dve.tensor_tensor(ou[:, r, :].rearrange("p (n h) -> p n h", n=N),
                                                bank[2][:, r * D:(r + 1) * D].rearrange("p (n h) -> p n h", n=N),
                                                bc(w[:, 2, 2 + r, :], 2, HD), ALU.mult)
                    wait(done.mark(ins))
                    wait(done.mark(dve.tensor_tensor(O[:, t, :], O[:, t, :], ou[:, 0, :], ALU.add)))
                    dve.tensor_tensor(O[:, t, :], O[:, t, :], ou[:, 1, :], ALU.add).then_inc(o_ready, 1)
                    dve.wait_ge(ao_mm, tile + 1)
                    wait(done.mark(dve.tensor_tensor(ou[:, 0, :], bank[3][:, D:2 * D], mod[:, b, 2 * D:3 * D], ALU.mult)))
                    dve.tensor_tensor(xs[:, tile, :], xs[:, tile, :], ou[:, 0, :], ALU.add).then_inc(x1_ready, 1)
                done.leave(saved_b, B, PER_B)

            dve.wait_ge(x1_ready, NT)
            layernorm_stats()
            rsqrt(2, NT, rstd[:, :])
            for t in range(NT):
                if t >= 2:
                    dve.wait_ge(h2_mm, t - 1)
                modulated(h[:, t % 2, :], t, t // TI, 4, 3).then_inc(h2_ready, 1)
            dve.wait_ge(r_mm, 1)
            wait(done.mark(dve.tensor_copy(rl[:, :, :], bank[2][:, 0:NT * E].rearrange("p (t e) -> p t e", e=E))))
            wait(done.mark(dve.tensor_reduce(rbest[:, :], rl[:, :, :], AX.X, ALU.max)))
            dve.tensor_tensor(rone[:, :, :], rl[:, :, :], bc(rbest[:, :], 2, E), ALU.is_equal).then_inc(r_max, 1)
            dve.wait_ge(r_max, 1)
            wait(done.mark(dve.tensor_scalar(rl[:, :, :], bc(eio[:, :], 1, NT), -float(E), None, ALU.add)))
            wait(done.mark(dve.tensor_tensor(rone[:, :, :], rone[:, :, :], rl[:, :, :], ALU.mult)))
            wait(done.mark(dve.tensor_reduce(rstd[:, :], rone[:, :, :], AX.X, ALU.min)))
            wait(done.mark(dve.tensor_tensor(rone[:, :, :], rl[:, :, :], bc(rstd[:, :], 2, E), ALU.is_equal)))
            dve.wait_ge(half_ready, 1)
            wait(done.mark(dve.tensor_scalar(rbest[:, :], rbest[:, :], 0.5, 0.5, ALU.mult, ALU.add)))
            dve.memset(half[:, :, 0:1], 0.5)
            dve.memset(pick[:, :, 0:1], 0.5)
            done.mark(dve.tensor_scalar(half[:, :, 1:E + 1], bc(rbest[:, :], 2, E), 0.5, None, ALU.mult))
            wait(done.mark(dve.tensor_tensor(rone[:, :, :], rone[:, :, :], bc(rbest[:, :], 2, E), ALU.mult)))
            dve.tensor_tensor(pick[:, :, 1:E + 1], rone[:, :, :], half[:, :, 1:E + 1], ALU.mult).then_inc(pick_ready, 1)
            dve.wait_ge(pick_ready, 1)

            def experts(first, count):
                for k in range(NT * count):
                    e, t = first + k // NT, k % NT
                    dve.wait_ge(th_ready, first * NT + (k + 1))
                    wait(done.mark(dve.scalar_tensor_tensor(Y[:, t % 2, 0:F], Y[:, t % 2, 0:F], 1.0, bank[t % 2][:, 0:F], ALU.add, ALU.mult)))
                    dve.wait_ge(hmT_mm, first * NT + (k - 1 + C_E))
                    dve.scalar_tensor_tensor(X[:, t % 2, 0:F], bank[t % 2][:, F:2 * F], pick[:, t, bass.ds(e, 1)], Y[:, t % 2, 0:F], ALU.mult, ALU.mult).then_inc(hm_ready, 1)

            experts(0, 1)
            with dve.Fori(0, E // 2) as i:
                saved = done.enter(i, 2 * NT)
                experts(i * 2 + 1, 2)
                done.leave(saved, E // 2, 2 * NT)
            dve.wait_ge(dn_mm, NT * (E + 1) + C_E)
            for t in range(NT):
                wait(done.mark(dve.tensor_tensor(ou[:, t % 2, :], bank[4 + t // 2][:, (t % 2) * D:(t % 2 + 1) * D], mod[:, t // TI, 5 * D:6 * D], ALU.mult)))
                dve.tensor_tensor(xs[:, t, :], xs[:, t, :], ou[:, t % 2, :], ALU.add).then_inc(out_ready, 1)

        @block.tensor
        def _(pe):
            pe.sem_inc(pt_mm, C_PT)
            pe.sem_inc(pv_mm, C_PV)
            pe.sem_inc(hmT_mm, C_E)
            pe.sem_inc(dn_mm, C_E)
            pe.wait_ge(c_ready, 1)
            pe.wait_ge(d_wm, 16 * KT)
            for b in range(B):
                for j in range(3):
                    for k in range(KT):
                        mm = pe.matmul(bank[3 * b + j][:, :], c_rows[k * B + b], wmod_s[k][:, 512 * j:512 * j + 512], start=(k == 0), stop=(k == KT - 1))
                    mm.then_inc(mod_mm, 1)
            pe.wait_ge(pool_ready, 1)
            pe.wait_ge(d_w, 16 * 6)
            pe.wait_ge(mod_copied, 3 * B)

            with pe.Fori(0, B) as b:
                for t in range(TI):
                    tile, p = b * TI + t, t % 2
                    bk = bank[4 * p:4 * p + 4]
                    pe.wait_ge(h_ready, tile + 1)
                    pe.wait_ge(proj_copied, tile - 1 + C_E)
                    for k in range(KT):
                        mm = pe.transpose(bk[0][:, k * P:(k + 1) * P], h[:, p, k * P:(k + 1) * P], ident[:, :])
                    mm.then_inc(hT_mm, 1)
                    pe.wait_ge(hT_ready, tile + 1)
                    for c in range(C):
                        for k in range(KT):
                            mm = pe.matmul(bk[2][:, c * P:(c + 1) * P], dw1_s[:, k, c * P:(c + 1) * P], hT[:, p, k, :], start=(k == 0), stop=(k == KT - 1))
                    mm.then_inc(dwh_mm, 1)
                    for k in range(KT):
                        pe.matmul(bk[1][:, :], hT[:, p, k, :], wqkv_s[:, k, 0:2 * D], start=(k == 0), stop=(k == KT - 1))
                    for k in range(KT):
                        pe.matmul(bk[0][:, D:2 * D], hT[:, p, k, :], wqkv_s[:, k, 2 * D:3 * D], start=(k == 0), stop=(k == KT - 1))
                    for k in range(KT):
                        pe.matmul(bk[3][:, D:D + 64], hT[:, p, k, :], ddw_s[:, k, :], start=(k == 0), stop=(k == KT - 1))
                    pe.wait_ge(g_ready, tile + 1)
                    for c in range(C):
                        mm = pe.matmul(bk[3][:, c * M4:(c + 1) * M4], gh[:, p, c, :], qkw_s[:, c, :], start=True, stop=True)
                    mm.then_inc(proj_mm, 1)
            pe.wait_ge(proj_copied, NT + C_E)

            with pe.Fori(0, B) as b:
                for t in range(TI):
                    tile = b * TI + t
                    if t > 0:
                        pe.wait_ge(stack_act, 3 * tile)
                        pe.wait_ge(stack_dve, 2 * tile)
                    for i in range(4):
                        pe.wait_ge(stack_ready, 4 * tile + i + 1)
                        for a in range(4):
                            mm = pe.transpose(bank[i][:, a * P:(a + 1) * P], stack[i][:, a * P:(a + 1) * P], ident[:, :])
                        mm.then_inc(stack_mm, 1)
                    for a in range(4):
                        mm = pe.transpose(bank[4][:, a * P:(a + 1) * P], stack[4][:, a * P:(a + 1) * P], ident[:, :])
                    mm.then_inc(stack_mm, 1)
                pe.wait_ge(stack_act, (b + 1) * 3 * TI)
                pe.wait_ge(stack_dve, (b + 1) * 2 * TI)
                for t in range(TI):
                    for r in range(R):
                        for side in range(2):
                            n = 4 * t + 2 * r + side
                            bk = bank[n % 8]
                            if n == 8:
                                pe.wait_ge(hq_copied, b * 8 + 4)
                                pe.wait_ge(hk_copied, b * 8 + 4)
                            for k in range(KT):
                                if side == 0:
                                    mm = pe.matmul(bk[:, 0:P * (t + 1)], QW[:, r * KT + k, P * t:P * (t + 1)], KTr[:, k, 0:P * (t + 1)], start=(k == 0), stop=(k == KT - 1))
                                else:
                                    mm = pe.matmul(bk[:, 0:P * (TI - t)], KW[:, r * KT + k, P * t:P * (t + 1)], QT[:, k, P * t:T], start=(k == 0), stop=(k == KT - 1))
                            mm.then_inc(hh_mm, 1)
                pe.wait_ge(hq_copied, (b + 1) * 8)
                pe.wait_ge(hk_copied, (b + 1) * 8)
                pe.sem_inc(pe_step, 1)

                with pe.Fori(0, G) as g:
                    base = (b * G + g) * HEADS
                    pe.wait_ge(group_ready, b * G + g + 1)

                    def logits(k):
                        t, p, j = at(k)
                        row = 32 * (2 * p + j)
                        bk = bank[k % 4]
                        if k % 8 == 0:
                            pe.wait_ge(pair_ready, (b * G + g) * 2 + (p + 1 + C_ONE))
                        pe.wait_ge(logit_read, base + (k - 3 + C_LOGIT))
                        pe.matmul(bk[:, 0:P * (t + 1)], QCg[row:row + 32, P * t:P * (t + 1)], KCg[row:row + 32, 0:P * (t + 1)],
                                  start=True, stop=False, tile_position=(row, 0))
                        for s in range(t + 1):
                            for r in range(R):
                                off = TRK[s] + P * (t - s)
                                pe.matmul(bk[:, s * P:(s + 1) * P], HK[:, r, off:off + P], DG[:, p, s, r, j, :], start=False, stop=False)
                        pe.matmul(bk[:, t * P:(t + 1) * P], ident_b[:, :], mask_b[:, :], start=False, stop=True).then_inc(logit_mm, 1)

                    def transposes(k):
                        t, p, j = at(k)
                        pe.wait_ge(prob_ready, base + (k + 1))
                        pe.wait_ge(pt_ready, base + (k - 1 + C_E))
                        for s in range(t + 1):
                            mm = pe.transpose(bank[4 + k % 2][:, s * P:(s + 1) * P], X[:, k % 4, s * P:(s + 1) * P], ident[:, :])
                        mm.then_inc(pt_mm, 1)

                    def values(k):
                        t, p, j = at(k)
                        u = k // 2
                        bk = bank[6 + u % 2]
                        if j == 0:
                            pe.wait_ge(o_read, (b * G + g) * 8 + (u - 1 + C_O))
                        pe.wait_ge(pt_ready, base + (k + 1 + C_E))
                        for s in range(t + 1):
                            pe.matmul(bk[:, 0:D], PT[:, k % 2, s * P:(s + 1) * P], VP[:, p, s, j, :],
                                      start=(j == 0 and s == 0), stop=(j == 1 and s == t), skip_group_check=True)
                        for s in range(t + 1):
                            mm = pe.matmul(bk[:, D + j * HD:D + (j + 1) * HD], PT[:, k % 2, s * P:(s + 1) * P], Vb[:, s, bass.ds((g * 4 + (2 * p + j)) * HD, HD)],
                                           start=False, stop=(s == t), skip_group_check=True)
                        mm.then_inc(pv_mm, 1)

                    for k in range(HEADS + 3):
                        if k < HEADS:
                            logits(k)
                        if 2 <= k < HEADS + 2:
                            transposes(k - 2)
                        if k >= 3:
                            values(k - 3)

                pe.wait_ge(hp_added, (b + 1) * G * HEADS + C_ONE)
                for t in range(TI):
                    tile = b * TI + t
                    if t > 0:
                        pe.wait_ge(x1_ready, tile)
                    for r in range(R):
                        for s in range(t + 1):
                            mm = pe.transpose(bank[r][:, s * P:(s + 1) * P], Hp[:, r, TRI[t] + s * P:TRI[t] + (s + 1) * P], ident[:, :])
                        mm.then_inc(hp_mm, 1)
                    pe.wait_ge(hp_ready, b * 8 + (2 * t + 2))
                    for r in range(R):
                        for s in range(t + 1):
                            mm = pe.matmul(bank[2][:, r * D:(r + 1) * D], X[:, r, s * P:(s + 1) * P], Vb[:, s, :], start=(s == 0), stop=(s == t))
                    mm.then_inc(hv_mm, 1)
                    pe.wait_ge(o_ready, tile + 1)
                    for k in range(KT):
                        mm = pe.transpose(bank[3][:, k * P:(k + 1) * P], O[:, t, k * P:(k + 1) * P], ident[:, :])
                    mm.then_inc(oT_mm, 1)
                    pe.wait_ge(oT_ready, tile + 1)
                    for k in range(KT):
                        mm = pe.matmul(bank[3][:, D:2 * D], hT[:, 0, k, :], woT_s[:, k, :], start=(k == 0), stop=(k == KT - 1))
                    mm.then_inc(ao_mm, 1)

            for t in range(NT):
                pe.wait_ge(h2_ready, t + 1)
                if t >= 2:
                    pe.wait_ge(h2_T, t - 1)
                for k in range(KT):
                    mm = pe.transpose(bank[t % 2][:, k * P:(k + 1) * P], h[:, t % 2, k * P:(k + 1) * P], ident[:, :])
                mm.then_inc(h2_mm, 1)
            pe.wait_ge(h2_T, NT)
            for t in range(NT):
                for k in range(KT):
                    mm = pe.matmul(bank[2][:, t * E:(t + 1) * E], x2T[:, k, P * t:P * (t + 1)], rw_s[:, k, :], start=(k == 0), stop=(k == KT - 1))
            mm.then_inc(r_mm, 1)
            pe.wait_ge(r_max, 1)

            def experts(first, count, slots, landed, fresh):
                def gate_up(k):
                    t = k % NT
                    w, _ = expert_slot(slots[k // NT])
                    if t == 0:
                        pe.wait_ge(d_gu[slots[k // NT]], landed[k // NT])
                    pe.wait_ge(hm_ready, first * NT + (k - 1 + C_E))
                    for c in range(KT):
                        mm = pe.matmul(bank[t % 2][:, :], x2T[:, c, P * t:P * (t + 1)], w[:, c, :], start=(c == 0), stop=(c == KT - 1))
                    mm.then_inc(gu_mm, 1)

                def transposes(k):
                    t = k % NT
                    pe.wait_ge(hm_ready, first * NT + (k + 1 + C_E))
                    pe.wait_ge(hmT_ready, first * NT + (k - 1 + C_E))
                    for c in range(KT):
                        mm = pe.transpose(bank[2 + t % 2][:, c * P:(c + 1) * P], X[:, t % 2, c * P:(c + 1) * P], ident[:, :])
                    mm.then_inc(hmT_mm, 1)

                def down(k):
                    t = k % NT
                    _, w = expert_slot(slots[k // NT])
                    pe.wait_ge(hmT_ready, first * NT + (k + 1 + C_E))
                    for c in range(KT):
                        mm = pe.matmul(bank[4 + t // 2][:, (t % 2) * D:(t % 2 + 1) * D], hT[:, t % 2, c, :], w[:, c, :],
                                       start=(fresh and t % 2 == 0 and c == 0), stop=(c == KT - 1), skip_group_check=True)
                    mm.then_inc(dn_mm, 1)

                for k in range(NT * count + 2):
                    if k < NT * count:
                        gate_up(k)
                    if 1 <= k < NT * count + 1:
                        transposes(k - 1)
                    if k >= 2:
                        down(k - 2)

            experts(0, 1, [0], [48], True)
            with pe.Fori(0, E // 2) as i:
                experts(i * 2 + 1, 2, [1, 0], [i * 48 + 48, i * 48 + 96], False)


def kernel(L0_attn_x, L0_attn_w_qkv, L0_attn_w_o, L0_attn_dw1, L0_attn_qkw, L0_attn_dd_w, L0_ffn_router_w,
           L0_ffn_gate_w, L0_ffn_up_w, L0_ffn_down_w, L0_ffn_shared_gate_w, L0_ffn_shared_up_w,
           L0_ffn_shared_down_w, L0_c, L0_wmod):
    import numpy as np
    import concourse.bacc as bacc
    from concourse import mybir as mb
    from concourse.bass_utils import run_bass_kernel_spmd

    x = np.asarray(L0_attn_x)
    b, t, d = x.shape
    laid_out = [
        ("x", x.reshape(b * t, d)),
        ("w_qkv", np.asarray(L0_attn_w_qkv)),
        ("w_oT", np.asarray(L0_attn_w_o).T),
        ("dw1", np.asarray(L0_attn_dw1).reshape(d, -1)),
        ("qkw", np.asarray(L0_attn_qkw).reshape(4, 128, -1)),
        ("dd_w", np.asarray(L0_attn_dd_w).reshape(d, -1)),
        ("router_w", np.asarray(L0_ffn_router_w)),
        ("gate_w", np.asarray(L0_ffn_gate_w)),
        ("up_w", np.asarray(L0_ffn_up_w)),
        ("down_w", np.asarray(L0_ffn_down_w)),
        ("shared_gate", np.asarray(L0_ffn_shared_gate_w)),
        ("shared_up", np.asarray(L0_ffn_shared_up_w)),
        ("shared_down", np.asarray(L0_ffn_shared_down_w)),
        ("cT", np.asarray(L0_c).T),
        ("wmod", np.asarray(L0_wmod)),
    ]
    nc = bacc.Bacc("TRN2", target_bir_lowering=False, num_devices=1)
    arrays, args = {}, []
    for name, a in laid_out:
        a = np.ascontiguousarray(a)
        arrays["in_" + name] = a
        args.append(nc.dram_tensor("in_" + name, a.shape, mb.dt.from_np(a.dtype), kind="ExternalInput").ap())
    out = nc.dram_tensor("out_x", (b * t, d), mb.dt.float32, kind="ExternalOutput").ap()
    adaln_layer(nc, *args, out)
    r = run_bass_kernel_spmd(nc, [arrays], core_ids=[0])
    return r.results[0]["out_x"].reshape(b, t, d)
```

```python
import concourse.bass as bass
from concourse import mybir
from contextlib import ExitStack, contextmanager

P = 128
F32 = mybir.dt.float32
BF16 = mybir.dt.bfloat16
ALU = mybir.AluOpType
ACT = mybir.ActivationFunctionType
AX = mybir.AxisListType
MASKED = 1e30


class Done:

    def __init__(self, sem):
        self.sem, self.base, self.n = sem, 0, 0

    def mark(self, ins, by=1):
        ins.then_inc(self.sem, by)
        self.n += by
        return self.base + self.n

    def now(self):
        return self.base + self.n

    def enter(self, var, per):
        saved = (self.base, self.n)
        self.base, self.n = self.base + self.n + var * per, 0
        return saved

    def leave(self, saved, times, per):
        assert self.n == per, (self.n, per)
        self.base, self.n = saved[0], saved[1] + times * per


def adaln_layer(nc, x, w_qkv, w_oT, dw1, qkw, dd_w, router_w, gate_w, up_w, down_w,
                shared_gate, shared_up, shared_down, cT, wmod, slots_in, slots_out, out):
    BT, D = x.shape
    B = cT.shape[1]
    T = BT // B
    NT = BT // P
    TI = T // P
    KT = D // P
    C, _, M4 = qkw.shape
    N = M4 // 4
    HD = D // N
    R = 2
    G = N // 4
    E = router_w.shape[1]
    F = gate_w.shape[2]
    NSLOT = slots_in.shape[0] // P
    EW = KT * 2 * F + (F // P) * D
    QSCALE = -float(HD) ** -0.5
    LN_EPS, RMS_EPS = 1e-5, 1e-6
    TRI = [P * (t * (t + 1) // 2) for t in range(TI + 1)]
    TRK = [P * (TI * s - s * (s - 1) // 2) for s in range(TI + 1)]
    assert D == 256 and N == 16 and C == 4 and TI == 4 and F == D and E == 8
    assert NSLOT * P >= BT + E * (P - 1) and NSLOT % 4 == 0

    with ExitStack() as ctx:
        def sb(name, shape, dt=F32):
            return ctx.enter_context(nc.sbuf_tensor(name, shape, dt))

        def sem(name):
            return ctx.enter_context(nc.semaphore(name))

        bank = [ctx.enter_context(nc.psum_tensor(f"bank{i}", [P, 512], F32)) for i in range(8)]

        xs = sb("xs", [P, NT, D])
        mod = sb("mod", [P, B, 6 * D])
        ident = sb("ident", [P, P])
        ident_b = sb("ident_b", [P, P], BF16)
        mask_b = sb("mask_b", [P, P], BF16)
        ones = sb("ones", [P, P])
        stats = sb("stats", [P, NT, 6])
        mean_var = sb("mean_var", [P, NT, 2])
        nw = sb("nw", [P, 3, 64])
        rstd = sb("rstd", [P, NT])
        rrms = sb("rrms", [P, 64])
        early = sb("early", [P, KT * 3 * D + KT * C * P])
        wqkv_s = early[:, 0:KT * 3 * D].rearrange("p (k n) -> p k n", k=KT)
        dw1_s = early[:, KT * 3 * D:].rearrange("p (k n) -> p k n", k=KT)
        qkw_s = sb("qkw_s", [P, C, M4])
        ddw_s = sb("ddw_s", [P, KT, 64])
        woT_s = sb("woT_s", [P, KT, D])
        c_s = sb("c_s", [P, KT * B])
        c_e = sb("c_e", [P, 3, KT * B])
        W = sb("W", [P, NT, C * M4])
        DD = sb("DD", [P, NT, 64])
        big = sb("big", [P, E * EW])
        cut = [0]

        def part(*shape):
            n = shape[0] * shape[1]
            cut[0] += n
            return big[:, cut[0] - n:cut[0]].rearrange("p (a b) -> p a b", a=shape[0])

        V = part(NT, D)
        QK = part(NT, 2 * D)
        QT = part(KT, T)
        KTr = part(KT, T)
        QW = part(R * KT, T)
        KW = part(R * KT, T)
        assert cut[0] <= E * EW
        QC = sb("QC", [P, G, T])
        KC = sb("KC", [P, G, T])
        HQ = sb("HQ", [P, R, TRI[TI]])
        HK = sb("HK", [P, R, TRK[TI]])
        Hp = early[:, :].rearrange("p (r n) -> p r n", r=R)
        O = sb("O", [P, TI, D])
        Bp = sb("Bp", [P, TI, N, N])
        Vb = sb("Vb", [P, TI, D])
        QCg = sb("QCg", [P, T])
        KCg = sb("KCg", [P, T])
        Wq2 = sb("Wq2", [P, TI, R, 4])
        Wp1 = sb("Wp1", [P, TI, R, 4])
        Wk2 = sb("Wk2", [P, TI, R, 4])
        DG = sb("DG", [P, 2, TI, R, 2, P])
        VP = sb("VP", [P, 2, TI, 2, D])
        X = sb("X", [P, 4, T])
        Y = sb("Y", [P, 2, T])
        PT = sb("PT", [P, 2, T])
        rowmin = sb("rowmin", [P, 4])
        rowsum = sb("rowsum", [P, 4])
        rsum = sb("rsum", [P, 4])
        ou = sb("ou", [P, 2, D])
        c_rows = [Y[:, i // 2, D + P * (i % 2):D + P * (i % 2) + P] for i in range(KT * B)]
        hT = sb("hT", [P, 2, KT, P])
        h = Y[:, :, 0:D]
        late = DG[:, 1, :, :, :, :].rearrange("p a b c d -> p (a b c d)")
        gl = late[:, 0:1024].rearrange("p (a n) -> p a n", a=2)
        gh = late[:, 1024:2048].rearrange("p (a c t) -> p a c t", a=2, c=C)

        wmod_s = [QC[:, :, :].rearrange("p a b -> p (a b)")[:, 0:6 * D],
                  KC[:, :, :].rearrange("p a b -> p (a b)")[:, 0:6 * D]]
        stackv = VP[:, :, :, :, :].rearrange("p a b c d -> p (a b c d)")
        stack = [stackv[:, 512 * i:512 * i + 512] for i in range(5)]
        sq = DG[:, 0, :, :, :, :].rearrange("p a b c d -> p (a b c d)")[:, 0:1024]
        bt = DG[:, 1, :, :, :, :].rearrange("p a b c d -> p (a b c d)")[:, 0:512]
        shared_s = QC[:, :, :].rearrange("p a b -> p (a b)")[:, 0:EW]
        x2T = late.rearrange("p (k t) -> p k t", k=KT)
        rows = stackv[:, 0:NT * D].rearrange("p (t d) -> p t d", d=D)
        back = stackv[:, NT * D:2 * NT * D].rearrange("p (t d) -> p t d", d=D)
        zeros = stackv[:, 3 * 1024:3 * 1024 + D]
        RING = 4
        slot_x = sq.rearrange("p (r d) -> p r d", r=RING)
        slot_y = Bp[:, :, :, :].rearrange("p s m n -> p s (m n)")
        slot_xT = O[:, 0:2, :].rearrange("p s (k t) -> p s k t", k=KT)
        rl = sb("rl", [P, NT, E])
        rbest = sb("rbest", [P, NT])
        rone = sb("rone", [P, NT, E])
        rank = sb("rank", [P, NT, E])
        eio = sb("eio", [P, E])
        rw_s = sb("rw_s", [P, KT, E])
        before = sb("before", [P, P])
        start_of = sb("start_of", [P, NT])
        below = sb("below", [P, E, E])
        slot_no = sb("slot_no", [P, NSLOT])
        tiles_of = sb("tiles_of", [P, 3, E])
        ecmp = sb("ecmp", [P, NSLOT * E])
        slot_e = sb("slot_e", [P, NSLOT])
        slot_expert = sb("slot_expert", [P, NSLOT], mybir.dt.int32)
        row_f = sb("row_f", [P, NT])
        row_of = sb("row_of", [P, NT], mybir.dt.uint32)

        d_x, d_c, d_wm, d_w, d_out = (sem(n) for n in ("d_x", "d_c", "d_wm", "d_w", "d_out"))
        d_zero, d_gu, d_shared, d_scatter = sem("d_zero"), sem("d_gu"), sem("d_shared"), sem("d_scatter")
        d_slot = [sem(f"d_slot{i}") for i in range(RING)]
        d_y = [sem(f"d_y{i}") for i in range(RING)]
        d_back = [sem(f"d_back{i}") for i in range(NT)]
        dve_done, pool_done = sem("dve_done"), sem("pool_done")
        dve_step, pe_step = sem("dve_step"), sem("pe_step")
        pool_ready, ones_ready = sem("pool_ready"), sem("ones_ready")
        c_exp, c_ready, mod_mm, mod_copied = (sem(n) for n in ("c_exp", "c_ready", "mod_mm", "mod_copied"))
        var_ready, root_ready = sem("var_ready"), sem("root_ready")
        h_ready, hT_mm, hT_ready = sem("h_ready"), sem("hT_mm"), sem("hT_ready")
        dwh_mm, g_sq, g_arg, g_tanh, g_ready = (sem(n) for n in ("dwh_mm", "g_sq", "g_arg", "g_tanh", "g_ready"))
        proj_mm, proj_copied = sem("proj_mm"), sem("proj_copied")
        stack_ready, stack_mm, stack_act, stack_dve = (sem(n) for n in ("stack_ready", "stack_mm", "stack_act", "stack_dve"))
        hh_mm, hq_copied, hk_copied = sem("hh_mm"), sem("hq_copied"), sem("hk_copied")
        rows_ready, wk2_ready, pair_ready = sem("rows_ready"), sem("wk2_ready"), sem("pair_ready")
        logit_mm, logit_read, prod_ready = sem("logit_mm"), sem("logit_read"), sem("prod_ready")
        exp_done, prob_ready, hp_added = sem("exp_done"), sem("prob_ready"), sem("hp_added")
        pt_mm, pt_ready, pv_mm, o_read = sem("pt_mm"), sem("pt_ready"), sem("pv_mm"), sem("o_read")
        hp_mm, hp_ready, hv_mm = sem("hp_mm"), sem("hp_ready"), sem("hv_mm")
        o_ready, oT_mm, oT_ready, ao_mm, x1_ready = (sem(n) for n in ("o_ready", "oT_mm", "oT_ready", "ao_mm", "x1_ready"))
        h2_ready, h2_mm, h2_T, r_mm, r_max = (sem(n) for n in ("h2_ready", "h2_mm", "h2_T", "r_mm", "r_max"))
        half_ready, one_ready, rank_mm, rows_scaled, route_ready, slot_known = (
            sem(n) for n in ("half_ready", "one_ready", "rank_mm", "rows_scaled", "route_ready", "slot_known"))
        xT_mm, xT_ready, y_ready, zeros_ready = sem("xT_mm"), sem("xT_ready"), sem("y_ready"), sem("zeros_ready")
        gu_mm, th_ready, hm_ready, hmT_mm, hmT_ready, dn_mm, dn_read, out_ready = (
            sem(n) for n in ("gu_mm", "th_ready", "hm_ready", "hmT_mm", "hmT_ready", "dn_mm", "dn_read", "out_ready"))
        C_LOGIT, C_PT, C_PV, C_EXP, C_HP, C_O, C_ONE, C_E = 4, 4, 16, 16, 16, 2, 1, 2

        HEADS = 16

        def at(k):
            return (k % 8) // 2, k // 8 % 2, k % 2

        @contextmanager
        def counted(done, loop, times, per):
            with loop as var:
                saved = done.enter(var, per)
                yield var
                done.leave(saved, times, per)

        def run_groups(fori, step, lag):
            for k in range(lag):
                step(0, k, False)
            with fori(0, G - 1) as g:
                for k in range(lag, HEADS + lag):
                    step(g, k, False)
            for k in range(lag, HEADS + lag):
                step(G - 1, k, True)

        def bc(ap, axis, n):
            a = ap.unsqueeze(axis)
            shape = list(a.shape)
            shape[axis] = n
            return a.broadcast_to(shape)

        def weights_of(tile):
            return W[:, bass.ds(tile, 1), :].rearrange("p a (c i n) -> p (a c) i n", c=C, i=4)

        def expert_weights(base, e=None):
            if e is None:
                w = base
            else:
                w = base[:, bass.ds(e * EW, EW)]
            return (w[:, 0:2 * KT * F].rearrange("p (k n) -> p k n", k=KT),
                    w[:, 2 * KT * F:EW].rearrange("p (k n) -> p k n", k=F // P))

        LAG = 3

        def run_experts(fori, step):
            for j in range(-NT, LAG):
                step(0, j, False)
            with fori(0, NSLOT // RING - 1) as i:
                for j in range(LAG, RING + LAG):
                    step(i, j, False)
            for j in range(LAG, RING + LAG):
                step(NSLOT // RING - 1, j, True)

        def there(j, last):
            return j >= -NT and (j < RING or not last)

        block = ctx.enter_context(nc.Block())

        @block.sync
        def _(sp):
            sp.dma_start(c_s[:, :].rearrange("p (k b) -> p k b", k=KT),
                         cT.rearrange("(k p) b -> p k b", p=P)).then_inc(d_c, 16)
            for k in range(KT):
                sp.dma_start(wmod_s[k], wmod[P * k:P * (k + 1), :]).then_inc(d_wm, 16)
            sp.dma_start(xs[:, :, :], x.rearrange("(a p) d -> p a d", p=P)).then_inc(d_x, 16)
            sp.dma_start(wqkv_s[:, :, :], w_qkv.rearrange("(k p) n -> p k n", p=P)).then_inc(d_w, 16)
            sp.dma_start(dw1_s[:, :, :], dw1.rearrange("(k p) n -> p k n", p=P)).then_inc(d_w, 16)
            sp.dma_start(qkw_s[:, :, :], qkw.rearrange("c k m -> k c m")).then_inc(d_w, 16)
            sp.dma_start(ddw_s[:, :, :], dd_w.rearrange("(k p) n -> p k n", p=P)).then_inc(d_w, 16)
            sp.dma_start(woT_s[:, :, :], w_oT.rearrange("(k p) n -> p k n", p=P)).then_inc(d_w, 16)
            sp.dma_start(rw_s[:, :, :], router_w.rearrange("(k p) n -> p k n", p=P)).then_inc(d_w, 16)

            sp.wait_ge(zeros_ready, 1)
            sp.dma_start(slots_in.rearrange("(a p) d -> p a d", p=P), bc(zeros, 1, NSLOT)).then_inc(d_zero, 16)

            def load_expert(base, gate, up, down, landed):
                g, d = expert_weights(base)
                sp.dma_start(g[:, :, 0:F], gate.rearrange("(k p) n -> p k n", p=P)).then_inc(landed, 16)
                sp.dma_start(g[:, :, F:2 * F], up.rearrange("(k p) n -> p k n", p=P)).then_inc(landed, 16)
                sp.dma_start(d, down.rearrange("(k p) n -> p k n", p=P)).then_inc(landed, 16)

            sp.wait_ge(hh_mm, B * 16)
            sp.wait_ge(hk_copied, B * 8)
            for e in range(E):
                load_expert(big[:, e * EW:(e + 1) * EW], gate_w[e], up_w[e], down_w[e], d_gu)
            sp.wait_ge(pair_ready, B * G * 2 + C_ONE)
            load_expert(shared_s, shared_gate, shared_up, shared_down, d_shared)
            for r in range(RING):
                sp.sem_inc(d_y[r], 16)
            with sp.Fori(0, NSLOT // RING) as i:
                for r in range(RING):
                    sp.wait_ge(y_ready, i * RING + (r + 1))
                    sp.dma_start(slots_out[bass.ds(i * (RING * P) + r * P, P), :], slot_y[:, r, :]).then_inc(d_y[r], 16)
            for t in range(NT):
                sp.wait_ge(out_ready, t + 1)
                sp.dma_start(out[P * t:P * (t + 1), :], xs[:, t, :]).then_inc(d_out, 16)
            sp.wait_ge(d_out, 16 * NT)

        @block.gpsimd
        def _(pool):
            pool.memset(ident[:, :], 0.0)
            pool.memset(mask_b[:, :], 0.0)
            pool.memset(ident_b[:, :], 0.0).then_inc(pool_done, 1)
            pool.wait_ge(pool_done, 1)
            for m in (ident, ident_b):
                pool.affine_select(out=m[:, :], in_=m[:, :], compare_op=ALU.not_equal, fill=1.0,
                                   base=0, pattern=[[-1, P]], channel_multiplier=1)
            pool.affine_select(out=mask_b[:, :], in_=mask_b[:, :], compare_op=ALU.is_ge, fill=MASKED,
                               base=0, pattern=[[-1, P]], channel_multiplier=1)
            pool.memset(zeros, 0.0).then_inc(zeros_ready, 1)
            pool.memset(before[:, :], 1.0)
            pool.memset(below[:, :, :], 1.0).then_inc(pool_done, 1)
            pool.wait_ge(pool_done, 2)
            pool.affine_select(out=before[:, :], in_=before[:, :], compare_op=ALU.is_ge, fill=0.0,
                               base=-1, pattern=[[1, P]], channel_multiplier=-1)
            pool.affine_select(out=below[:, :, :], in_=below[:, :, :], compare_op=ALU.is_ge, fill=0.0,
                               base=-1, pattern=[[1, E], [-1, E]], channel_multiplier=0)
            pool.iota(start_of[:, :], pattern=[[P, NT]], base=0, channel_multiplier=0,
                      allow_small_or_imprecise_dtypes=True)
            pool.iota(slot_no[:, :], pattern=[[1, NSLOT]], base=0, channel_multiplier=0,
                      allow_small_or_imprecise_dtypes=True)
            pool.iota(eio[:, :], pattern=[[1, E]], base=0, channel_multiplier=0,
                      allow_small_or_imprecise_dtypes=True).then_inc(pool_ready, 1)
            pool.wait_ge(pool_ready, 1)
            pool.sem_inc(pair_ready, C_ONE)

            pool.wait_ge(d_zero, 16)
            with pool.Fori(0, B) as b:
                with pool.Fori(0, G) as g:
                    bg = b * G + g

                    pool.wait_ge(stack_act, (b + 1) * 3 * TI)
                    pool.wait_ge(stack_dve, (b + 1) * 2 * TI)
                    for p in range(2):
                        def copy_rows(dst, c, i):
                            src = W[:, bass.ds(b * TI, TI), bass.ds(g * 4 + (c * M4 + i * N + 2 * p), N + 2)]
                            for r in range(R):
                                last = pool.tensor_copy(dst[:, :, r, 2 * p:2 * p + 2], src[:, :, r * N:r * N + 2])
                            return last

                        pool.wait_ge(pair_ready, bg * 2 + p + C_ONE)
                        pool.wait_ge(exp_done, bg * HEADS + (8 * p + 8 - HEADS + C_EXP))
                        pool.wait_ge(hp_added, bg * HEADS + (8 * p + 8 - HEADS + C_HP))
                        pool.wait_ge(pv_mm, bg * HEADS + (8 * p + 8 - HEADS + C_PV))
                        pool.tensor_copy(QCg[64 * p:64 * p + 64, :], QC[64 * p:64 * p + 64, g, :])
                        pool.tensor_copy(KCg[64 * p:64 * p + 64, :], KC[64 * p:64 * p + 64, g, :]).then_inc(rows_ready, 1)
                        pool.wait_ge(rows_ready, bg * 2 + p + 1)
                        copy_rows(Wq2, 0, 2)
                        copy_rows(Wp1, 2, 0)
                        copy_rows(Wk2, 1, 2).then_inc(wk2_ready, 1)
                        pool.wait_ge(wk2_ready, bg * 2 + p + 1)
                        for s in range(TI):
                            for r in range(R):
                                pool.tensor_tensor(DG[:, p, s, r, :, :], bc(ident[:, :], 1, 2),
                                                   bc(Wk2[:, s, r, 2 * p:2 * p + 2], 2, P), ALU.mult)
                            for j in range(2):
                                m = g * 4 + (2 * p + j)
                                last = pool.tensor_tensor(
                                    VP[:, p, s, j, :].rearrange("p (n h) -> p n h", n=N),
                                    Vb[:, s, :].rearrange("p (n h) -> p n h", n=N),
                                    bc(Bp[:, s, bass.ds(m, 1), :].rearrange("p a n -> p (a n)"), 2, HD), ALU.mult)
                        last.then_inc(pair_ready, 1)

            pool.wait_ge(route_ready, 1)
            for t in range(NT):
                pool.wait_ge(rows_scaled, t + 1)
                pool.indirect_dma_start(out=slots_in[:, :], out_offset=bass.IndirectOffsetOnAxis(ap=row_of[:, t:t + 1], axis=0),
                                        in_=rows[:, t, :], in_offset=None).then_inc(d_scatter, 16)
            pool.wait_ge(d_scatter, 16 * NT)
            for r in range(RING):
                pool.dma_start(slot_x[:, r, :], slots_in[P * r:P * (r + 1), :]).then_inc(d_slot[r], 16)
            with pool.Fori(0, NSLOT // RING - 1) as i:
                for r in range(RING):
                    pool.wait_ge(xT_mm, i * RING + (r + 1))
                    pool.dma_start(slot_x[:, r, :], slots_in[bass.ds(i * (RING * P) + (RING + r) * P, P), :]).then_inc(d_slot[r], 16)
            for r in range(RING):
                pool.wait_ge(d_y[r], 16 * (NSLOT // RING + 1))
            for t in range(NT):
                pool.indirect_dma_start(out=back[:, t, :], out_offset=None, in_=slots_out[:, :],
                                        in_offset=bass.IndirectOffsetOnAxis(ap=row_of[:, t:t + 1], axis=0)).then_inc(d_back[t], 16)

        @block.scalar
        def _(act):
            act.sem_inc(exp_done, C_EXP)
            act.sem_inc(pt_ready, C_E)
            act.sem_inc(hmT_ready, C_E)
            act.sem_inc(xT_ready, C_E)
            act.sem_inc(proj_copied, C_E)
            act.wait_ge(d_c, 16)
            act.activation(c_e[:, 0, :], c_s[:, :], ACT.Exp, scale=-1.0).then_inc(c_exp, 1)
            for i in range(3 * B):
                act.wait_ge(mod_mm, i + 1)
                act.activation(mod[:, i // 3, 512 * (i % 3):512 * (i % 3) + 512], bank[i][:, :], ACT.Copy).then_inc(mod_copied, 1)

            def root(i, n):
                act.wait_ge(var_ready, i + 1)
                act.activation(nw[:, 1, 0:n], nw[:, 0, 0:n], ACT.Sqrt).then_inc(root_ready, 1)

            root(0, NT)

            with act.Fori(0, B) as b:
                for t in range(TI):
                    tile, p = b * TI + t, t % 2
                    bk = bank[4 * p:4 * p + 4]
                    act.wait_ge(hT_mm, tile + 1)
                    act.activation(hT[:, p, :, :], bk[0][:, 0:D].rearrange("p (k t) -> p k t", k=KT), ACT.Copy).then_inc(hT_ready, 1)
                    act.wait_ge(dwh_mm, tile + 1)
                    act.activation(gl[:, p, :], bk[2][:, :], ACT.Square).then_inc(g_sq, 1)
                    act.wait_ge(g_arg, tile + 1)
                    act.activation(gl[:, p, :], gl[:, p, :], ACT.Tanh, scale=0.7978845608028654).then_inc(g_tanh, 1)
                    act.wait_ge(proj_mm, tile + 1)
                    act.activation(QK[:, tile, 0:D], bk[1][:, 0:D], ACT.Copy, scale=QSCALE)
                    act.activation(QK[:, tile, D:2 * D], bk[1][:, D:2 * D], ACT.Copy)
                    act.activation(V[:, tile, :], bk[0][:, D:2 * D], ACT.Copy)
                    act.activation(DD[:, tile, :], bk[3][:, D:D + 64], ACT.Tanh)
                    act.activation(W[:, tile, :], bk[3][:, 0:D], ACT.Copy, scale=0.5).then_inc(proj_copied, 1)

            root(1, 64)

            with act.Fori(0, B) as b:
                for t in range(TI):
                    tile = b * TI + t
                    act.wait_ge(stack_mm, tile * 5 + 1)
                    act.activation(QC[:, :, P * t:P * (t + 1)], bank[0][:, :].rearrange("p (a t) -> p a t", t=P), ACT.Copy).then_inc(stack_act, 1)
                    act.wait_ge(stack_mm, tile * 5 + 3)
                    act.activation(KC[:, :, P * t:P * (t + 1)], bank[2][:, :].rearrange("p (a t) -> p a t", t=P), ACT.Copy).then_inc(stack_act, 1)
                    act.wait_ge(stack_mm, tile * 5 + 5)
                    act.activation(QT[:, :, P * t:P * (t + 1)], bank[4][:, 0:2 * P].rearrange("p (a t) -> p a t", t=P), ACT.Copy)
                    act.activation(KTr[:, :, P * t:P * (t + 1)], bank[4][:, 2 * P:4 * P].rearrange("p (a t) -> p a t", t=P), ACT.Copy).then_inc(stack_act, 1)
                for t in range(TI):
                    for r in range(R):
                        n = 4 * t + 2 * r
                        act.wait_ge(hh_mm, b * 16 + (n + 1))
                        act.activation(HQ[:, r, TRI[t]:TRI[t + 1]], bank[n % 8][:, 0:P * (t + 1)], ACT.Copy).then_inc(hq_copied, 1)
                act.wait_ge(hq_copied, (b + 1) * 8)

                def step(g, k, last):
                    base = (b * G + g) * HEADS

                    def product(k):
                        t, p, j = at(k)
                        if k % 8 == 0:
                            act.wait_ge(pair_ready, (b * G + g) * 2 + (k // 8 + 1 + C_ONE))
                        act.wait_ge(logit_read, base + (k - 1 + C_LOGIT))
                        act.activation(Y[:, k % 2, 0:P * (t + 1)], HQ[:, 0, TRI[t]:TRI[t + 1]], ACT.Copy,
                                       scale=Wq2[:, t, 0, 2 * p + j:2 * p + j + 1]).then_inc(prod_ready, 1)

                    def exponential(k):
                        t, p, j = at(k)
                        xk = X[:, k % 4, 0:P * (t + 1)]
                        act.wait_ge(logit_read, base + (k + 1 + C_LOGIT))
                        act.activation(xk, xk, ACT.Exp, bias=rowmin[:, k % 4:k % 4 + 1], scale=-1.0,
                                       accum_out=rowsum[:, k % 4:k % 4 + 1]).then_inc(exp_done, 1)

                    def transposed(k):
                        t, p, j = at(k)
                        act.wait_ge(pt_mm, base + (k + 1 + C_PT))
                        act.wait_ge(pv_mm, base + (k - 1 + C_PV))
                        act.activation(PT[:, k % 2, 0:P * (t + 1)], bank[4 + k % 2][:, 0:P * (t + 1)], ACT.Copy).then_inc(pt_ready, 1)

                    if k == 0:
                        product(0)
                    if k + 1 < HEADS or not last:
                        product(k + 1)
                    if k < HEADS or not last:
                        exponential(k)
                    if k >= 2 and (k - 2 < HEADS or not last):
                        transposed(k - 2)

                run_groups(act.Fori, step, 2)

                for t in range(TI):
                    for r in range(R):
                        act.wait_ge(hp_mm, b * 8 + (2 * t + r + 1))
                        act.activation(X[:, r, 0:P * (t + 1)], bank[r][:, 0:P * (t + 1)], ACT.Copy).then_inc(hp_ready, 1)
                    act.wait_ge(oT_mm, b * TI + t + 1)
                    act.activation(hT[:, 0, :, :], bank[3][:, 0:D].rearrange("p (k t) -> p k t", k=KT), ACT.Copy).then_inc(oT_ready, 1)

            root(2, NT)
            for t in range(NT):
                act.wait_ge(h2_mm, t + 1)
                act.activation(x2T[:, :, P * t:P * (t + 1)], bank[t % 2][:, 0:D].rearrange("p (k t) -> p k t", k=KT), ACT.Copy).then_inc(h2_T, 1)
            act.wait_ge(r_max, 1)
            act.activation(rbest[:, :], rbest[:, :], ACT.Tanh, scale=0.5).then_inc(half_ready, 1)

            def step(i, j, last):
                def slot_transposed(j):
                    act.wait_ge(xT_mm, i * RING + (j + 1))
                    act.wait_ge(gu_mm, i * RING + (NT + j - 1))
                    act.activation(slot_xT[:, j % 2, :, :], bank[6 + j % 2][:, 0:D].rearrange("p (k t) -> p k t", k=KT), ACT.Copy).then_inc(xT_ready, 1)

                def tanh(j):
                    act.wait_ge(gu_mm, i * RING + (NT + j + 1))
                    act.wait_ge(hm_ready, i * RING + (NT + j - 1 + C_E))
                    act.activation(Y[:, j % 2, 0:F], bank[j % 2][:, 0:F], ACT.Tanh, scale=0.5).then_inc(th_ready, 1)

                def hidden_transposed(j):
                    act.wait_ge(hmT_mm, i * RING + (NT + j + 1 + C_E))
                    act.wait_ge(dn_mm, i * RING + (NT + j - 1 + C_E))
                    act.activation(hT[:, j % 2, :, :], bank[2 + j % 2][:, 0:F].rearrange("p (k t) -> p k t", k=KT), ACT.Copy).then_inc(hmT_ready, 1)

                if j >= 0 and there(j, last):
                    slot_transposed(j)
                if there(j - 2, last):
                    hidden_transposed(j - 2)
                if there(j - 1, last):
                    tanh(j - 1)

            run_experts(act.Fori, step)

        @block.vector
        def _(dve):
            done = Done(dve_done)

            def wait(v):
                dve.wait_ge(dve_done, v)

            dve.sem_inc(logit_read, C_LOGIT)
            dve.sem_inc(o_read, C_O)
            dve.sem_inc(hp_added, C_HP)
            dve.sem_inc(hm_ready, C_E)
            dve.sem_inc(dn_read, C_E)
            dve.memset(ones[:, :], 1.0).then_inc(ones_ready, 1)
            dve.wait_ge(ones_ready, 1)
            dve.wait_ge(c_exp, 1)
            wait(done.mark(dve.tensor_scalar(c_e[:, 1, :], c_e[:, 0, :], 1.0, None, ALU.add)))
            wait(done.mark(dve.reciprocal(c_e[:, 2, :], c_e[:, 1, :])))
            wait(done.mark(dve.tensor_tensor(c_e[:, 0, :], c_e[:, 2, :], c_s[:, :], ALU.mult)))
            for i in range(KT * B):
                ins = dve.tensor_scalar(c_rows[i], ones[:, :], c_e[:, 0, i:i + 1], None, ALU.mult)
            ins.then_inc(c_ready, 1)

            def layernorm_stats():
                for t in range(NT):
                    v = done.mark(dve.bn_stats(stats[:, t, :], xs[:, t, :]))
                wait(v)
                for t in range(NT):
                    v = done.mark(dve.bn_aggr(mean_var[:, t, :], stats[:, t, :]))
                wait(v)
                dve.tensor_scalar(nw[:, 0, 0:NT], mean_var[:, :, 1], LN_EPS, None, ALU.add).then_inc(var_ready, 1)

            def rsqrt(i, n, r):
                dve.wait_ge(root_ready, i + 1)
                wait(done.mark(dve.reciprocal(r, nw[:, 1, 0:n])))
                wait(done.mark(dve.tensor_tensor(nw[:, 2, 0:n], r, r, ALU.mult)))
                wait(done.mark(dve.tensor_tensor(nw[:, 2, 0:n], nw[:, 2, 0:n], nw[:, 0, 0:n], ALU.mult)))
                wait(done.mark(dve.tensor_scalar(nw[:, 2, 0:n], nw[:, 2, 0:n], -0.5, 1.5, ALU.mult, ALU.add)))
                wait(done.mark(dve.tensor_tensor(r, r, nw[:, 2, 0:n], ALU.mult)))

            dve.wait_ge(d_x, 16)
            layernorm_stats()
            rsqrt(0, NT, rstd[:, :])

            dve.wait_ge(mod_copied, 3 * B)
            for o in (1, 4):
                v = done.mark(dve.tensor_scalar(mod[:, :, o * D:(o + 1) * D], mod[:, :, o * D:(o + 1) * D], 1.0, None, ALU.add))
            for o in (2, 5):
                gate = mod[:, :, o * D:(o + 1) * D]
                up, low = (sq[:, i * B * D:(i + 1) * B * D].rearrange("p (b d) -> p b d", b=B) for i in range(2))
                done.mark(dve.tensor_scalar(up, gate, 0.0, None, ALU.is_ge))
                wait(done.mark(dve.tensor_scalar(low, gate, 0.0, None, ALU.is_lt)))
                done.mark(dve.scalar_tensor_tensor(up, gate, 0.25, up, ALU.max, ALU.mult))
                wait(done.mark(dve.scalar_tensor_tensor(low, gate, -0.25, low, ALU.min, ALU.mult)))
                wait(done.mark(dve.tensor_tensor(gate, up, low, ALU.add)))

            def modulated(dst, tile, b, scale, shift):
                wait(done.mark(dve.tensor_scalar(dst, xs[:, tile, :], mean_var[:, tile, 0:1], rstd[:, bass.ds(tile, 1)], ALU.subtract, ALU.mult)))
                wait(done.mark(dve.tensor_tensor(dst, dst, mod[:, b, scale * D:(scale + 1) * D], ALU.mult)))
                return dve.tensor_tensor(dst, dst, mod[:, b, shift * D:(shift + 1) * D], ALU.add)

            PER = 3 * TI
            with dve.Fori(0, B) as b:
                saved = done.enter(b, PER)
                modulated(h[:, 0, :], b * TI, b, 1, 0).then_inc(h_ready, 1)
                for t in range(TI):
                    tile, p = b * TI + t, t % 2
                    pre = bank[4 * p + 2]
                    if t + 1 < TI:
                        modulated(h[:, 1 - p, :], tile + 1, b, 1, 0).then_inc(h_ready, 1)
                    dve.wait_ge(g_sq, tile + 1)
                    wait(done.mark(dve.tensor_scalar(gl[:, p, :], gl[:, p, :], 0.044715, 1.0, ALU.mult, ALU.add)))
                    dve.tensor_tensor(gl[:, p, :], pre[:, :], gl[:, p, :], ALU.mult).then_inc(g_arg, 1)
                    dve.wait_ge(g_tanh, tile + 1)
                    dve.scalar_tensor_tensor(gh[:, p, :, :].rearrange("p c t -> p (c t)"), gl[:, p, :], 1.0, pre[:, :], ALU.add, ALU.mult).then_inc(g_ready, 1)
                done.leave(saved, B, PER)

            dve.wait_ge(proj_copied, NT + C_E)
            w1 = W[:, :, :].rearrange("p t (c i n) -> p (t c) (i n)", c=C, i=4)[:, :, 0:2 * N]
            wait(done.mark(dve.tensor_tensor(sq.rearrange("p (a b) -> p a b", b=2 * N), w1, w1, ALU.mult)))
            wait(done.mark(dve.tensor_reduce(nw[:, 0, :], sq.rearrange("p (a b) -> p a b", b=N), AX.X, ALU.add)))
            dve.tensor_scalar(nw[:, 0, :], nw[:, 0, :], 1.0 / N, RMS_EPS, ALU.mult, ALU.add).then_inc(var_ready, 1)
            rsqrt(1, 64, rrms[:, :])
            w1 = W[:, :, :].rearrange("p t (c i n) -> p (t c) i n", c=C, i=4)[:, :, 0:2, :]
            done.mark(dve.tensor_tensor(w1, w1, bc(rrms[:, :].rearrange("p (a i) -> p a i", i=2), 3, N), ALU.mult))
            for o in (0, 2 * N):
                v = done.mark(dve.tensor_scalar(DD[:, :, o:o + N], DD[:, :, o:o + N], 1.0, None, ALU.add))
            wait(v)
            dve.wait_ge(pool_ready, 1)

            PER_G = HEADS * 2 + HEADS // 2 * 2
            PER_TAIL = TI * 3
            PER_B = TI * 3 + 1 + G * PER_G + PER_TAIL
            with dve.Fori(0, B) as b:
                saved_b = done.enter(b, PER_B)
                for t in range(TI):
                    tile = b * TI + t
                    w = weights_of(tile)
                    q3 = QK[:, tile, 0:D].rearrange("p (n h) -> p n h", n=N)
                    k3 = QK[:, tile, D:2 * D].rearrange("p (n h) -> p n h", n=N)
                    qc = stack[0].rearrange("p (n u h) -> p n u h", n=N, u=2)
                    kc = stack[2].rearrange("p (n u h) -> p n u h", n=N, u=2)
                    if t > 0:
                        dve.wait_ge(stack_mm, tile * 5)
                    dve.tensor_copy(stack[4], QK[:, tile, :])
                    dve.tensor_tensor(qc[:, :, 0, :], q3, bc(DD[:, tile, 0:N], 2, HD), ALU.mult)
                    dve.tensor_copy(qc[:, :, 1, :], q3).then_inc(stack_ready, 1)
                    for r in range(R):
                        ins = dve.tensor_tensor(stack[1][:, r * D:(r + 1) * D].rearrange("p (n h) -> p n h", n=N), q3, bc(w[:, 0, r, :], 2, HD), ALU.mult)
                    ins.then_inc(stack_ready, 1)
                    dve.tensor_copy(kc[:, :, 0, :], k3)
                    dve.tensor_tensor(kc[:, :, 1, :], k3, bc(DD[:, tile, N:2 * N], 2, HD), ALU.mult).then_inc(stack_ready, 1)
                    for r in range(R):
                        ins = dve.tensor_tensor(stack[3][:, r * D:(r + 1) * D].rearrange("p (n h) -> p n h", n=N), k3, bc(w[:, 1, r, :], 2, HD), ALU.mult)
                    ins.then_inc(stack_ready, 1)
                    for r in range(R):
                        ins = dve.tensor_tensor(bt[:, r * D:(r + 1) * D].rearrange("p (m n) -> p m n", m=N),
                                                bc(w[:, 3, r, :], 2, N), bc(w[:, 3, 2 + r, :], 1, N), ALU.mult)
                    wait(done.mark(ins))
                    flat = Bp[:, t, :, :].rearrange("p m n -> p (m n)")
                    wait(done.mark(dve.tensor_tensor(flat, bt[:, 0:D], bt[:, D:2 * D], ALU.add)))
                    dve.tensor_copy(Vb[:, t, :], V[:, tile, :])
                    wait(done.mark(dve.tensor_tensor(flat[:, 0:N * N:N + 1], flat[:, 0:N * N:N + 1], DD[:, tile, 3 * N:4 * N], ALU.add)))
                    for i, dst in ((1, QW), (3, KW)):
                        dve.wait_ge(stack_mm, tile * 5 + i + 1)
                        dve.tensor_copy(dst[:, :, P * t:P * (t + 1)], bank[i][:, :].rearrange("p (a t) -> p a t", t=P)).then_inc(stack_dve, 1)
                for s in range(TI):
                    for r in range(R):
                        n = 4 * s + 2 * r + 1
                        dve.wait_ge(hh_mm, b * 16 + (n + 1))
                        dve.tensor_copy(HK[:, r, TRK[s]:TRK[s + 1]], bank[n % 8][:, 0:P * (TI - s)]).then_inc(hk_copied, 1)
                for r in range(R):
                    dve.memset(Hp[:, r, :], 0.0)
                wait(done.mark(dve.memset(O[:, :, :], 0.0)))
                dve.wait_ge(hq_copied, (b + 1) * 8)
                dve.sem_inc(dve_step, 1)

                def step(g, k, last):
                    base = (b * G + g) * HEADS

                    def query_term(k):
                        t, p, j = at(k)
                        yk = Y[:, k % 2, 0:P * (t + 1)]
                        if k % 8 == 0:
                            dve.wait_ge(pair_ready, (b * G + g) * 2 + (k // 8 + 1 + C_ONE))
                        dve.wait_ge(prod_ready, base + (k + 1))
                        return done.mark(dve.scalar_tensor_tensor(yk, HQ[:, 1, TRI[t]:TRI[t + 1]], Wq2[:, t, 1, 2 * p + j:2 * p + j + 1], yk, ALU.mult, ALU.add))

                    def logits(k, term):
                        t, p, j = at(k)
                        dve.wait_ge(logit_mm, base + (k + 1))
                        dve.wait_ge(pt_mm, base + (k - 3 + C_PT))
                        wait(term)
                        dve.sem_inc(dve_step, 1)
                        dve.tensor_tensor_reduce(out=X[:, k % 4, 0:P * (t + 1)], in0=bank[k % 4][:, 0:P * (t + 1)], in1=Y[:, k % 2, 0:P * (t + 1)],
                                                 scale=1.0, scalar=3e38, op0=ALU.add, op1=ALU.min,
                                                 accum_out=rowmin[:, k % 4:k % 4 + 1]).then_inc(logit_read, 1)

                    def probabilities(k):
                        t, p, j = at(k)
                        xk = X[:, k % 4, 0:P * (t + 1)]
                        dve.wait_ge(exp_done, base + (k + 1 + C_EXP))
                        wait(done.mark(dve.reciprocal(rsum[:, k % 4:k % 4 + 1], rowsum[:, k % 4:k % 4 + 1])))
                        dve.tensor_scalar(xk, xk, rsum[:, k % 4:k % 4 + 1], None, ALU.mult).then_inc(prob_ready, 1)
                        dve.wait_ge(prob_ready, base + (k + 1))
                        dve.wait_ge(hp_added, base + (k + C_HP))
                        for r in range(R):
                            hp = Hp[:, r, TRI[t]:TRI[t + 1]]
                            ins = dve.scalar_tensor_tensor(hp, xk, Wp1[:, t, r, 2 * p + j:2 * p + j + 1], hp, ALU.mult, ALU.add)
                        ins.then_inc(hp_added, 1)

                    def outputs(u):
                        t, p = u % TI, u // TI
                        tile, n0 = b * TI + t, g * 4 + 2 * p
                        bk = bank[6 + u % 2]
                        dve.wait_ge(pv_mm, base + (2 * u + 2 + C_PV))
                        v = done.mark(dve.tensor_tensor(O[:, t, :], bk[:, 0:D], O[:, t, :], ALU.add))
                        dve.tensor_tensor(ou[:, u % 2, 0:2 * HD].rearrange("p (n h) -> p n h", n=2),
                                          bk[:, D:D + 2 * HD].rearrange("p (n h) -> p n h", n=2),
                                          bc(DD[:, tile, bass.ds(n0 + 2 * N, 2)], 2, HD), ALU.mult).then_inc(o_read, 1)
                        wait(v)
                        dve.wait_ge(o_read, (b * G + g) * 8 + (u + 1 + C_O))
                        on = O[:, t, bass.ds(n0 * HD, 2 * HD)]
                        done.mark(dve.tensor_tensor(on, on, ou[:, u % 2, 0:2 * HD], ALU.add))

                    if k < HEADS or not last:
                        term = query_term(k)
                    if k >= 1 and (k - 1 < HEADS or not last):
                        probabilities(k - 1)
                    if k < HEADS or not last:
                        logits(k, term)
                    if k >= 6 and k % 2 == 0:
                        outputs(k // 2 - 3)

                def fori(lo, hi):
                    return counted(done, dve.Fori(lo, hi), hi - lo, PER_G)

                run_groups(fori, step, 6)

                wait(done.now())
                for t in range(TI):
                    tile = b * TI + t
                    w = weights_of(tile)
                    dve.wait_ge(hv_mm, tile + 1)
                    for r in range(R):
                        ins = dve.tensor_tensor(ou[:, r, :].rearrange("p (n h) -> p n h", n=N),
                                                bank[2][:, r * D:(r + 1) * D].rearrange("p (n h) -> p n h", n=N),
                                                bc(w[:, 2, 2 + r, :], 2, HD), ALU.mult)
                    wait(done.mark(ins))
                    wait(done.mark(dve.tensor_tensor(O[:, t, :], O[:, t, :], ou[:, 0, :], ALU.add)))
                    dve.tensor_tensor(O[:, t, :], O[:, t, :], ou[:, 1, :], ALU.add).then_inc(o_ready, 1)
                    dve.wait_ge(ao_mm, tile + 1)
                    wait(done.mark(dve.tensor_tensor(ou[:, 0, :], bank[3][:, D:2 * D], mod[:, b, 2 * D:3 * D], ALU.mult)))
                    dve.tensor_tensor(xs[:, tile, :], xs[:, tile, :], ou[:, 0, :], ALU.add).then_inc(x1_ready, 1)
                done.leave(saved_b, B, PER_B)

            dve.wait_ge(x1_ready, NT)
            layernorm_stats()
            rsqrt(2, NT, rstd[:, :])
            for t in range(NT):
                modulated(rows[:, t, :], t, t // TI, 4, 3).then_inc(h2_ready, 1)
            dve.wait_ge(r_mm, 1)
            wait(done.mark(dve.tensor_copy(rl[:, :, :], bank[2][:, 0:NT * E].rearrange("p (t e) -> p t e", e=E))))
            wait(done.mark(dve.tensor_reduce(rbest[:, :], rl[:, :, :], AX.X, ALU.max)))
            dve.tensor_tensor(rone[:, :, :], rl[:, :, :], bc(rbest[:, :], 2, E), ALU.is_equal).then_inc(r_max, 1)
            dve.wait_ge(r_max, 1)
            wait(done.mark(dve.tensor_scalar(rl[:, :, :], bc(eio[:, :], 1, NT), -float(E), None, ALU.add)))
            wait(done.mark(dve.tensor_tensor(rone[:, :, :], rone[:, :, :], rl[:, :, :], ALU.mult)))
            wait(done.mark(dve.tensor_reduce(rstd[:, :], rone[:, :, :], AX.X, ALU.min)))
            dve.tensor_tensor(rone[:, :, :], rl[:, :, :], bc(rstd[:, :], 2, E), ALU.is_equal).then_inc(one_ready, 1)
            dve.wait_ge(one_ready, 1)
            dve.wait_ge(half_ready, 1)
            wait(done.mark(dve.tensor_scalar(rbest[:, :], rbest[:, :], 0.5, 0.5, ALU.mult, ALU.add)))
            for t in range(NT):
                dve.tensor_scalar(rows[:, t, :], rows[:, t, :], rbest[:, t:t + 1], None, ALU.mult).then_inc(rows_scaled, 1)

            dve.wait_ge(rank_mm, 1)
            cnt = bank[3][:, NT * E:(NT + 1) * E]
            need = ecmp[:, 0:NT * E].rearrange("p (e j) -> p e j", j=NT)
            wait(done.mark(dve.tensor_copy(rank[:, 0, :], cnt)))
            wait(done.mark(dve.tensor_tensor(need, bc(rank[:, 0, :], 2, NT), bc(start_of[:, :], 1, E), ALU.is_gt)))
            wait(done.mark(dve.tensor_reduce(tiles_of[:, 0, :], need, AX.X, ALU.add)))
            prior = ecmp[:, 0:E * E].rearrange("p (e f) -> p e f", f=E)
            wait(done.mark(dve.tensor_tensor(prior, bc(tiles_of[:, 0, :], 1, E), below[:, :, :], ALU.mult)))
            wait(done.mark(dve.tensor_reduce(tiles_of[:, 1, :], prior, AX.X, ALU.add)))
            v = done.mark(dve.tensor_tensor(tiles_of[:, 2, :], tiles_of[:, 0, :], tiles_of[:, 1, :], ALU.add))
            wait(done.mark(dve.scalar_tensor_tensor(rank[:, :, :], bc(tiles_of[:, 1, :], 1, NT), float(P),
                                                    bank[3][:, 0:NT * E].rearrange("p (t e) -> p t e", e=E), ALU.mult, ALU.add)))
            wait(done.mark(dve.tensor_tensor(rank[:, :, :], rank[:, :, :], rone[:, :, :], ALU.mult)))
            wait(done.mark(dve.tensor_reduce(row_f[:, :], rank[:, :, :], AX.X, ALU.add)))
            dve.tensor_copy(row_of[:, :], row_f[:, :]).then_inc(route_ready, 1)
            ended = ecmp[:, :].rearrange("p (s e) -> p s e", e=E)
            wait(done.mark(dve.tensor_tensor(ended, bc(tiles_of[:, 2, :], 1, NSLOT), bc(slot_no[:, :], 2, E), ALU.is_le)))
            wait(done.mark(dve.tensor_reduce(slot_e[:, :], ended, AX.X, ALU.add)))
            dve.tensor_scalar(slot_expert[:, :], slot_e[:, :], float(E - 1), None, ALU.min).then_inc(slot_known, 1)

            def step(i, j, last):
                def hidden(j):
                    p = j % 2
                    dve.wait_ge(th_ready, i * RING + (NT + j + 1))
                    wait(done.mark(dve.scalar_tensor_tensor(Y[:, p, 0:F], Y[:, p, 0:F], 1.0, bank[p][:, 0:F], ALU.add, ALU.mult)))
                    dve.wait_ge(hmT_mm, i * RING + (NT + j - 1 + C_E))
                    dve.scalar_tensor_tensor(X[:, p, 0:F], bank[p][:, F:2 * F], 0.5, Y[:, p, 0:F], ALU.mult, ALU.mult).then_inc(hm_ready, 1)

                def output(j):
                    y = bank[4 + j % 2][:, 0:D]
                    dve.wait_ge(dn_mm, i * RING + (NT + j + 1 + C_E))
                    if j < 0:
                        t = NT + j
                        dve.tensor_tensor(ou[:, t % 2, :], y, mod[:, t // TI, 5 * D:6 * D], ALU.mult).then_inc(dn_read, 1)
                        dve.wait_ge(dn_read, t + 1 + C_E)
                        v = done.mark(dve.tensor_tensor(xs[:, t, :], xs[:, t, :], ou[:, t % 2, :], ALU.add))
                        wait(v)
                    else:
                        r = j % RING
                        dve.wait_ge(d_y[r], (i + j // RING + 1) * 16)
                        dve.tensor_copy(slot_y[:, r, :], y).then_inc(dn_read, 1)
                        dve.wait_ge(dn_read, i * RING + (NT + j + 1 + C_E))
                        dve.sem_inc(y_ready, 1)

                if there(j - 1, last):
                    hidden(j - 1)
                if there(j - 3, last):
                    output(j - 3)

            def fori(lo, hi):
                return counted(done, dve.Fori(lo, hi), hi - lo, RING)

            run_experts(fori, step)
            for t in range(NT):
                dve.wait_ge(d_back[t], 16)
                if t >= 2:
                    dve.wait_ge(out_ready, t - 1)
                wait(done.mark(dve.tensor_tensor(ou[:, t % 2, :], back[:, t, :], mod[:, t // TI, 5 * D:6 * D], ALU.mult)))
                dve.tensor_tensor(xs[:, t, :], xs[:, t, :], ou[:, t % 2, :], ALU.add).then_inc(out_ready, 1)

        @block.tensor
        def _(pe):
            pe.sem_inc(pt_mm, C_PT)
            pe.sem_inc(pv_mm, C_PV)
            pe.sem_inc(hmT_mm, C_E)
            pe.sem_inc(dn_mm, C_E)
            pe.wait_ge(c_ready, 1)
            pe.wait_ge(d_wm, 16 * KT)
            for b in range(B):
                for j in range(3):
                    for k in range(KT):
                        mm = pe.matmul(bank[3 * b + j][:, :], c_rows[k * B + b], wmod_s[k][:, 512 * j:512 * j + 512], start=(k == 0), stop=(k == KT - 1))
                    mm.then_inc(mod_mm, 1)
            pe.wait_ge(pool_ready, 1)
            pe.wait_ge(d_w, 16 * 6)
            pe.wait_ge(mod_copied, 3 * B)

            with pe.Fori(0, B) as b:
                for t in range(TI):
                    tile, p = b * TI + t, t % 2
                    bk = bank[4 * p:4 * p + 4]
                    pe.wait_ge(h_ready, tile + 1)
                    pe.wait_ge(proj_copied, tile - 1 + C_E)
                    for k in range(KT):
                        mm = pe.transpose(bk[0][:, k * P:(k + 1) * P], h[:, p, k * P:(k + 1) * P], ident[:, :])
                    mm.then_inc(hT_mm, 1)
                    pe.wait_ge(hT_ready, tile + 1)
                    for c in range(C):
                        for k in range(KT):
                            mm = pe.matmul(bk[2][:, c * P:(c + 1) * P], dw1_s[:, k, c * P:(c + 1) * P], hT[:, p, k, :], start=(k == 0), stop=(k == KT - 1))
                    mm.then_inc(dwh_mm, 1)
                    for k in range(KT):
                        pe.matmul(bk[1][:, :], hT[:, p, k, :], wqkv_s[:, k, 0:2 * D], start=(k == 0), stop=(k == KT - 1))
                    for k in range(KT):
                        pe.matmul(bk[0][:, D:2 * D], hT[:, p, k, :], wqkv_s[:, k, 2 * D:3 * D], start=(k == 0), stop=(k == KT - 1))
                    for k in range(KT):
                        pe.matmul(bk[3][:, D:D + 64], hT[:, p, k, :], ddw_s[:, k, :], start=(k == 0), stop=(k == KT - 1))
                    pe.wait_ge(g_ready, tile + 1)
                    for c in range(C):
                        mm = pe.matmul(bk[3][:, c * M4:(c + 1) * M4], gh[:, p, c, :], qkw_s[:, c, :], start=True, stop=True)
                    mm.then_inc(proj_mm, 1)
            pe.wait_ge(proj_copied, NT + C_E)

            with pe.Fori(0, B) as b:
                for t in range(TI):
                    tile = b * TI + t
                    if t > 0:
                        pe.wait_ge(stack_act, 3 * tile)
                        pe.wait_ge(stack_dve, 2 * tile)
                    for i in range(4):
                        pe.wait_ge(stack_ready, 4 * tile + i + 1)
                        for a in range(4):
                            mm = pe.transpose(bank[i][:, a * P:(a + 1) * P], stack[i][:, a * P:(a + 1) * P], ident[:, :])
                        mm.then_inc(stack_mm, 1)
                    for a in range(4):
                        mm = pe.transpose(bank[4][:, a * P:(a + 1) * P], stack[4][:, a * P:(a + 1) * P], ident[:, :])
                    mm.then_inc(stack_mm, 1)
                pe.wait_ge(stack_act, (b + 1) * 3 * TI)
                pe.wait_ge(stack_dve, (b + 1) * 2 * TI)
                for t in range(TI):
                    for r in range(R):
                        for side in range(2):
                            n = 4 * t + 2 * r + side
                            bk = bank[n % 8]
                            if n == 8:
                                pe.wait_ge(hq_copied, b * 8 + 4)
                                pe.wait_ge(hk_copied, b * 8 + 4)
                            for k in range(KT):
                                if side == 0:
                                    mm = pe.matmul(bk[:, 0:P * (t + 1)], QW[:, r * KT + k, P * t:P * (t + 1)], KTr[:, k, 0:P * (t + 1)], start=(k == 0), stop=(k == KT - 1))
                                else:
                                    mm = pe.matmul(bk[:, 0:P * (TI - t)], KW[:, r * KT + k, P * t:P * (t + 1)], QT[:, k, P * t:T], start=(k == 0), stop=(k == KT - 1))
                            mm.then_inc(hh_mm, 1)
                pe.wait_ge(hq_copied, (b + 1) * 8)
                pe.wait_ge(hk_copied, (b + 1) * 8)
                pe.sem_inc(pe_step, 1)

                def step(g, k, last):
                    base = (b * G + g) * HEADS

                    def logits(k):
                        t, p, j = at(k)
                        row = 32 * (2 * p + j)
                        bk = bank[k % 4]
                        if k % 8 == 0:
                            pe.wait_ge(pair_ready, (b * G + g) * 2 + (k // 8 + 1 + C_ONE))
                        pe.wait_ge(logit_read, base + (k - 3 + C_LOGIT))
                        pe.matmul(bk[:, 0:P * (t + 1)], QCg[row:row + 32, P * t:P * (t + 1)], KCg[row:row + 32, 0:P * (t + 1)],
                                  start=True, stop=False, tile_position=(row, 0))
                        for s in range(t + 1):
                            for r in range(R):
                                off = TRK[s] + P * (t - s)
                                pe.matmul(bk[:, s * P:(s + 1) * P], HK[:, r, off:off + P], DG[:, p, s, r, j, :], start=False, stop=False)
                        pe.matmul(bk[:, t * P:(t + 1) * P], ident_b[:, :], mask_b[:, :], start=False, stop=True).then_inc(logit_mm, 1)

                    def transposes(k):
                        t, p, j = at(k)
                        pe.wait_ge(prob_ready, base + (k + 1))
                        pe.wait_ge(pt_ready, base + (k - 1 + C_E))
                        for s in range(t + 1):
                            mm = pe.transpose(bank[4 + k % 2][:, s * P:(s + 1) * P], X[:, k % 4, s * P:(s + 1) * P], ident[:, :])
                        mm.then_inc(pt_mm, 1)

                    def values(k):
                        t, p, j = at(k)
                        u = k // 2
                        bk = bank[6 + u % 2]
                        if j == 0:
                            pe.wait_ge(o_read, (b * G + g) * 8 + (u - 1 + C_O))
                        pe.wait_ge(pt_ready, base + (k + 1 + C_E))
                        for s in range(t + 1):
                            pe.matmul(bk[:, 0:D], PT[:, k % 2, s * P:(s + 1) * P], VP[:, p, s, j, :],
                                      start=(j == 0 and s == 0), stop=(j == 1 and s == t), skip_group_check=True)
                        for s in range(t + 1):
                            mm = pe.matmul(bk[:, D + j * HD:D + (j + 1) * HD], PT[:, k % 2, s * P:(s + 1) * P], Vb[:, s, bass.ds((g * 4 + (2 * p + j)) * HD, HD)],
                                           start=False, stop=(s == t), skip_group_check=True)
                        mm.then_inc(pv_mm, 1)

                    if k < HEADS or not last:
                        logits(k)
                    if k >= 2 and (k - 2 < HEADS or not last):
                        transposes(k - 2)
                    if k >= 3:
                        values(k - 3)

                run_groups(pe.Fori, step, 3)

                pe.wait_ge(hp_added, (b + 1) * G * HEADS + C_HP)
                for t in range(TI):
                    tile = b * TI + t
                    if t > 0:
                        pe.wait_ge(x1_ready, tile)
                    for r in range(R):
                        for s in range(t + 1):
                            mm = pe.transpose(bank[r][:, s * P:(s + 1) * P], Hp[:, r, TRI[t] + s * P:TRI[t] + (s + 1) * P], ident[:, :])
                        mm.then_inc(hp_mm, 1)
                    pe.wait_ge(hp_ready, b * 8 + (2 * t + 2))
                    for r in range(R):
                        for s in range(t + 1):
                            mm = pe.matmul(bank[2][:, r * D:(r + 1) * D], X[:, r, s * P:(s + 1) * P], Vb[:, s, :], start=(s == 0), stop=(s == t))
                    mm.then_inc(hv_mm, 1)
                    pe.wait_ge(o_ready, tile + 1)
                    for k in range(KT):
                        mm = pe.transpose(bank[3][:, k * P:(k + 1) * P], O[:, t, k * P:(k + 1) * P], ident[:, :])
                    mm.then_inc(oT_mm, 1)
                    pe.wait_ge(oT_ready, tile + 1)
                    for k in range(KT):
                        mm = pe.matmul(bank[3][:, D:2 * D], hT[:, 0, k, :], woT_s[:, k, :], start=(k == 0), stop=(k == KT - 1))
                    mm.then_inc(ao_mm, 1)

            for t in range(NT):
                pe.wait_ge(h2_ready, t + 1)
                if t >= 2:
                    pe.wait_ge(h2_T, t - 1)
                for k in range(KT):
                    mm = pe.transpose(bank[t % 2][:, k * P:(k + 1) * P], rows[:, t, k * P:(k + 1) * P], ident[:, :])
                mm.then_inc(h2_mm, 1)
            pe.wait_ge(h2_T, NT)
            for t in range(NT):
                for k in range(KT):
                    mm = pe.matmul(bank[2][:, t * E:(t + 1) * E], x2T[:, k, P * t:P * (t + 1)], rw_s[:, k, :], start=(k == 0), stop=(k == KT - 1))
            mm.then_inc(r_mm, 1)
            pe.wait_ge(r_max, 1)

            def routing():
                flat = rone[:, :, :].rearrange("p t e -> p (t e)")
                pe.wait_ge(one_ready, 1)
                pe.matmul(bank[3][:, 0:NT * E], before[:, :], flat, start=True, stop=False, skip_group_check=True)
                for d in range(1, NT):
                    pe.matmul(bank[3][:, d * E:NT * E], ones[:, :], flat[:, 0:(NT - d) * E], start=False, stop=(d == NT - 1), skip_group_check=True)
                for t in range(NT):
                    mm = pe.matmul(bank[3][:, NT * E:(NT + 1) * E], ones[:, :], flat[:, t * E:(t + 1) * E], start=False, stop=(t == NT - 1), skip_group_check=True)
                mm.then_inc(rank_mm, 1)

            def step(i, j, last):
                def slot_transposes(j):
                    r = j % RING
                    if j == 0 and i == 0:
                        pe.wait_ge(slot_known, 1)
                        pe.wait_ge(d_gu, 16 * 3 * E)
                    pe.wait_ge(d_slot[r], (i + j // RING + 1) * 16)
                    pe.wait_ge(xT_ready, i * RING + (j - 1 + C_E))
                    for k in range(KT):
                        mm = pe.transpose(bank[6 + j % 2][:, k * P:(k + 1) * P], slot_x[:, r, k * P:(k + 1) * P], ident[:, :])
                    mm.then_inc(xT_mm, 1)

                def expert_of(j):
                    return pe.value_load(slot_expert[0:1, bass.ds(i * RING + j, 1)], min_val=0, max_val=E - 1)

                def gate_up(j):
                    if j == -NT:
                        pe.wait_ge(d_shared, 16 * 3)
                    if j < 0:
                        src, (w, _) = x2T[:, :, P * (NT + j):P * (NT + j + 1)], expert_weights(shared_s)
                    else:
                        pe.wait_ge(xT_ready, i * RING + (j + 1 + C_E))
                        src, (w, _) = slot_xT[:, j % 2, :, :], expert_weights(big, expert_of(j))
                    pe.wait_ge(hm_ready, i * RING + (NT + j - 1 + C_E))
                    for c in range(KT):
                        mm = pe.matmul(bank[j % 2][:, :], src[:, c, :], w[:, c, :], start=(c == 0), stop=(c == KT - 1))
                    mm.then_inc(gu_mm, 1)

                def hidden_transposes(j):
                    pe.wait_ge(hm_ready, i * RING + (NT + j + 1 + C_E))
                    pe.wait_ge(hmT_ready, i * RING + (NT + j - 1 + C_E))
                    if j == -NT + 1:
                        pe.wait_ge(route_ready, 1)
                    for c in range(KT):
                        mm = pe.transpose(bank[2 + j % 2][:, c * P:(c + 1) * P], X[:, j % 2, c * P:(c + 1) * P], ident[:, :])
                    mm.then_inc(hmT_mm, 1)

                def down(j):
                    _, w = expert_weights(shared_s) if j < 0 else expert_weights(big, expert_of(j))
                    pe.wait_ge(hmT_ready, i * RING + (NT + j + 1 + C_E))
                    pe.wait_ge(dn_read, i * RING + (NT + j - 1 + C_E))
                    for c in range(F // P):
                        mm = pe.matmul(bank[4 + j % 2][:, 0:D], hT[:, j % 2, c, :], w[:, c, :], start=(c == 0), stop=(c == KT - 1))
                    mm.then_inc(dn_mm, 1)

                if j >= 0 and there(j, last):
                    slot_transposes(j)
                if there(j - 1, last):
                    gate_up(j - 1)
                if j == -NT + 1:
                    routing()
                if there(j - 2, last):
                    hidden_transposes(j - 2)
                if there(j - 3, last):
                    down(j - 3)

            run_experts(pe.Fori, step)


def kernel(L0_attn_x, L0_attn_w_qkv, L0_attn_w_o, L0_attn_dw1, L0_attn_qkw, L0_attn_dd_w, L0_ffn_router_w,
           L0_ffn_gate_w, L0_ffn_up_w, L0_ffn_down_w, L0_ffn_shared_gate_w, L0_ffn_shared_up_w,
           L0_ffn_shared_down_w, L0_c, L0_wmod):
    import numpy as np
    import concourse.bacc as bacc
    from concourse import mybir as mb
    from concourse.bass_utils import run_bass_kernel_spmd

    x = np.asarray(L0_attn_x)
    b, t, d = x.shape
    laid_out = [
        ("x", x.reshape(b * t, d)),
        ("w_qkv", np.asarray(L0_attn_w_qkv)),
        ("w_oT", np.asarray(L0_attn_w_o).T),
        ("dw1", np.asarray(L0_attn_dw1).reshape(d, -1)),
        ("qkw", np.asarray(L0_attn_qkw).reshape(4, 128, -1)),
        ("dd_w", np.asarray(L0_attn_dd_w).reshape(d, -1)),
        ("router_w", np.asarray(L0_ffn_router_w)),
        ("gate_w", np.asarray(L0_ffn_gate_w)),
        ("up_w", np.asarray(L0_ffn_up_w)),
        ("down_w", np.asarray(L0_ffn_down_w)),
        ("shared_gate", np.asarray(L0_ffn_shared_gate_w)),
        ("shared_up", np.asarray(L0_ffn_shared_up_w)),
        ("shared_down", np.asarray(L0_ffn_shared_down_w)),
        ("cT", np.asarray(L0_c).T),
        ("wmod", np.asarray(L0_wmod)),
    ]
    nc = bacc.Bacc("TRN2", target_bir_lowering=False, num_devices=1)
    arrays, args = {}, []
    for name, a in laid_out:
        a = np.ascontiguousarray(a)
        arrays["in_" + name] = a
        args.append(nc.dram_tensor("in_" + name, a.shape, mb.dt.from_np(a.dtype), kind="ExternalInput").ap())
    slot_tiles = -(-(b * t + 8 * 127) // 512) * 4
    for name in ("slots_in", "slots_out"):
        args.append(nc.dram_tensor(name, (slot_tiles * 128, d), mb.dt.float32, kind="Internal").ap())
    out = nc.dram_tensor("out_x", (b * t, d), mb.dt.float32, kind="ExternalOutput").ap()
    adaln_layer(nc, *args, out)
    r = run_bass_kernel_spmd(nc, [arrays], core_ids=[0])
    return r.results[0]["out_x"].reshape(b, t, d)
```

```python
import concourse.bass as bass
from concourse import mybir
from contextlib import ExitStack, contextmanager

P = 128
F32 = mybir.dt.float32
BF16 = mybir.dt.bfloat16
ALU = mybir.AluOpType
ACT = mybir.ActivationFunctionType
AX = mybir.AxisListType
MASKED = 1e30


class Done:

    def __init__(self, sem):
        self.sem, self.base, self.n = sem, 0, 0

    def mark(self, ins, by=1):
        ins.then_inc(self.sem, by)
        self.n += by
        return self.base + self.n

    def now(self):
        return self.base + self.n

    def enter(self, var, per):
        saved = (self.base, self.n)
        self.base, self.n = self.base + self.n + var * per, 0
        return saved

    def leave(self, saved, times, per):
        assert self.n == per, (self.n, per)
        self.base, self.n = saved[0], saved[1] + times * per


def adaln_layer(nc, x, w_qkv, w_oT, dw1, qkw, dd_w, router_w, gate_w, up_w, down_w,
                shared_gate, shared_up, shared_down, cT, wmod, slots_in, slots_out, out):
    BT, D = x.shape
    B = cT.shape[1]
    T = BT // B
    NT = BT // P
    TI = T // P
    KT = D // P
    C, _, M4 = qkw.shape
    N = M4 // 4
    HD = D // N
    R = 2
    G = N // 4
    E = router_w.shape[1]
    F = gate_w.shape[2]
    NSLOT = slots_in.shape[0] // P
    EW = KT * 2 * F + (F // P) * D
    QSCALE = -float(HD) ** -0.5
    LN_EPS, RMS_EPS = 1e-5, 1e-6
    TRI = [P * (t * (t + 1) // 2) for t in range(TI + 1)]
    TRK = [P * (TI * s - s * (s - 1) // 2) for s in range(TI + 1)]
    assert D == 256 and N == 16 and C == 4 and TI == 4 and F == D and E == 8
    assert NSLOT * P >= BT + E * (P - 1) and NSLOT % 4 == 0

    with ExitStack() as ctx:
        def sb(name, shape, dt=F32):
            return ctx.enter_context(nc.sbuf_tensor(name, shape, dt))

        def sem(name):
            return ctx.enter_context(nc.semaphore(name))

        bank = [ctx.enter_context(nc.psum_tensor(f"bank{i}", [P, 512], F32)) for i in range(8)]

        xs = sb("xs", [P, NT, D])
        mod = sb("mod", [P, B, 6 * D])
        ident = sb("ident", [P, P])
        ident_b = sb("ident_b", [P, P], BF16)
        mask_b = sb("mask_b", [P, P], BF16)
        ones = sb("ones", [P, P])
        stats = sb("stats", [P, NT, 6])
        mean_var = sb("mean_var", [P, NT, 2])
        nw = sb("nw", [P, 3, 64])
        rstd = sb("rstd", [P, NT])
        rrms = sb("rrms", [P, 64])
        early = sb("early", [P, KT * 3 * D + KT * C * P])
        wqkv_s = early[:, 0:KT * 3 * D].rearrange("p (k n) -> p k n", k=KT)
        dw1_s = early[:, KT * 3 * D:].rearrange("p (k n) -> p k n", k=KT)
        qkw_s = sb("qkw_s", [P, C, M4])
        ddw_s = sb("ddw_s", [P, KT, 64])
        woT_s = sb("woT_s", [P, KT, D])
        c_s = sb("c_s", [P, KT * B])
        c_e = sb("c_e", [P, 3, KT * B])
        W = sb("W", [P, NT, C * M4])
        DD = sb("DD", [P, NT, 64])
        big = sb("big", [P, E * EW])
        cut = [0]

        def part(*shape):
            n = shape[0] * shape[1]
            cut[0] += n
            return big[:, cut[0] - n:cut[0]].rearrange("p (a b) -> p a b", a=shape[0])

        V = part(NT, D)
        QK = part(NT, 2 * D)
        QT = part(KT, T)
        KTr = part(KT, T)
        QW = part(R * KT, T)
        KW = part(R * KT, T)
        assert cut[0] <= E * EW
        QC = sb("QC", [P, G, T])
        KC = sb("KC", [P, G, T])
        HQ = sb("HQ", [P, R, TRI[TI]])
        HK = sb("HK", [P, R, TRK[TI]])
        Hp = early[:, :].rearrange("p (r n) -> p r n", r=R)
        O = sb("O", [P, TI, D])
        VK = sb("VK", [P, TI, N, 2, HD])
        QCg = sb("QCg", [P, T])
        KCg = sb("KCg", [P, T])
        Wq2 = sb("Wq2", [P, TI, R, 4])
        Wk2 = sb("Wk2", [P, TI, R, 4])
        DG = sb("DG", [P, 2, TI, R, 2, P])
        late4 = sb("late4", [P, 4096])
        Hk = late4[:, 0:R * TRK[TI]].rearrange("p (r n) -> p r n", r=R)
        VW = DG[:, 0, :, :, :, :].rearrange("p s r j c -> p s r (j c)")
        X = sb("X", [P, 4, T])
        Xf = X[:, :, :].rearrange("p a n -> p (a n)")
        XH = [Xf[:, 0:TRI[TI]], late4[:, R * TRK[TI]:R * TRK[TI] + TRI[TI]]]
        Y = sb("Y", [P, 2, T])
        YT = [Y[:, 1, 2 * P:3 * P], Y[:, 1, 0:2 * P], Xf[:, TRI[TI]:TRI[TI] + 3 * P], Y[:, 0, :]]
        hT = sb("hT", [P, 2, KT, P])
        ZT = [Y[:, 1, 3 * P:4 * P], late4[:, R * TRK[TI] + TRI[TI]:], Xf[:, TRI[TI] + 3 * P:TRI[TI] + 6 * P],
              hT[:, :, :, :].rearrange("p a k t -> p (a k t)")]
        PT = sb("PT", [P, 2, T])
        rowmin = sb("rowmin", [P, 4])
        rowsum = sb("rowsum", [P, 4])
        rsum = sb("rsum", [P, 4])
        w1r = sb("w1r", [P, TI, R])
        ou = sb("ou", [P, 2, D])
        c_rows = [Y[:, i // 2, D + P * (i % 2):D + P * (i % 2) + P] for i in range(KT * B)]
        RD = sb("RD", [P, 2 * TI, P])
        h = Y[:, :, 0:D]
        late = DG[:, 1, :, :, :, :].rearrange("p a b c d -> p (a b c d)")
        gl = late[:, 0:1024].rearrange("p (a n) -> p a n", a=2)
        gh = late[:, 1024:2048].rearrange("p (a c t) -> p a c t", a=2, c=C)

        wmod_s = [QC[:, :, :].rearrange("p a b -> p (a b)")[:, 0:6 * D],
                  KC[:, :, :].rearrange("p a b -> p (a b)")[:, 0:6 * D]]
        stackv = late4
        stack = [stackv[:, 512 * i:512 * i + 512] for i in range(5)]
        sq = DG[:, 0, :, :, :, :].rearrange("p a b c d -> p (a b c d)")[:, 0:1024]
        shared_s = QC[:, :, :].rearrange("p a b -> p (a b)")[:, 0:EW]
        x2T = late.rearrange("p (k t) -> p k t", k=KT)
        rows = stackv[:, 0:NT * D].rearrange("p (t d) -> p t d", d=D)
        back = stackv[:, NT * D:2 * NT * D].rearrange("p (t d) -> p t d", d=D)
        zeros = stackv[:, 3 * 1024:3 * 1024 + D]
        RING = 4
        slot_x = sq.rearrange("p (r d) -> p r d", r=RING)
        slot_y = PT[:, :, :].rearrange("p a (b d) -> p (a b) d", d=D)
        slot_xT = O[:, 0:2, :].rearrange("p s (k t) -> p s k t", k=KT)
        rl = sb("rl", [P, NT, E])
        rbest = sb("rbest", [P, NT])
        rone = sb("rone", [P, NT, E])
        rone_b = sb("rone_b", [P, NT, E], BF16)
        ones_b = sb("ones_b", [P, P], BF16)
        rank = sb("rank", [P, NT, E])
        eio = sb("eio", [P, E])
        rw_s = sb("rw_s", [P, KT, E])
        before = sb("before", [P, P], BF16)
        start_of = sb("start_of", [P, NT])
        below = sb("below", [P, E, E])
        slot_no = sb("slot_no", [P, NSLOT])
        tiles_of = sb("tiles_of", [P, 3, E])
        ecmp = sb("ecmp", [P, NSLOT * E])
        slot_e = sb("slot_e", [P, NSLOT])
        slot_expert = sb("slot_expert", [P, NSLOT], mybir.dt.int32)
        row_f = sb("row_f", [P, NT])
        row_of = sb("row_of", [P, NT], mybir.dt.uint32)

        d_x, d_c, d_wm, d_w, d_out = (sem(n) for n in ("d_x", "d_c", "d_wm", "d_w", "d_out"))
        d_zero, d_gu, d_shared, d_scatter = sem("d_zero"), sem("d_gu"), sem("d_shared"), sem("d_scatter")
        d_slot = [sem(f"d_slot{i}") for i in range(RING)]
        d_y = [sem(f"d_y{i}") for i in range(RING)]
        d_back = [sem(f"d_back{i}") for i in range(NT)]
        dve_done, pool_done = sem("dve_done"), sem("pool_done")
        dve_step, pe_step, pool_step = sem("dve_step"), sem("pe_step"), sem("pool_step")
        pool_ready, ones_ready = sem("pool_ready"), sem("ones_ready")
        c_exp, c_ready, mod_mm, mod_copied = (sem(n) for n in ("c_exp", "c_ready", "mod_mm", "mod_copied"))
        var_ready, root_ready = sem("var_ready"), sem("root_ready")
        h_ready, hT_mm, hT_ready = sem("h_ready"), sem("hT_mm"), sem("hT_ready")
        dwh_mm, g_sq, g_arg, g_tanh, g_ready = (sem(n) for n in ("dwh_mm", "g_sq", "g_arg", "g_tanh", "g_ready"))
        qkv_mm, proj_mm, proj_copied, qkv_copied = sem("qkv_mm"), sem("proj_mm"), sem("proj_copied"), sem("qkv_copied")
        stack_ready, stack_mm, stack_act, stack_dve = (sem(n) for n in ("stack_ready", "stack_mm", "stack_act", "stack_dve"))
        hq_mm, hk_mm, hq_copied, hk_copied = sem("hq_mm"), sem("hk_mm"), sem("hq_copied"), sem("hk_copied")
        k_ready, vk_ready = sem("k_ready"), sem("vk_ready")
        rows_ready, w2_ready, pair_ready, vw_ready = sem("rows_ready"), sem("w2_ready"), sem("pair_ready"), sem("vw_ready")
        own_read, sums_clear, term_ready, rsum_ready, w1r_ready, rd_ready, hk_added = (
            sem(n) for n in ("own_read", "sums_clear", "term_ready", "rsum_ready", "w1r_ready", "rd_ready", "hk_added"))
        logit_mm, logit_read, prod_ready = sem("logit_mm"), sem("logit_read"), sem("prod_ready")
        exp_done, hp_added = sem("exp_done"), sem("hp_added")
        pt_mm, pt_ready, pv_mm = sem("pt_mm"), sem("pt_ready"), sem("pv_mm")
        hp_mm, hp_ready, hv_mm = sem("hp_mm"), sem("hp_ready"), sem("hv_mm")
        o_ready, oT_mm, oT_ready, ao_mm, x1_ready = (sem(n) for n in ("o_ready", "oT_mm", "oT_ready", "ao_mm", "x1_ready"))
        n2_ready, m2_ready = sem("n2_ready"), sem("m2_ready")
        h2_ready, h2_mm, h2_T, r_mm, r_max = (sem(n) for n in ("h2_ready", "h2_mm", "h2_T", "r_mm", "r_max"))
        half_ready, one_ready, rank_mm, rows_scaled, route_ready, slot_known = (
            sem(n) for n in ("half_ready", "one_ready", "rank_mm", "rows_scaled", "route_ready", "slot_known"))
        xT_mm, xT_ready, y_ready, zeros_ready = sem("xT_mm"), sem("xT_ready"), sem("y_ready"), sem("zeros_ready")
        gu_mm, th_ready, hm_ready, hmT_mm, hmT_ready, dn_mm, dn_read, out_ready = (
            sem(n) for n in ("gu_mm", "th_ready", "hm_ready", "hmT_mm", "hmT_ready", "dn_mm", "dn_read", "out_ready"))
        C_LOGIT, C_PT, C_HP, C_ONE, C_E, C_X1 = 16, 8, 8, 1, 2, 1

        STEPS = 4 * TI
        T_LAG, C_LAG, V_LAG = 6, 7, 8
        STACKS = (0, 2, 1, 4, 3)
        HK_BANKS = (7, 0, 1, 2, 3, 4, 7, 0)
        P_LAG = 2

        def at(k):
            return k % TI, k // TI % 4

        @contextmanager
        def counted(done, loop, times, per):
            with loop as var:
                saved = done.enter(var, per)
                yield var
                done.leave(saved, times, per)

        def run_groups(fori, step, lag):
            for k in range(lag):
                step(0, k, False)
            with fori(0, G - 1) as g:
                for k in range(lag, STEPS + lag):
                    step(g, k, False)
            for k in range(lag, STEPS + lag):
                step(G - 1, k, True)

        def run_tiles(fori, step, lag):
            for t in range(lag):
                step(0, t, False)
            with fori(0, B - 1) as b:
                for t in range(lag, TI + lag):
                    step(b, t, False)
            for t in range(lag, TI + lag):
                step(B - 1, t, True)

        def bc(ap, axis, n):
            a = ap.unsqueeze(axis)
            shape = list(a.shape)
            shape[axis] = n
            return a.broadcast_to(shape)

        def weight(b, t, c, r, head):
            flat = W[:, :, :].rearrange("p t w -> p (t w)")
            return flat[:, bass.ds(b * (TI * C * M4) + head + (t * C * M4 + c * M4 + r * N), 1)]

        def weights_of(tile):
            return W[:, bass.ds(tile, 1), :].rearrange("p a (c i n) -> p (a c) i n", c=C, i=4)

        def expert_weights(base, e=None):
            if e is None:
                w = base
            else:
                w = base[:, bass.ds(e * EW, EW)]
            return (w[:, 0:2 * KT * F].rearrange("p (k n) -> p k n", k=KT),
                    w[:, 2 * KT * F:EW].rearrange("p (k n) -> p k n", k=F // P))

        LAG = 3

        def run_experts(fori, step):
            for j in range(-NT, LAG):
                step(0, j, False)
            with fori(0, NSLOT // RING - 1) as i:
                for j in range(LAG, RING + LAG):
                    step(i, j, False)
            for j in range(LAG, RING + LAG):
                step(NSLOT // RING - 1, j, True)

        def there(j, last):
            return j >= -NT and (j < RING or not last)

        block = ctx.enter_context(nc.Block())

        @block.sync
        def _(sp):
            sp.dma_start(c_s[:, :].rearrange("p (k b) -> p k b", k=KT),
                         cT.rearrange("(k p) b -> p k b", p=P)).then_inc(d_c, 16)
            for k in range(KT):
                sp.dma_start(wmod_s[k][:, 0:2 * D], wmod[P * k:P * (k + 1), 0:2 * D]).then_inc(d_wm, 16)
            sp.dma_start(xs[:, :, :], x.rearrange("(a p) d -> p a d", p=P)).then_inc(d_x, 16)
            sp.dma_start(wqkv_s[:, :, :], w_qkv.rearrange("(k p) n -> p k n", p=P)).then_inc(d_w, 16)
            sp.dma_start(dw1_s[:, :, :], dw1.rearrange("(k p) n -> p k n", p=P)).then_inc(d_w, 16)
            sp.dma_start(qkw_s[:, :, :], qkw.rearrange("c k m -> k c m")).then_inc(d_w, 16)
            sp.dma_start(ddw_s[:, :, :], dd_w.rearrange("(k p) n -> p k n", p=P)).then_inc(d_w, 16)
            for k in range(KT):
                sp.dma_start(wmod_s[k][:, 2 * D:], wmod[P * k:P * (k + 1), 2 * D:]).then_inc(d_w, 16)
            sp.dma_start(woT_s[:, :, :], w_oT.rearrange("(k p) n -> p k n", p=P)).then_inc(d_w, 16)
            sp.dma_start(rw_s[:, :, :], router_w.rearrange("(k p) n -> p k n", p=P)).then_inc(d_w, 16)

            sp.wait_ge(zeros_ready, 1)
            sp.dma_start(slots_in.rearrange("(a p) d -> p a d", p=P), bc(zeros, 1, NSLOT)).then_inc(d_zero, 16)

            def load_expert(base, gate, up, down, landed):
                g, d = expert_weights(base)
                sp.dma_start(g[:, :, 0:F], gate.rearrange("(k p) n -> p k n", p=P)).then_inc(landed, 16)
                sp.dma_start(g[:, :, F:2 * F], up.rearrange("(k p) n -> p k n", p=P)).then_inc(landed, 16)
                sp.dma_start(d, down.rearrange("(k p) n -> p k n", p=P)).then_inc(landed, 16)

            sp.wait_ge(hk_mm, B * 8)
            sp.wait_ge(hk_copied, B * 8)
            sp.wait_ge(vk_ready, NT)
            for e in range(E):
                load_expert(big[:, e * EW:(e + 1) * EW], gate_w[e], up_w[e], down_w[e], d_gu)
            sp.wait_ge(pair_ready, B * G * 2 * TI + C_ONE)
            load_expert(shared_s, shared_gate, shared_up, shared_down, d_shared)
            for r in range(RING):
                sp.sem_inc(d_y[r], 16)
            with sp.Fori(0, NSLOT // RING) as i:
                for r in range(RING):
                    sp.wait_ge(y_ready, i * RING + (r + 1))
                    sp.dma_start(slots_out[bass.ds(i * (RING * P) + r * P, P), :], slot_y[:, r, :]).then_inc(d_y[r], 16)
            for t in range(NT):
                sp.wait_ge(out_ready, t + 1)
                sp.dma_start(out[P * t:P * (t + 1), :], xs[:, t, :]).then_inc(d_out, 16)
            sp.wait_ge(d_out, 16 * NT)

        @block.gpsimd
        def _(pool):
            pool.memset(ident[:, :], 0.0)
            pool.memset(mask_b[:, :], 0.0)
            pool.memset(ident_b[:, :], 0.0).then_inc(pool_done, 1)
            pool.wait_ge(pool_done, 1)
            for m in (ident, ident_b):
                pool.affine_select(out=m[:, :], in_=m[:, :], compare_op=ALU.not_equal, fill=1.0,
                                   base=0, pattern=[[-1, P]], channel_multiplier=1)
            pool.affine_select(out=mask_b[:, :], in_=mask_b[:, :], compare_op=ALU.is_ge, fill=MASKED,
                               base=0, pattern=[[-1, P]], channel_multiplier=1)
            pool.memset(zeros, 0.0).then_inc(zeros_ready, 1)
            pool.memset(before[:, :], 1.0)
            pool.memset(ones_b[:, :], 1.0)
            pool.memset(below[:, :, :], 1.0).then_inc(pool_done, 1)
            pool.wait_ge(pool_done, 2)
            pool.affine_select(out=before[:, :], in_=before[:, :], compare_op=ALU.is_ge, fill=0.0,
                               base=-1, pattern=[[1, P]], channel_multiplier=-1)
            pool.affine_select(out=below[:, :, :], in_=below[:, :, :], compare_op=ALU.is_ge, fill=0.0,
                               base=-1, pattern=[[1, E], [-1, E]], channel_multiplier=0)
            pool.iota(start_of[:, :], pattern=[[P, NT]], base=0, channel_multiplier=0,
                      allow_small_or_imprecise_dtypes=True)
            pool.iota(slot_no[:, :], pattern=[[1, NSLOT]], base=0, channel_multiplier=0,
                      allow_small_or_imprecise_dtypes=True)
            pool.iota(eio[:, :], pattern=[[1, E]], base=0, channel_multiplier=0,
                      allow_small_or_imprecise_dtypes=True).then_inc(pool_ready, 1)
            pool.wait_ge(pool_ready, 1)
            pool.sem_inc(pair_ready, C_ONE)
            pool.sem_inc(vw_ready, C_ONE)

            pool.wait_ge(d_zero, 16)
            pool.wait_ge(proj_copied, NT + C_E)
            with pool.Fori(0, B) as b:
                pool.wait_ge(x1_ready, b * TI + C_X1)
                for t in range(TI):
                    tile = b * TI + t
                    k3 = QK[:, tile, D:2 * D].rearrange("p (n h) -> p n h", n=N)
                    kc = stack[2].rearrange("p (n u h) -> p n u h", n=N, u=2)
                    if t > 0:
                        pool.wait_ge(stack_mm, tile * 5 - 4 + STACKS.index(2))
                    pool.sem_inc(pool_step, 1)
                    pool.tensor_copy(kc[:, :, 0, :], k3)
                    pool.tensor_tensor(kc[:, :, 1, :], k3, bc(DD[:, tile, N:2 * N], 2, HD), ALU.mult).then_inc(k_ready, 1)
                    if t > 0:
                        pool.wait_ge(stack_mm, tile * 5 - 4 + STACKS.index(4))
                    pool.sem_inc(pool_step, 1)
                    pool.tensor_copy(stack[4], QK[:, tile, :]).then_inc(k_ready, 1)
                pool.wait_ge(stack_act, (b + 1) * 4 * TI)
                pool.wait_ge(stack_dve, (b + 1) * TI)

                def copy_rows(g, p, s, after=None):
                    n = (b * G + g) * 2 + p
                    if after is None:
                        pool.wait_ge(pair_ready, n * TI + (s + C_ONE))
                    else:
                        pool.wait_ge(term_ready, after)
                    if s == 0:
                        pool.wait_ge(logit_read, (b * G + g) * STEPS + (8 * p + 8 - STEPS + C_LOGIT))
                    pool.sem_inc(pool_step, 1)
                    cols = slice(P * s, P * (s + 1))
                    for dst, src in ((QCg, QC), (KCg, KC)):
                        ins = pool.tensor_copy(dst[64 * p:64 * p + 64, cols], src[64 * p:64 * p + 64, bass.ds(g, 1), cols].rearrange("q a t -> q (a t)"))
                    ins.then_inc(rows_ready, 1)
                    pool.wait_ge(rows_ready, n * TI + (s + 1))
                    if s == 0:
                        pool.sem_inc(pool_step, 1)
                        for dst, c in ((Wq2, 0), (Wk2, 1)):
                            src = W[:, bass.ds(b * TI, TI), bass.ds(g * 4 + (c * M4 + 2 * N + 2 * p), N + 2)]
                            for r in range(R):
                                ins = pool.tensor_copy(dst[:, :, r, 2 * p:2 * p + 2], src[:, :, r * N:r * N + 2])
                        ins.then_inc(w2_ready, 1)

                def diagonals(g, p, s):
                    pool.wait_ge(w2_ready, (b * G + g) * 2 + (p + 1))
                    pool.tensor_tensor(DG[:, p, s, :, :, :], bc(bc(ident[:, :], 1, 2), 1, R),
                                       bc(Wk2[:, s, :, 2 * p:2 * p + 2], 3, P), ALU.mult).then_inc(pair_ready, 1)

                pool.wait_ge(k_ready, (b + 1) * 2 * TI)
                for s in range(TI):
                    copy_rows(0, 0, s)
                    diagonals(0, 0, s)
                def step(g, k, last):
                    def term(k):
                        t, m = at(k)
                        y = YT[t][:, 0:P * (t + 1)]
                        pool.wait_ge(prod_ready, (b * G + g) * STEPS + (k + 1))
                        pool.sem_inc(pool_step, 1)
                        pool.tensor_tensor(y, y, ZT[t][:, 0:P * (t + 1)], ALU.add).then_inc(term_ready, 1)

                    def prepare(k):
                        gk, p = (g, 1) if k % STEPS < 8 else (g + 1, 0)
                        if p == 1 or not last:
                            if k % 2 == 0:
                                copy_rows(gk, p, k % 8 // 2, (b * G + g) * STEPS + (k + P_LAG + 1))
                            else:
                                diagonals(gk, p, k % 8 // 2)

                    if k < STEPS or not last:
                        term(k)
                    if k >= P_LAG and (k - P_LAG < STEPS or not last):
                        prepare(k - P_LAG)

                run_groups(pool.Fori, step, P_LAG)
                pool.wait_ge(vk_ready, (b + 1) * TI)
                pool.wait_ge(logit_read, (b + 1) * G * STEPS - 8 + C_LOGIT)
                for s in range(TI):
                    for r in range(R):
                        ins = pool.tensor_tensor(VW[:, s, r, :].rearrange("p (n h) -> p n h", n=N), VK[:, s, :, 0, :],
                                                 bc(weights_of(b * TI + s)[:, 3, 2 + r, :], 2, HD), ALU.mult)
                ins.then_inc(vw_ready, 1)

            for t in range(NT):
                pool.wait_ge(m2_ready, t + 1)
                pool.tensor_tensor(rows[:, t, :], rows[:, t, :], mod[:, t // TI, 3 * D:4 * D], ALU.add).then_inc(h2_ready, 1)

            pool.wait_ge(route_ready, 1)
            for t in range(NT):
                pool.wait_ge(rows_scaled, t + 1)
                pool.indirect_dma_start(out=slots_in[:, :], out_offset=bass.IndirectOffsetOnAxis(ap=row_of[:, t:t + 1], axis=0),
                                        in_=rows[:, t, :], in_offset=None).then_inc(d_scatter, 16)
            pool.wait_ge(d_scatter, 16 * NT)
            for r in range(RING):
                pool.dma_start(slot_x[:, r, :], slots_in[P * r:P * (r + 1), :]).then_inc(d_slot[r], 16)
            with pool.Fori(0, NSLOT // RING - 1) as i:
                for r in range(RING):
                    pool.wait_ge(xT_mm, i * RING + (r + 1))
                    pool.dma_start(slot_x[:, r, :], slots_in[bass.ds(i * (RING * P) + (RING + r) * P, P), :]).then_inc(d_slot[r], 16)
            for r in range(RING):
                pool.wait_ge(d_y[r], 16 * (NSLOT // RING + 1))
            for t in range(NT):
                pool.indirect_dma_start(out=back[:, t, :], out_offset=None, in_=slots_out[:, :],
                                        in_offset=bass.IndirectOffsetOnAxis(ap=row_of[:, t:t + 1], axis=0)).then_inc(d_back[t], 16)

        @block.scalar
        def _(act):
            act.sem_inc(pt_ready, C_E)
            act.sem_inc(hmT_ready, C_E)
            act.sem_inc(xT_ready, C_E)
            act.sem_inc(proj_copied, C_E)
            act.sem_inc(qkv_copied, C_E)
            act.wait_ge(d_c, 16)
            act.activation(c_e[:, 0, :], c_s[:, :], ACT.Exp, scale=-1.0).then_inc(c_exp, 1)

            def root(i, n):
                act.wait_ge(var_ready, i + 1)
                act.activation(nw[:, 1, 0:n], nw[:, 0, 0:n], ACT.Sqrt).then_inc(root_ready, 1)

            def modulation(j, b):
                act.wait_ge(mod_mm, j * B + b + 1)
                act.activation(mod[:, b, 512 * j:512 * j + 512], bank[(j * B + b) % 4][:, :], ACT.Copy).then_inc(mod_copied, 1)

            modulation(0, 0)
            root(0, NT)
            modulation(0, 1)

            def step(b, t, last):
                def h_transposed(t):
                    act.wait_ge(hT_mm, b * TI + t + 1)
                    act.activation(hT[:, t % 2, :, :], bank[4 * (t % 2)][:, 0:D].rearrange("p (k t) -> p k t", k=KT), ACT.Copy).then_inc(hT_ready, 1)

                def square(t):
                    act.wait_ge(dwh_mm, b * TI + t + 1)
                    act.activation(gl[:, t % 2, :], bank[4 * (t % 2) + 2][:, :], ACT.Square).then_inc(g_sq, 1)

                def tanh(t):
                    act.wait_ge(g_arg, b * TI + t + 1)
                    act.activation(gl[:, t % 2, :], gl[:, t % 2, :], ACT.Tanh, scale=0.7978845608028654).then_inc(g_tanh, 1)

                def qkv(t):
                    tile, bk = b * TI + t, bank[4 * (t % 2):4 * (t % 2) + 4]
                    act.wait_ge(qkv_mm, tile + 1)
                    act.activation(QK[:, tile, 0:D], bk[1][:, 0:D], ACT.Copy, scale=QSCALE)
                    act.activation(QK[:, tile, D:2 * D], bk[1][:, D:2 * D], ACT.Copy)
                    act.activation(V[:, tile, :], bk[0][:, D:2 * D], ACT.Copy).then_inc(qkv_copied, 1)

                def compositions(t):
                    tile, bk = b * TI + t, bank[4 * (t % 2) + 3]
                    act.wait_ge(proj_mm, tile + 1)
                    act.activation(DD[:, tile, :], bk[:, D:D + 64], ACT.Tanh)
                    act.activation(W[:, tile, :], bk[:, 0:D], ACT.Copy, scale=0.5).then_inc(proj_copied, 1)

                before_it = 1 <= t and (t - 1 < TI or not last)
                if before_it:
                    square(t - 1)
                if t < TI or not last:
                    h_transposed(t)
                if before_it:
                    tanh(t - 1)
                if t >= 2:
                    compositions(t - 2)
                if before_it:
                    qkv(t - 1)

            run_tiles(act.Fori, step, 2)

            root(1, 64)
            for j in (1, 2):
                for b in range(B):
                    modulation(j, b)

            with act.Fori(0, B) as b:
                def stacks_transposed(t):
                    tile, cols = b * TI + t, slice(P * t, P * (t + 1))
                    for i in STACKS:
                        if i != 3:
                            act.wait_ge(stack_mm, tile * 5 + STACKS.index(i) + 1)
                            bk = bank[i][:, :].rearrange("p (a t) -> p a t", t=P)
                            if i == 4:
                                act.activation(QT[:, :, cols], bk[:, 0:2, :], ACT.Copy)
                                ins = act.activation(KTr[:, :, cols], bk[:, 2:4, :], ACT.Copy)
                            else:
                                ins = act.activation({0: QC, 1: QW, 2: KC}[i][:, :, cols], bk, ACT.Copy)
                            ins.then_inc(stack_act, 1)

                def hq(t):
                    for r in range(R):
                        act.wait_ge(hq_mm, b * 8 + (2 * t + r + 1))
                        act.activation(HQ[:, r, TRI[t]:TRI[t + 1]], bank[5 + r][:, 0:P * (t + 1)], ACT.Copy).then_inc(hq_copied, 1)

                for t in range(TI + 1):
                    if t < TI:
                        stacks_transposed(t)
                    if t >= 1:
                        hq(t - 1)
                act.wait_ge(hq_copied, (b + 1) * 8)

                def step(g, k, last):
                    base = (b * G + g) * STEPS

                    def product(k):
                        t, m = at(k)
                        if k % 8 == 0:
                            act.wait_ge(w2_ready, (b * G + g) * 2 + (k // 8 + 1))
                        act.wait_ge(logit_read, base + (k - 3 + C_LOGIT))
                        act.activation(YT[t][:, 0:P * (t + 1)], HQ[:, 0, TRI[t]:TRI[t + 1]], ACT.Copy, scale=Wq2[:, t, 0, m:m + 1])
                        act.activation(ZT[t][:, 0:P * (t + 1)], HQ[:, 1, TRI[t]:TRI[t + 1]], ACT.Copy,
                                       scale=Wq2[:, t, 1, m:m + 1]).then_inc(prod_ready, 1)

                    def exponential(k):
                        t, m = at(k)
                        x = XH[m % 2][:, TRI[t]:TRI[t + 1]]
                        act.wait_ge(logit_read, base + (k + 1 + C_LOGIT))
                        act.activation(x, x, ACT.Exp, bias=rowmin[:, t:t + 1], scale=-1.0,
                                       accum_out=rowsum[:, t:t + 1]).then_inc(exp_done, 1)

                    def diagonal(k):
                        t, m = at(k)
                        act.wait_ge(rsum_ready, base + (k + 1))
                        act.activation(RD[:, m % 2 * TI + t, :], ident[:, :], ACT.Copy, scale=rsum[:, t:t + 1]).then_inc(rd_ready, 1)

                    def weights(k):
                        t, m = at(k)
                        head = g * 4 + (m + k // STEPS * 4)
                        w = W[:, :, :].rearrange("p t w -> p (t w)")[:, bass.ds(b * (TI * C * M4) + head + (t * C * M4 + 2 * M4), 2 * N)]
                        act.wait_ge(hp_added, base + (k - 3 + C_HP))
                        act.activation(w1r[:, t, :], w[:, 0:N + 1:N], ACT.Copy, scale=rsum[:, t:t + 1]).then_inc(w1r_ready, 1)

                    def transposed(k):
                        s, m = at(k)
                        act.wait_ge(pt_mm, base + (k + 1 + C_PT))
                        act.wait_ge(pv_mm, base + (k - 1 + C_E))
                        act.wait_ge(hk_added, base + (k - 1 + C_HP))
                        act.activation(PT[:, k % 2, 0:P * (TI - s)], bank[4 + k % 2][:, 0:P * (TI - s)], ACT.Copy).then_inc(pt_ready, 1)

                    if k == 0:
                        product(0)
                        product(1)
                    if k >= 1 and (k - 1 < STEPS or not last):
                        diagonal(k - 1)
                        weights(k - 1)
                    if k >= C_LAG:
                        transposed(k - C_LAG)
                    if k + 2 < STEPS or not last:
                        product(k + 2)
                    if k < STEPS or not last:
                        exponential(k)

                run_groups(act.Fori, step, C_LAG)

                for i in range(TI + 2):
                    if i >= 2:
                        t = i - 2
                        act.wait_ge(oT_mm, b * TI + t + 1)
                        act.activation(hT[:, t % 2, :, :], bank[6 + t % 2][:, D:2 * D].rearrange("p (k t) -> p k t", k=KT), ACT.Copy).then_inc(oT_ready, 1)
                    if i < TI:
                        if i >= 2:
                            act.wait_ge(hv_mm, b * TI + i - 1)
                        for r in range(R):
                            act.wait_ge(hp_mm, b * 8 + (2 * i + r + 1))
                            act.activation(X[:, i % 2 * 2 + r, 0:P * (i + 1)], bank[i % 2 * 2 + r][:, 0:P * (i + 1)], ACT.Copy).then_inc(hp_ready, 1)

            root(2, NT)
            for t in range(NT):
                act.wait_ge(h2_mm, t + 1)
                act.activation(x2T[:, :, P * t:P * (t + 1)], bank[t % 2][:, 0:D].rearrange("p (k t) -> p k t", k=KT), ACT.Copy).then_inc(h2_T, 1)
            act.wait_ge(r_max, 1)
            act.activation(rbest[:, :], rbest[:, :], ACT.Tanh, scale=0.5).then_inc(half_ready, 1)

            def step(i, j, last):
                def slot_transposed(j):
                    act.wait_ge(xT_mm, i * RING + (j + 1))
                    act.wait_ge(gu_mm, i * RING + (NT + j - 1))
                    act.activation(slot_xT[:, j % 2, :, :], bank[6 + j % 2][:, 0:D].rearrange("p (k t) -> p k t", k=KT), ACT.Copy).then_inc(xT_ready, 1)

                def tanh(j):
                    act.wait_ge(gu_mm, i * RING + (NT + j + 1))
                    act.wait_ge(hm_ready, i * RING + (NT + j - 1 + C_E))
                    act.activation(Y[:, j % 2, 0:F], bank[j % 2][:, 0:F], ACT.Tanh, scale=0.5).then_inc(th_ready, 1)

                def hidden_transposed(j):
                    act.wait_ge(hmT_mm, i * RING + (NT + j + 1 + C_E))
                    act.wait_ge(dn_mm, i * RING + (NT + j - 1 + C_E))
                    act.activation(hT[:, j % 2, :, :], bank[2 + j % 2][:, 0:F].rearrange("p (k t) -> p k t", k=KT), ACT.Copy).then_inc(hmT_ready, 1)

                if j >= 0 and there(j, last):
                    slot_transposed(j)
                if there(j - 2, last):
                    hidden_transposed(j - 2)
                if there(j - 1, last):
                    tanh(j - 1)

            run_experts(act.Fori, step)

        @block.vector
        def _(dve):
            done = Done(dve_done)

            def wait(v):
                dve.wait_ge(dve_done, v)

            dve.sem_inc(logit_read, C_LOGIT)
            dve.sem_inc(hp_added, C_HP)
            dve.sem_inc(hk_added, C_HP)
            dve.sem_inc(own_read, C_E)
            dve.sem_inc(x1_ready, C_X1)
            dve.sem_inc(hm_ready, C_E)
            dve.sem_inc(dn_read, C_E)
            dve.memset(ones[:, :], 1.0).then_inc(ones_ready, 1)
            dve.wait_ge(ones_ready, 1)
            dve.wait_ge(c_exp, 1)
            wait(done.mark(dve.tensor_scalar(c_e[:, 1, :], c_e[:, 0, :], 1.0, None, ALU.add)))
            wait(done.mark(dve.reciprocal(c_e[:, 2, :], c_e[:, 1, :])))
            wait(done.mark(dve.tensor_tensor(c_e[:, 0, :], c_e[:, 2, :], c_s[:, :], ALU.mult)))
            for i in range(KT * B):
                ins = dve.tensor_scalar(c_rows[i], ones[:, :], c_e[:, 0, i:i + 1], None, ALU.mult)
            ins.then_inc(c_ready, 1)

            def variances(v):
                wait(v)
                for t in range(NT):
                    v = done.mark(dve.bn_aggr(mean_var[:, t, :], stats[:, t, :]))
                wait(v)
                dve.tensor_scalar(nw[:, 0, 0:NT], mean_var[:, :, 1], LN_EPS, None, ALU.add).then_inc(var_ready, 1)

            def rsqrt(i, n, r):
                dve.wait_ge(root_ready, i + 1)
                wait(done.mark(dve.reciprocal(r, nw[:, 1, 0:n])))
                wait(done.mark(dve.tensor_tensor(nw[:, 2, 0:n], r, r, ALU.mult)))
                wait(done.mark(dve.tensor_tensor(nw[:, 2, 0:n], nw[:, 2, 0:n], nw[:, 0, 0:n], ALU.mult)))
                wait(done.mark(dve.tensor_scalar(nw[:, 2, 0:n], nw[:, 2, 0:n], -0.5, 1.5, ALU.mult, ALU.add)))
                wait(done.mark(dve.tensor_tensor(r, r, nw[:, 2, 0:n], ALU.mult)))

            dve.wait_ge(d_x, 16)
            for t in range(NT):
                v = done.mark(dve.bn_stats(stats[:, t, :], xs[:, t, :]))
            variances(v)
            rsqrt(0, NT, rstd[:, :])

            dve.wait_ge(mod_copied, B)
            wait(done.mark(dve.tensor_scalar(mod[:, :, D:2 * D], mod[:, :, D:2 * D], 1.0, None, ALU.add)))

            def gates(b):
                part = lambda o: mod[:, bass.ds(b, 1), o * D:(o + 1) * D].rearrange("p b d -> p (b d)")
                wait(done.mark(dve.tensor_scalar(part(4), part(4), 1.0, None, ALU.add)))
                for i, o in enumerate((2, 5)):
                    gate = part(o)
                    up, low = (late[:, (2 * i + u) * D:(2 * i + u + 1) * D] for u in range(2))
                    done.mark(dve.tensor_scalar(up, gate, 0.0, None, ALU.is_ge))
                    wait(done.mark(dve.tensor_scalar(low, gate, 0.0, None, ALU.is_lt)))
                    done.mark(dve.scalar_tensor_tensor(up, gate, 0.25, up, ALU.max, ALU.mult))
                    wait(done.mark(dve.scalar_tensor_tensor(low, gate, -0.25, low, ALU.min, ALU.mult)))
                    wait(done.mark(dve.tensor_tensor(gate, up, low, ALU.add)))

            def modulated(dst, tile, b, scale, shift):
                wait(done.mark(dve.tensor_scalar(dst, xs[:, tile, :], mean_var[:, tile, 0:1], rstd[:, bass.ds(tile, 1)], ALU.subtract, ALU.mult)))
                wait(done.mark(dve.tensor_tensor(dst, dst, mod[:, b, scale * D:(scale + 1) * D], ALU.mult)))
                return dve.tensor_tensor(dst, dst, mod[:, b, shift * D:(shift + 1) * D], ALU.add)

            def step(b, t, last):
                if t < TI or not last:
                    if t >= 2:
                        dve.wait_ge(hT_mm, b * TI + t - 1)
                        dve.sem_inc(dve_step, 1)
                    modulated(h[:, t % 2, :], b * TI + t, b + t // TI, 1, 0).then_inc(h_ready, 1)
                if t >= 1:
                    tile, p = b * TI + (t - 1), (t - 1) % 2
                    pre = bank[4 * p + 2]
                    dve.wait_ge(g_sq, tile + 1)
                    wait(done.mark(dve.tensor_scalar(gl[:, p, :], gl[:, p, :], 0.044715, 1.0, ALU.mult, ALU.add)))
                    dve.tensor_tensor(gl[:, p, :], pre[:, :], gl[:, p, :], ALU.mult).then_inc(g_arg, 1)
                    dve.wait_ge(g_tanh, tile + 1)
                    dve.scalar_tensor_tensor(gh[:, p, :, :].rearrange("p c t -> p (c t)"), gl[:, p, :], 1.0, pre[:, :], ALU.add, ALU.mult).then_inc(g_ready, 1)

            run_tiles(lambda lo, hi: counted(done, dve.Fori(lo, hi), hi - lo, 3 * TI), step, 1)

            dve.wait_ge(proj_copied, NT + C_E)
            w1 = W[:, :, :].rearrange("p t (c i n) -> p (t c) (i n)", c=C, i=4)[:, :, 0:2 * N]
            wait(done.mark(dve.tensor_tensor(sq.rearrange("p (a b) -> p a b", b=2 * N), w1, w1, ALU.mult)))
            wait(done.mark(dve.tensor_reduce(nw[:, 0, :], sq.rearrange("p (a b) -> p a b", b=N), AX.X, ALU.add)))
            dve.tensor_scalar(nw[:, 0, :], nw[:, 0, :], 1.0 / N, RMS_EPS, ALU.mult, ALU.add).then_inc(var_ready, 1)
            rsqrt(1, 64, rrms[:, :])
            w1 = W[:, :, :].rearrange("p t (c i n) -> p (t c) i n", c=C, i=4)[:, :, 0:2, :]
            done.mark(dve.tensor_tensor(w1, w1, bc(rrms[:, :].rearrange("p (a i) -> p a i", i=2), 3, N), ALU.mult))
            for o in (0, 2 * N):
                v = done.mark(dve.tensor_scalar(DD[:, :, o:o + N], DD[:, :, o:o + N], 1.0, None, ALU.add))
            wait(v)
            dve.wait_ge(pool_ready, 1)

            PER_B = 2 * G + TI * 3 + 11
            with dve.Fori(0, B) as b:
                saved_b = done.enter(b, PER_B)
                def kw_transposed(t):
                    dve.wait_ge(stack_mm, (b * TI + t) * 5 + STACKS.index(3) + 1)
                    dve.tensor_copy(KW[:, :, P * t:P * (t + 1)], bank[3][:, :].rearrange("p (a t) -> p a t", t=P)).then_inc(stack_dve, 1)

                for t in range(TI):
                    tile = b * TI + t
                    w = weights_of(tile)
                    q3 = QK[:, tile, 0:D].rearrange("p (n h) -> p n h", n=N)
                    k3 = QK[:, tile, D:2 * D].rearrange("p (n h) -> p n h", n=N)
                    qc = stack[0].rearrange("p (n u h) -> p n u h", n=N, u=2)

                    def stack_free(i):
                        if t > 0:
                            dve.wait_ge(stack_mm, tile * 5 - 4 + STACKS.index(i))

                    stack_free(0)
                    dve.tensor_tensor(qc[:, :, 0, :], q3, bc(DD[:, tile, 0:N], 2, HD), ALU.mult)
                    dve.tensor_copy(qc[:, :, 1, :], q3).then_inc(stack_ready, 1)
                    for i, src, c in ((1, q3, 0), (3, k3, 1)):
                        stack_free(i)
                        for r in range(R):
                            ins = dve.tensor_tensor(stack[i][:, r * D:(r + 1) * D].rearrange("p (n h) -> p n h", n=N), src, bc(w[:, c, r, :], 2, HD), ALU.mult)
                        ins.then_inc(stack_ready, 1)
                        if t > 0 and i == 1:
                            kw_transposed(t - 1)
                kw_transposed(TI - 1)
                dve.wait_ge(stack_mm, (b + 1) * 5 * TI)
                dve.sem_inc(dve_step, 1)
                dve.memset(Hk[:, :, :], 0.0)
                dve.memset(Hp[:, :, :], 0.0).then_inc(sums_clear, 1)
                for t in range(TI):
                    tile = b * TI + t
                    v3 = V[:, tile, :].rearrange("p (n h) -> p n h", n=N)
                    dve.tensor_copy(VK[:, t, :, 0, :], v3)
                    dve.tensor_tensor(VK[:, t, :, 1, :], v3, bc(DD[:, tile, 3 * N:4 * N], 2, HD), ALU.mult).then_inc(vk_ready, 1)
                for s in range(TI):
                    for r in range(R):
                        n = 2 * s + r
                        dve.wait_ge(hk_mm, b * 8 + (n + 1))
                        dve.tensor_copy(HK[:, r, TRK[s]:TRK[s + 1]], bank[HK_BANKS[n]][:, 0:P * (TI - s)]).then_inc(hk_copied, 1)
                dve.wait_ge(sums_clear, b + 1)
                dve.sem_inc(dve_step, 1)

                def step(g, k, last):
                    base = (b * G + g) * STEPS

                    def logits(k):
                        t, m = at(k)
                        dve.wait_ge(logit_mm, base + (k + 1))
                        dve.wait_ge(term_ready, base + (k + 1))
                        dve.wait_ge(pt_mm, base + (k - 7 + C_PT))
                        dve.wait_ge(hp_added, base + (k - 7 + C_HP))
                        dve.sem_inc(dve_step, 1)
                        dve.tensor_tensor_reduce(out=XH[m % 2][:, TRI[t]:TRI[t + 1]], in0=bank[k % 4][:, 0:P * (t + 1)], in1=YT[t][:, 0:P * (t + 1)],
                                                 scale=1.0, scalar=3e38, op0=ALU.add, op1=ALU.min,
                                                 accum_out=rowmin[:, t:t + 1]).then_inc(logit_read, 1)

                    def sum_inverted(k):
                        t, m = at(k)
                        dve.wait_ge(exp_done, base + (k + 1))
                        dve.reciprocal(rsum[:, t:t + 1], rowsum[:, t:t + 1]).then_inc(rsum_ready, 1)

                    def query_sums(k):
                        t, m = at(k)
                        dve.wait_ge(w1r_ready, base + (k + 1))
                        dve.wait_ge(hp_added, base + (k - 3 + C_HP))
                        for r in range(R):
                            hp = Hp[:, r, TRI[t]:TRI[t + 1]]
                            ins = dve.scalar_tensor_tensor(hp, XH[m % 2][:, TRI[t]:TRI[t + 1]], w1r[:, t, r:r + 1], hp, ALU.mult, ALU.add)
                        ins.then_inc(hp_added, 1)

                    def key_sums(k):
                        s, m = at(k)
                        dve.wait_ge(pt_ready, base + (k + 1 + C_E))
                        dve.wait_ge(hk_added, base + (k - 3 + C_HP))
                        for r in range(R):
                            hk = Hk[:, r, TRK[s]:TRK[s + 1]]
                            ins = dve.scalar_tensor_tensor(hk, PT[:, k % 2, 0:P * (TI - s)], weight(b, s, 3, r, g * 4 + (m + k // STEPS * 4)), hk, ALU.mult, ALU.add)
                        ins.then_inc(hk_added, 1)

                    def own_outputs(p):
                        n0 = g * 4 + 2 * p
                        own = bank[6 + p][:, 0:TI * 4 * HD].rearrange("p (t j u h) -> p t j u h", t=TI, j=2, u=2)
                        o = O[:, :, bass.ds(n0 * HD, 2 * HD)].rearrange("p t (j h) -> p t j h", j=2)
                        dve.wait_ge(pv_mm, base + (8 * p + 8 + C_E))
                        wait(done.mark(dve.tensor_tensor(o, own[:, :, :, 0, :], bc(DD[:, bass.ds(b * TI, TI), bass.ds(n0 + 2 * N, 2)], 3, HD), ALU.mult)))
                        dve.tensor_tensor(o, own[:, :, :, 1, :], o, ALU.add).then_inc(own_read, 1)

                    if k >= 1 and (k - 1 < STEPS or not last):
                        sum_inverted(k - 1)
                    if k < STEPS or not last:
                        logits(k)
                    if k >= V_LAG and (k - V_LAG < STEPS or not last):
                        key_sums(k - V_LAG)
                    if k >= 1 and (k - 1 < STEPS or not last):
                        query_sums(k - 1)
                    if k >= V_LAG:
                        if (k - V_LAG) % 8 == 0 and k > V_LAG:
                            own_outputs((k - V_LAG) // 8 - 1)

                def fori(lo, hi):
                    return counted(done, dve.Fori(lo, hi), hi - lo, 2)

                run_groups(fori, step, V_LAG + 1)

                def combine(t):
                    tile, p = b * TI + t, t % 2
                    w = weights_of(tile)
                    dve.wait_ge(hv_mm, tile + 1)
                    for r in range(R):
                        ins = dve.tensor_tensor(ou[:, r, :].rearrange("p (n h) -> p n h", n=N),
                                                bank[4 + p][:, r * D:(r + 1) * D].rearrange("p (n h) -> p n h", n=N),
                                                bc(w[:, 2, 2 + r, :], 2, HD), ALU.mult)
                    wait(done.mark(ins))
                    dve.tensor_tensor(O[:, t, :], bank[6 + p][:, 0:D], O[:, t, :], ALU.add).then_inc(o_ready, 1)
                    dve.tensor_tensor(ou[:, 0, :], ou[:, 0, :], ou[:, 1, :], ALU.add).then_inc(o_ready, 1)
                    dve.wait_ge(o_ready, tile * 3 + 2)
                    dve.tensor_tensor(O[:, t, :], O[:, t, :], ou[:, 0, :], ALU.add).then_inc(o_ready, 1)
                    dve.wait_ge(o_ready, tile * 3 + 3)

                def residual(t):
                    tile, p = b * TI + t, t % 2
                    dve.wait_ge(ao_mm, tile + 1)
                    wait(done.mark(dve.tensor_tensor(ou[:, 0, :], bank[6 + p][:, 0:D], mod[:, b, 2 * D:3 * D], ALU.mult)))
                    dve.tensor_tensor(xs[:, tile, :], xs[:, tile, :], ou[:, 0, :], ALU.add).then_inc(x1_ready, 1)
                    dve.wait_ge(x1_ready, tile + 1 + C_X1)
                    done.mark(dve.bn_stats(stats[:, bass.ds(tile, 1), :].rearrange("p a s -> p (a s)"), xs[:, tile, :]))

                gates(b)
                wait(done.now())
                dve.wait_ge(own_read, (b + 1) * G * 2 + C_E)
                for i in range(TI + 1):
                    if i < TI:
                        combine(i)
                    if i >= 1:
                        residual(i - 1)
                done.leave(saved_b, B, PER_B)

            dve.wait_ge(x1_ready, NT + C_X1)
            variances(done.now())
            rsqrt(2, NT, rstd[:, :])
            for t in range(NT + 1):
                if t < NT:
                    dve.tensor_scalar(rows[:, t, :], xs[:, t, :], mean_var[:, t, 0:1], rstd[:, t:t + 1], ALU.subtract, ALU.mult).then_inc(n2_ready, 1)
                if t >= 1:
                    dve.wait_ge(n2_ready, t)
                    dve.tensor_tensor(rows[:, t - 1, :], rows[:, t - 1, :], mod[:, (t - 1) // TI, 4 * D:5 * D], ALU.mult).then_inc(m2_ready, 1)
            dve.wait_ge(r_mm, 1)
            wait(done.mark(dve.tensor_copy(rl[:, :, :], bank[2][:, 0:NT * E].rearrange("p (t e) -> p t e", e=E))))
            wait(done.mark(dve.tensor_reduce(rbest[:, :], rl[:, :, :], AX.X, ALU.max)))
            dve.tensor_tensor(rone[:, :, :], rl[:, :, :], bc(rbest[:, :], 2, E), ALU.is_equal).then_inc(r_max, 1)
            dve.wait_ge(r_max, 1)
            wait(done.mark(dve.tensor_scalar(rl[:, :, :], bc(eio[:, :], 1, NT), -float(E), None, ALU.add)))
            wait(done.mark(dve.tensor_tensor(rone[:, :, :], rone[:, :, :], rl[:, :, :], ALU.mult)))
            wait(done.mark(dve.tensor_reduce(rstd[:, :], rone[:, :, :], AX.X, ALU.min)))
            dve.tensor_tensor(rone_b[:, :, :], rl[:, :, :], bc(rstd[:, :], 2, E), ALU.is_equal).then_inc(one_ready, 1)
            wait(done.mark(dve.tensor_tensor(rone[:, :, :], rl[:, :, :], bc(rstd[:, :], 2, E), ALU.is_equal)))
            dve.wait_ge(half_ready, 1)
            wait(done.mark(dve.tensor_scalar(rbest[:, :], rbest[:, :], 0.5, 0.5, ALU.mult, ALU.add)))
            for t in range(NT):
                dve.tensor_scalar(rows[:, t, :], rows[:, t, :], rbest[:, t:t + 1], None, ALU.mult).then_inc(rows_scaled, 1)

            def slots():
                dve.wait_ge(rank_mm, 1)
                cnt = bank[7][:, NT * E:(NT + 1) * E]
                need = ecmp[:, 0:NT * E].rearrange("p (e j) -> p e j", j=NT)
                wait(done.mark(dve.tensor_copy(rank[:, 0, :], cnt)))
                wait(done.mark(dve.tensor_tensor(need, bc(rank[:, 0, :], 2, NT), bc(start_of[:, :], 1, E), ALU.is_gt)))
                wait(done.mark(dve.tensor_reduce(tiles_of[:, 0, :], need, AX.X, ALU.add)))
                prior = ecmp[:, 0:E * E].rearrange("p (e f) -> p e f", f=E)
                wait(done.mark(dve.tensor_tensor(prior, bc(tiles_of[:, 0, :], 1, E), below[:, :, :], ALU.mult)))
                wait(done.mark(dve.tensor_reduce(tiles_of[:, 1, :], prior, AX.X, ALU.add)))
                v = done.mark(dve.tensor_tensor(tiles_of[:, 2, :], tiles_of[:, 0, :], tiles_of[:, 1, :], ALU.add))
                wait(done.mark(dve.scalar_tensor_tensor(rank[:, :, :], bc(tiles_of[:, 1, :], 1, NT), float(P),
                                                        bank[7][:, 0:NT * E].rearrange("p (t e) -> p t e", e=E), ALU.mult, ALU.add)))
                wait(done.mark(dve.tensor_tensor(rank[:, :, :], rank[:, :, :], rone[:, :, :], ALU.mult)))
                wait(done.mark(dve.tensor_reduce(row_f[:, :], rank[:, :, :], AX.X, ALU.add)))
                dve.tensor_copy(row_of[:, :], row_f[:, :]).then_inc(route_ready, 1)
                ended = ecmp[:, :].rearrange("p (s e) -> p s e", e=E)
                wait(done.mark(dve.tensor_tensor(ended, bc(tiles_of[:, 2, :], 1, NSLOT), bc(slot_no[:, :], 2, E), ALU.is_le)))
                wait(done.mark(dve.tensor_reduce(slot_e[:, :], ended, AX.X, ALU.add)))
                dve.tensor_scalar(slot_expert[:, :], slot_e[:, :], float(E - 1), None, ALU.min).then_inc(slot_known, 1)

            def step(i, j, last):
                def hidden(j):
                    p = j % 2
                    dve.wait_ge(th_ready, i * RING + (NT + j + 1))
                    wait(done.mark(dve.scalar_tensor_tensor(Y[:, p, 0:F], Y[:, p, 0:F], 1.0, bank[p][:, 0:F], ALU.add, ALU.mult)))
                    dve.wait_ge(hmT_mm, i * RING + (NT + j - 1 + C_E))
                    dve.scalar_tensor_tensor(X[:, p, 0:F], bank[p][:, F:2 * F], 0.5, Y[:, p, 0:F], ALU.mult, ALU.mult).then_inc(hm_ready, 1)

                def output(j):
                    y = bank[4 + j % 2][:, 0:D]
                    dve.wait_ge(dn_mm, i * RING + (NT + j + 1 + C_E))
                    if j < 0:
                        t = NT + j
                        dve.tensor_tensor(ou[:, t % 2, :], y, mod[:, t // TI, 5 * D:6 * D], ALU.mult).then_inc(dn_read, 1)
                        dve.wait_ge(dn_read, t + 1 + C_E)
                        v = done.mark(dve.tensor_tensor(xs[:, t, :], xs[:, t, :], ou[:, t % 2, :], ALU.add))
                        wait(v)
                    else:
                        r = j % RING
                        dve.wait_ge(d_y[r], (i + j // RING + 1) * 16)
                        dve.tensor_copy(slot_y[:, r, :], y).then_inc(dn_read, 1)
                        dve.wait_ge(dn_read, i * RING + (NT + j + 1 + C_E))
                        dve.sem_inc(y_ready, 1)

                if j == -NT + 3:
                    slots()
                if there(j - 1, last):
                    hidden(j - 1)
                if there(j - 3, last):
                    output(j - 3)

            def fori(lo, hi):
                return counted(done, dve.Fori(lo, hi), hi - lo, RING)

            run_experts(fori, step)
            for t in range(NT):
                dve.wait_ge(d_back[t], 16)
                if t >= 2:
                    dve.wait_ge(out_ready, t - 1)
                wait(done.mark(dve.tensor_tensor(ou[:, t % 2, :], back[:, t, :], mod[:, t // TI, 5 * D:6 * D], ALU.mult)))
                dve.tensor_tensor(xs[:, t, :], xs[:, t, :], ou[:, t % 2, :], ALU.add).then_inc(out_ready, 1)

        @block.tensor
        def _(pe):
            pe.sem_inc(pt_mm, C_PT)
            pe.sem_inc(pv_mm, C_E)
            pe.sem_inc(hmT_mm, C_E)
            pe.sem_inc(dn_mm, C_E)
            pe.wait_ge(c_ready, 1)
            pe.wait_ge(d_wm, 16 * KT)

            def modulation(j):
                for b in range(B):
                    for k in range(KT):
                        mm = pe.matmul(bank[(j * B + b) % 4][:, :], c_rows[k * B + b], wmod_s[k][:, 512 * j:512 * j + 512], start=(k == 0), stop=(k == KT - 1))
                    mm.then_inc(mod_mm, 1)

            modulation(0)
            pe.wait_ge(pool_ready, 1)
            pe.wait_ge(d_w, 16 * 8)
            pe.wait_ge(mod_copied, B)

            def step(b, t, last):
                def h_transposes(t):
                    tile, p = b * TI + t, t % 2
                    pe.wait_ge(h_ready, tile + 1)
                    pe.wait_ge(qkv_copied, tile - 1 + C_E)
                    for k in range(KT):
                        mm = pe.transpose(bank[4 * p][:, k * P:(k + 1) * P], h[:, p, k * P:(k + 1) * P], ident[:, :])
                    mm.then_inc(hT_mm, 1)

                def hidden(t):
                    p = t % 2
                    pe.wait_ge(hT_ready, b * TI + t + 1)
                    for c in range(C):
                        for k in range(KT):
                            mm = pe.matmul(bank[4 * p + 2][:, c * P:(c + 1) * P], dw1_s[:, k, c * P:(c + 1) * P], hT[:, p, k, :], start=(k == 0), stop=(k == KT - 1))
                    mm.then_inc(dwh_mm, 1)

                def qkv(t):
                    p = t % 2
                    bk = bank[4 * p:4 * p + 4]
                    pe.wait_ge(proj_copied, b * TI + (t - 1 + C_E))
                    for k in range(KT):
                        pe.matmul(bk[1][:, :], hT[:, p, k, :], wqkv_s[:, k, 0:2 * D], start=(k == 0), stop=(k == KT - 1))
                    for k in range(KT):
                        pe.matmul(bk[0][:, D:2 * D], hT[:, p, k, :], wqkv_s[:, k, 2 * D:3 * D], start=(k == 0), stop=(k == KT - 1))
                    for k in range(KT):
                        mm = pe.matmul(bk[3][:, D:D + 64], hT[:, p, k, :], ddw_s[:, k, :], start=(k == 0), stop=(k == KT - 1))
                    mm.then_inc(qkv_mm, 1)

                def compositions(t):
                    p = t % 2
                    pe.wait_ge(g_ready, b * TI + t + 1)
                    for c in range(C):
                        mm = pe.matmul(bank[4 * p + 3][:, c * M4:(c + 1) * M4], gh[:, p, c, :], qkw_s[:, c, :], start=True, stop=True)
                    mm.then_inc(proj_mm, 1)

                before_it = 1 <= t and (t - 1 < TI or not last)
                if before_it:
                    hidden(t - 1)
                if t >= 2:
                    compositions(t - 2)
                if t < TI or not last:
                    h_transposes(t)
                if before_it:
                    qkv(t - 1)

            run_tiles(pe.Fori, step, 2)
            pe.wait_ge(proj_copied, NT - 1 + C_E)
            modulation(1)
            modulation(2)
            pe.wait_ge(proj_copied, NT + C_E)
            pe.wait_ge(mod_copied, 3 * B)

            with pe.Fori(0, B) as b:
                def stack_transposes(t):
                    tile = b * TI + t
                    for o, i in enumerate(STACKS):
                        if i in (2, 4):
                            pe.wait_ge(k_ready, tile * 2 + i // 2)
                        else:
                            pe.wait_ge(stack_ready, tile * 3 + {0: 1, 1: 2, 3: 3}[i])
                        if t > 0:
                            if i == 3:
                                pe.wait_ge(stack_dve, tile)
                            else:
                                pe.wait_ge(stack_act, tile * 4 - 3 + o)
                        for a in range(4):
                            mm = pe.transpose(bank[i][:, a * P:(a + 1) * P], stack[i][:, a * P:(a + 1) * P], ident[:, :])
                        mm.then_inc(stack_mm, 1)

                def hq(t):
                    pe.wait_ge(stack_act, (b * TI + t + 1) * 4)
                    for r in range(R):
                        if t > 0:
                            pe.wait_ge(hq_copied, b * 8 + (2 * t - 1 + r))
                        for k in range(KT):
                            mm = pe.matmul(bank[5 + r][:, 0:P * (t + 1)], QW[:, r * KT + k, P * t:P * (t + 1)], KTr[:, k, 0:P * (t + 1)], start=(k == 0), stop=(k == KT - 1))
                        mm.then_inc(hq_mm, 1)

                def hk(s):
                    for r in range(R):
                        n = 2 * s + r
                        if n >= 6:
                            pe.wait_ge(hk_copied, b * 8 + (n - 5))
                        for k in range(KT):
                            mm = pe.matmul(bank[HK_BANKS[n]][:, 0:P * (TI - s)], KW[:, r * KT + k, P * s:P * (s + 1)], QT[:, k, P * s:T], start=(k == 0), stop=(k == KT - 1))
                        mm.then_inc(hk_mm, 1)

                for t in range(TI + 1):
                    if t < TI:
                        stack_transposes(t)
                    if t >= 1:
                        hq(t - 1)
                pe.wait_ge(stack_dve, (b + 1) * TI)
                for s in range(TI):
                    hk(s)
                pe.wait_ge(hq_copied, (b + 1) * 8)
                pe.wait_ge(hk_copied, (b + 1) * 8)
                pe.sem_inc(pe_step, 1)
                def step(g, k, last):
                    base = (b * G + g) * STEPS

                    def logits(k):
                        t, m = at(k)
                        row, p, j = 32 * m, m // 2, m % 2
                        bk = bank[k % 4]
                        if k % 8 < TI:
                            pe.wait_ge(pair_ready, (b * G + g) * (2 * TI) + (k // 8 * TI + (t + 1) + C_ONE))
                        pe.wait_ge(logit_read, base + (k - 3 + C_LOGIT))
                        pe.sem_inc(pe_step, 1)
                        pe.matmul(bk[:, 0:P * (t + 1)], QCg[row:row + 32, P * t:P * (t + 1)],
                                  KCg[row:row + 32, 0:P * (t + 1)],
                                  start=True, stop=False, tile_position=(row, 0))
                        for s in range(t + 1):
                            for r in range(R):
                                off = TRK[s] + P * (t - s)
                                pe.matmul(bk[:, s * P:(s + 1) * P], HK[:, r, off:off + P], DG[:, p, s, r, j, :], start=False, stop=False)
                        pe.matmul(bk[:, t * P:(t + 1) * P], ident_b[:, :], mask_b[:, :], start=False, stop=True).then_inc(logit_mm, 1)

                    def transposes(k):
                        s, m = at(k)
                        pe.wait_ge(rd_ready, base + (k - s + TI))
                        pe.wait_ge(pt_ready, base + (k - 1 + C_E))
                        for t in range(s, TI):
                            mm = pe.matmul(bank[4 + k % 2][:, (t - s) * P:(t - s + 1) * P], XH[m % 2][:, TRI[t] + s * P:TRI[t] + (s + 1) * P],
                                           RD[:, m % 2 * TI + t, :], start=True, stop=True)
                        mm.then_inc(pt_mm, 1)

                    def values(k):
                        s, m = at(k)
                        pe.wait_ge(pt_ready, base + (k + 1 + C_E))
                        head = g * 4 + (m + k // STEPS * 4)
                        p, j = m // 2, m % 2
                        if s == 0 and j == 0:
                            pe.wait_ge(own_read, (b * G + g) * 2 + (k // 8 - 1 + C_E))
                            pe.sem_inc(pe_step, 1)
                        for t in range(s, TI):
                            mm = pe.matmul(bank[6 + p][:, (t * 2 + j) * 2 * HD:(t * 2 + j + 1) * 2 * HD], PT[:, k % 2, (t - s) * P:(t - s + 1) * P],
                                           VK[:, s, bass.ds(head, 1), :, :].rearrange("p a u h -> p (a u h)"),
                                           start=(s == 0 and t == 0 and j == 0), stop=(s == t), skip_group_check=True)
                        mm.then_inc(pv_mm, 1)

                    if k < STEPS or not last:
                        logits(k)
                    if k >= T_LAG and (k - T_LAG < STEPS or not last):
                        transposes(k - T_LAG)
                    if k >= V_LAG:
                        values(k - V_LAG)

                run_groups(pe.Fori, step, V_LAG)

                pe.wait_ge(hp_added, (b + 1) * G * STEPS + C_HP)
                pe.wait_ge(hk_added, (b + 1) * G * STEPS + C_HP)
                pe.wait_ge(vw_ready, b + 1 + C_ONE)
                pe.wait_ge(own_read, (b + 1) * G * 2 + C_E)

                def sums_transposes(t):
                    if t >= 2:
                        pe.wait_ge(hp_ready, b * 8 + 2 * t - 2)
                    for r in range(R):
                        for s in range(t + 1):
                            mm = pe.transpose(bank[t % 2 * 2 + r][:, s * P:(s + 1) * P], Hp[:, r, TRI[t] + s * P:TRI[t] + (s + 1) * P], ident[:, :])
                        mm.then_inc(hp_mm, 1)

                def sums_values(t):
                    p = t % 2
                    pe.wait_ge(hp_ready, b * 8 + (2 * t + 2))
                    if t >= 2:
                        pe.wait_ge(x1_ready, b * TI + (t - 1 + C_X1))
                    for r in range(R):
                        for s in range(t + 1):
                            pe.matmul(bank[4 + p][:, r * D:(r + 1) * D], X[:, p * 2 + r, s * P:(s + 1) * P],
                                      VK[:, s, :, 0, :], start=(s == 0), stop=(s == t))
                    for r in range(R):
                        for s in range(t + 1):
                            off = TRK[s] + P * (t - s)
                            mm = pe.matmul(bank[6 + p][:, 0:D], Hk[:, r, off:off + P], VW[:, s, r, :], start=(r == 0 and s == 0), stop=(r == R - 1 and s == t))
                    mm.then_inc(hv_mm, 1)

                def output_transposes(t):
                    pe.wait_ge(o_ready, (b * TI + t + 1) * 3)
                    for k in range(KT):
                        mm = pe.transpose(bank[6 + t % 2][:, D + k * P:D + (k + 1) * P], O[:, t, k * P:(k + 1) * P], ident[:, :])
                    mm.then_inc(oT_mm, 1)

                def projection(t):
                    pe.wait_ge(oT_ready, b * TI + t + 1)
                    for k in range(KT):
                        mm = pe.matmul(bank[6 + t % 2][:, 0:D], hT[:, t % 2, k, :], woT_s[:, k, :], start=(k == 0), stop=(k == KT - 1))
                    mm.then_inc(ao_mm, 1)

                for i in range(TI + 2):
                    if i < TI:
                        sums_transposes(i)
                    if i >= 2:
                        output_transposes(i - 2)
                    if 1 <= i < TI + 1:
                        sums_values(i - 1)
                    if i >= 2:
                        projection(i - 2)

            def router(t):
                pe.wait_ge(h2_T, t + 1)
                for k in range(KT):
                    mm = pe.matmul(bank[2][:, t * E:(t + 1) * E], x2T[:, k, P * t:P * (t + 1)], rw_s[:, k, :], start=(k == 0), stop=(k == KT - 1))
                return mm

            for t in range(NT):
                pe.wait_ge(h2_ready, t + 1)
                if t >= 2:
                    pe.wait_ge(h2_T, t - 1)
                for k in range(KT):
                    mm = pe.transpose(bank[t % 2][:, k * P:(k + 1) * P], rows[:, t, k * P:(k + 1) * P], ident[:, :])
                mm.then_inc(h2_mm, 1)
                if t >= 1:
                    router(t - 1)
            router(NT - 1).then_inc(r_mm, 1)

            def routing():
                flat = rone_b[:, :, :].rearrange("p t e -> p (t e)")
                pe.wait_ge(one_ready, 1)
                pe.matmul(bank[7][:, 0:NT * E], before[:, :], flat, start=True, stop=False, skip_group_check=True)
                for d in range(1, NT):
                    pe.matmul(bank[7][:, d * E:NT * E], ones_b[:, :], flat[:, 0:(NT - d) * E], start=False, stop=(d == NT - 1), skip_group_check=True)
                for t in range(NT):
                    mm = pe.matmul(bank[7][:, NT * E:(NT + 1) * E], ones_b[:, :], flat[:, t * E:(t + 1) * E], start=False, stop=(t == NT - 1), skip_group_check=True)
                mm.then_inc(rank_mm, 1)

            def step(i, j, last):
                def slot_transposes(j):
                    r = j % RING
                    if j == 0 and i == 0:
                        pe.wait_ge(slot_known, 1)
                        pe.wait_ge(d_gu, 16 * 3 * E)
                    pe.wait_ge(d_slot[r], (i + j // RING + 1) * 16)
                    pe.wait_ge(xT_ready, i * RING + (j - 1 + C_E))
                    for k in range(KT):
                        mm = pe.transpose(bank[6 + j % 2][:, k * P:(k + 1) * P], slot_x[:, r, k * P:(k + 1) * P], ident[:, :])
                    mm.then_inc(xT_mm, 1)

                def expert_of(j):
                    return pe.value_load(slot_expert[0:1, bass.ds(i * RING + j, 1)], min_val=0, max_val=E - 1)

                def gate_up(j):
                    if j == -NT:
                        pe.wait_ge(d_shared, 16 * 3)
                    if j < 0:
                        src, (w, _) = x2T[:, :, P * (NT + j):P * (NT + j + 1)], expert_weights(shared_s)
                    else:
                        pe.wait_ge(xT_ready, i * RING + (j + 1 + C_E))
                        src, (w, _) = slot_xT[:, j % 2, :, :], expert_weights(big, expert_of(j))
                    pe.wait_ge(hm_ready, i * RING + (NT + j - 1 + C_E))
                    for c in range(KT):
                        mm = pe.matmul(bank[j % 2][:, :], src[:, c, :], w[:, c, :], start=(c == 0), stop=(c == KT - 1))
                    mm.then_inc(gu_mm, 1)

                def hidden_transposes(j):
                    pe.wait_ge(hm_ready, i * RING + (NT + j + 1 + C_E))
                    pe.wait_ge(hmT_ready, i * RING + (NT + j - 1 + C_E))
                    for c in range(KT):
                        mm = pe.transpose(bank[2 + j % 2][:, c * P:(c + 1) * P], X[:, j % 2, c * P:(c + 1) * P], ident[:, :])
                    mm.then_inc(hmT_mm, 1)

                def down(j):
                    _, w = expert_weights(shared_s) if j < 0 else expert_weights(big, expert_of(j))
                    pe.wait_ge(hmT_ready, i * RING + (NT + j + 1 + C_E))
                    pe.wait_ge(dn_read, i * RING + (NT + j - 1 + C_E))
                    for c in range(F // P):
                        mm = pe.matmul(bank[4 + j % 2][:, 0:D], hT[:, j % 2, c, :], w[:, c, :], start=(c == 0), stop=(c == KT - 1))
                    mm.then_inc(dn_mm, 1)

                if j >= 0 and there(j, last):
                    slot_transposes(j)
                if there(j - 1, last):
                    gate_up(j - 1)
                if j == -NT + 1:
                    routing()
                if there(j - 2, last):
                    hidden_transposes(j - 2)
                if there(j - 3, last):
                    down(j - 3)

            run_experts(pe.Fori, step)


def kernel(L0_attn_x, L0_attn_w_qkv, L0_attn_w_o, L0_attn_dw1, L0_attn_qkw, L0_attn_dd_w, L0_ffn_router_w,
           L0_ffn_gate_w, L0_ffn_up_w, L0_ffn_down_w, L0_ffn_shared_gate_w, L0_ffn_shared_up_w,
           L0_ffn_shared_down_w, L0_c, L0_wmod):
    import numpy as np
    import concourse.bacc as bacc
    from concourse import mybir as mb
    from concourse.bass_utils import run_bass_kernel_spmd

    x = np.asarray(L0_attn_x)
    b, t, d = x.shape
    laid_out = [
        ("x", x.reshape(b * t, d)),
        ("w_qkv", np.asarray(L0_attn_w_qkv)),
        ("w_oT", np.asarray(L0_attn_w_o).T),
        ("dw1", np.asarray(L0_attn_dw1).reshape(d, -1)),
        ("qkw", np.asarray(L0_attn_qkw).reshape(4, 128, -1)),
        ("dd_w", np.asarray(L0_attn_dd_w).reshape(d, -1)),
        ("router_w", np.asarray(L0_ffn_router_w)),
        ("gate_w", np.asarray(L0_ffn_gate_w)),
        ("up_w", np.asarray(L0_ffn_up_w)),
        ("down_w", np.asarray(L0_ffn_down_w)),
        ("shared_gate", np.asarray(L0_ffn_shared_gate_w)),
        ("shared_up", np.asarray(L0_ffn_shared_up_w)),
        ("shared_down", np.asarray(L0_ffn_shared_down_w)),
        ("cT", np.asarray(L0_c).T),
        ("wmod", np.asarray(L0_wmod)),
    ]
    nc = bacc.Bacc("TRN2", target_bir_lowering=False, num_devices=1)
    arrays, args = {}, []
    for name, a in laid_out:
        a = np.ascontiguousarray(a)
        arrays["in_" + name] = a
        args.append(nc.dram_tensor("in_" + name, a.shape, mb.dt.from_np(a.dtype), kind="ExternalInput").ap())
    slot_tiles = -(-(b * t + 8 * 127) // 512) * 4
    for name in ("slots_in", "slots_out"):
        args.append(nc.dram_tensor(name, (slot_tiles * 128, d), mb.dt.float32, kind="Internal").ap())
    out = nc.dram_tensor("out_x", (b * t, d), mb.dt.float32, kind="ExternalOutput").ap()
    adaln_layer(nc, *args, out)
    r = run_bass_kernel_spmd(nc, [arrays], core_ids=[0])
    return r.results[0]["out_x"].reshape(b, t, d)
```
